# Optimizing a Trainium2 kernel written in Bass

```python
import numpy as np
import jax
import jax.numpy as jnp

def _softmax(x, axis=-1):
    return jax.nn.softmax(x, axis=axis)

def _gelu(x):
    return jax.nn.gelu(x, approximate=True)

def _silu(x):
    return jax.nn.silu(x)

def _sigmoid(x):
    return jax.nn.sigmoid(x)

def _layernorm(x, axis=-1, eps=1e-05):
    m = jnp.mean(x, axis=axis, keepdims=True)
    v = jnp.var(x, axis=axis, keepdims=True)
    return (x - m) / jnp.sqrt(v + eps)

def _scatter_add(tgt, idx, src, axis=0):
    return tgt.at[idx].add(src)

def _segment_sum(src, seg, n):
    return jax.ops.segment_sum(src, seg, n)
kernel_name = 'mk_conv_attn_hybrid_d2_conv_nchw256_r2_97eb2b'

def setup_inputs(seed: int=0):
    np.random.seed(seed)
    _w = jnp.asarray

    def _rec_inputs():
        import jax
        import jax.numpy as jnp
        _gk = jax.random.key(seed)
        x = -0.0002928 + 1 * jax.random.normal(jax.random.fold_in(_gk, 1), (16, 128, 32, 32), jnp.float32)
        return x
    x = _rec_inputs()

    def _L0_conv_setup():
        import jax, jax.numpy as jnp
        import numpy as np
        EPS = 1e-05
        NUM_HEADS = 4
        key = jax.random.key(seed)
        ks = jax.random.split(key, 6)
        B, C, H, W = (16, 128, 32, 32)
        x = jax.random.normal(ks[0], (B, C, H, W), dtype=jnp.float32)
        gamma = jnp.ones((C,), jnp.float32)
        beta = jnp.zeros((C,), jnp.float32)
        run_mean = jax.random.normal(ks[1], (C,), dtype=jnp.float32) * 0.1
        run_var = jax.random.uniform(ks[2], (C,), dtype=jnp.float32, minval=0.5, maxval=1.5)
        qkv_w = jax.random.normal(ks[3], (3 * C, C), dtype=jnp.float32) * (1.0 / np.sqrt(C))
        qkv_b = jnp.zeros((3 * C,), jnp.float32)
        out_w = jax.random.normal(ks[4], (C, C), dtype=jnp.float32) * (1.0 / np.sqrt(C))
        out_b = jnp.zeros((C,), jnp.float32)
        return {'x': x, 'gamma': gamma, 'beta': beta, 'run_mean': run_mean, 'run_var': run_var, 'qkv_w': qkv_w, 'qkv_b': qkv_b, 'out_w': out_w, 'out_b': out_b}
    _L0_conv_all = _L0_conv_setup()
    _L0_conv_in = {k: v for k, v in _L0_conv_all.items() if k in ('gamma', 'beta', 'run_mean', 'run_var', 'qkv_w', 'qkv_b', 'out_w', 'out_b')}
    del _L0_conv_all

    def _L1_attn_setup():
        import jax, jax.numpy as jnp
        import numpy as np
        HEADS = 8
        EPS = 1e-05

        def _ln(t, w, b, headc):
            m = jnp.mean(t, axis=-1, keepdims=True)
            d = t - m
            std = jnp.sqrt(jnp.sum(d * d, axis=-1, keepdims=True) / (headc - 1))
            return w * (d / (std + EPS)) + b
        key = jax.random.key(seed)
        B, N, C = (32, 2048, 128)
        headc = C // HEADS
        x = jax.random.normal(key, (B, N, C), dtype=jnp.float32)
        return {'x': x, 'kln_weight': jnp.ones((HEADS, 1, headc), dtype=jnp.float32), 'kln_bias': jnp.zeros((HEADS, 1, headc), dtype=jnp.float32), 'vln_weight': jnp.ones((HEADS, 1, headc), dtype=jnp.float32), 'vln_bias': jnp.zeros((HEADS, 1, headc), dtype=jnp.float32)}
    _L1_attn_all = _L1_attn_setup()
    _L1_attn_in = {k: v for k, v in _L1_attn_all.items() if k in ('kln_weight', 'kln_bias', 'vln_weight', 'vln_bias')}
    del _L1_attn_all

    def _L1_ffn_setup():
        import jax, jax.numpy as jnp
        import numpy as np
        B, T, D, H, E = (16, 2048, 128, 256, 8)
        key = jax.random.key(seed)
        ks = jax.random.split(key, 5)
        x = jax.random.normal(ks[0], (B, T, D), dtype=jnp.float32)
        gate_w = jax.random.normal(ks[1], (D, E), dtype=jnp.float32) * 0.02
        gate_b = jnp.zeros((E,), dtype=jnp.float32)
        W1 = jax.random.normal(ks[2], (E, D, H), dtype=jnp.float32) * 0.02
        b1 = jnp.zeros((E, H), dtype=jnp.float32)
        W2 = jax.random.normal(ks[3], (E, H, D), dtype=jnp.float32) * 0.02
        b2 = jnp.zeros((E, D), dtype=jnp.float32)
        return {'x': x, 'gate_w': gate_w, 'gate_b': gate_b, 'W1': W1, 'b1': b1, 'W2': W2, 'b2': b2}
    _L1_ffn_all = _L1_ffn_setup()
    _L1_ffn_in = {k: v for k, v in _L1_ffn_all.items() if k in ('gate_w', 'gate_b', 'W1', 'b1', 'W2', 'b2')}
    del _L1_ffn_all
    return {'x': x, 'L0_conv_gamma': _L0_conv_in['gamma'], 'L0_conv_beta': _L0_conv_in['beta'], 'L0_conv_run_mean': _L0_conv_in['run_mean'], 'L0_conv_run_var': _L0_conv_in['run_var'], 'L0_conv_qkv_w': _L0_conv_in['qkv_w'], 'L0_conv_qkv_b': _L0_conv_in['qkv_b'], 'L0_conv_out_w': _L0_conv_in['out_w'], 'L0_conv_out_b': _L0_conv_in['out_b'], 'L1_attn_kln_weight': _L1_attn_in['kln_weight'], 'L1_attn_kln_bias': _L1_attn_in['kln_bias'], 'L1_attn_vln_weight': _L1_attn_in['vln_weight'], 'L1_attn_vln_bias': _L1_attn_in['vln_bias'], 'L1_ffn_gate_w': _L1_ffn_in['gate_w'], 'L1_ffn_gate_b': _L1_ffn_in['gate_b'], 'L1_ffn_W1': _L1_ffn_in['W1'], 'L1_ffn_b1': _L1_ffn_in['b1'], 'L1_ffn_W2': _L1_ffn_in['W2'], 'L1_ffn_b2': _L1_ffn_in['b2']}

def reference(x, L0_conv_gamma, L0_conv_beta, L0_conv_run_mean, L0_conv_run_var, L0_conv_qkv_w, L0_conv_qkv_b, L0_conv_out_w, L0_conv_out_b, L1_attn_kln_weight, L1_attn_kln_bias, L1_attn_vln_weight, L1_attn_vln_bias, L1_ffn_gate_w, L1_ffn_gate_b, L1_ffn_W1, L1_ffn_b1, L1_ffn_W2, L1_ffn_b2):
    import jax
    import jax.numpy as jnp

    def _L0_conv_ref(x, gamma, beta, run_mean, run_var, qkv_w, qkv_b, out_w, out_b):
        import jax, jax.numpy as jnp
        import numpy as np
        EPS = 1e-05
        NUM_HEADS = 4
        B, C, H, W = x.shape
        n = NUM_HEADS
        hd = C // n
        inv = jax.lax.rsqrt(run_var + EPS)
        xn = (x - run_mean[:, None, None]) * (inv * gamma)[:, None, None] + beta[:, None, None]
        qkv = jnp.einsum('oc,bchw->bohw', qkv_w, xn) + qkv_b[:, None, None]
        qkv = qkv.reshape(B, n, 3 * hd, H, W)
        q, k, v = (qkv[:, :, :hd], qkv[:, :, hd:2 * hd], qkv[:, :, 2 * hd:])
        attn = jnp.einsum('bnchw,bncyx->bnhwyx', q, k) / jnp.sqrt(jnp.float32(C))
        attn = jax.nn.softmax(attn.reshape(B, n, H, W, H * W), axis=-1)
        attn = attn.reshape(B, n, H, W, H, W)
        av = jnp.einsum('bnhwyx,bncyx->bnchw', attn, v).reshape(B, C, H, W)
        out = jnp.einsum('oc,bchw->bohw', out_w, av) + out_b[:, None, None]
        return x + out

    def _L1_attn_ref(x, kln_weight, kln_bias, vln_weight, vln_bias):
        import jax, jax.numpy as jnp
        import numpy as np
        HEADS = 8
        EPS = 1e-05

        def _ln(t, w, b, headc):
            m = jnp.mean(t, axis=-1, keepdims=True)
            d = t - m
            std = jnp.sqrt(jnp.sum(d * d, axis=-1, keepdims=True) / (headc - 1))
            return w * (d / (std + EPS)) + b
        B, N, C = x.shape
        headc = C // HEADS
        qkv = x.reshape(B, N, HEADS, headc).transpose(0, 2, 1, 3)
        k = _ln(qkv, kln_weight, kln_bias, headc)
        v = _ln(qkv, vln_weight, vln_bias, headc)
        kv = jnp.einsum('bhnd,bhne->bhde', k, v) / N
        out = jnp.einsum('bhnd,bhde->bhne', qkv, kv)
        out = out.transpose(0, 2, 1, 3).reshape(B, N, C)
        return out + x

    def _L1_ffn_ref(x, gate_w, gate_b, W1, b1, W2, b2):
        import jax, jax.numpy as jnp
        import numpy as np
        B, T, D, H, E = (16, 2048, 128, 256, 8)
        Bb, Tt, Dd = x.shape
        Ee = gate_w.shape[1]
        xf = x.reshape(-1, Dd)
        N = xf.shape[0]
        logits = xf @ gate_w + gate_b
        probs = jax.nn.softmax(logits, axis=-1)
        top2_vals, top2_idx = jax.lax.top_k(probs, 2)
        cw = jnp.zeros((N, Ee), dtype=xf.dtype).at[jnp.arange(N)[:, None], top2_idx].add(top2_vals)

        def step(acc, params):
            w1, bb1, w2, bb2, we = params
            h = jax.nn.gelu(xf @ w1 + bb1, approximate=False)
            y = h @ w2 + bb2
            return (acc + we[:, None] * y, None)
        out, _ = jax.lax.scan(step, jnp.zeros_like(xf), (W1, b1, W2, b2, cw.T))
        return out.reshape(Bb, Tt, Dd)

    def _gn(v, G=32, eps=1e-05):
        B_, C_, H_, W_ = v.shape
        g = v.reshape(B_, G, C_ // G, H_, W_)
        m = jnp.mean(g, axis=(2, 3, 4), keepdims=True)
        s = jnp.var(g, axis=(2, 3, 4), keepdims=True)
        return ((g - m) / jnp.sqrt(s + eps)).reshape(v.shape)

    def _ln_c(v, eps=1e-06):
        m = jnp.mean(v, axis=1, keepdims=True)
        s = jnp.var(v, axis=1, keepdims=True)
        return (v - m) / jnp.sqrt(s + eps)

    def _ln_t(v, eps=1e-05):
        m = jnp.mean(v, axis=-1, keepdims=True)
        s = jnp.var(v, axis=-1, keepdims=True)
        return (v - m) / jnp.sqrt(s + eps)

    def _to_tokens(v):
        B_, C_, H_, W_ = v.shape
        return v.reshape(B_, C_, H_ * W_).transpose(0, 2, 1)

    def _from_tokens(t, like):
        B_, C_, H_, W_ = like.shape
        return t.transpose(0, 2, 1).reshape(B_, C_, H_, W_)
    x = _L0_conv_ref(x, L0_conv_gamma, L0_conv_beta, L0_conv_run_mean, L0_conv_run_var, L0_conv_qkv_w, L0_conv_qkv_b, L0_conv_out_w, L0_conv_out_b)
    t = _to_tokens(x)
    t = t + _L1_attn_ref(_ln_t(t), L1_attn_kln_weight, L1_attn_kln_bias, L1_attn_vln_weight, L1_attn_vln_bias)
    t = t + _L1_ffn_ref(_ln_t(t), L1_ffn_gate_w, L1_ffn_gate_b, L1_ffn_W1, L1_ffn_b1, L1_ffn_W2, L1_ffn_b2)
    x = _from_tokens(t, x)
    return x

_drawn_inputs = setup_inputs


def setup_inputs(seed=0):
    import zlib

    import numpy as np

    out = dict(_drawn_inputs(seed))
    spreads = {'L0_conv_gamma': (1.0, 0.2),
     'L0_conv_beta': (0.0, 0.1),
     'L0_conv_qkv_b': (0.0, 0.1),
     'L0_conv_out_b': (0.0, 0.1),
     'L1_attn_kln_weight': (1.0, 0.2),
     'L1_attn_kln_bias': (0.0, 0.269),
     'L1_attn_vln_weight': (1.0, 0.2),
     'L1_attn_vln_bias': (0.0, 0.1),
     'L1_ffn_gate_b': (0.0, 0.8),
     'L1_ffn_b1': (0.0, 0.8),
     'L1_ffn_b2': (0.0, 0.8)}
    factors = {'L1_ffn_gate_w': 7.903, 'L1_ffn_W1': 8.0, 'L1_ffn_W2': 8.0}
    for name, (base, spread) in spreads.items():
        noise = np.random.default_rng([zlib.crc32(name.encode()), seed]).standard_normal(out[name].shape)
        drawn = base * np.exp(spread * noise) if base else spread * noise
        out[name] = jnp.asarray(drawn.astype(out[name].dtype))
    for name, factor in factors.items():
        out[name] = (out[name] * factor).astype(out[name].dtype)
    return out
```

```python
from contextlib import ExitStack

import concourse.bass as bass
from concourse import mybir

P = 128
EPS_BN = 1e-5
EPS_LN = 1e-5
EPS_HEAD = 1e-5

ALU = mybir.AluOpType
ACT = mybir.ActivationFunctionType
AX = mybir.AxisListType
F32 = mybir.dt.float32
BF16 = mybir.dt.bfloat16


class Linear:

    def __init__(self, pair, multiples, scratch, scale=1, plus=0):
        self.pair, self.multiples, self.scratch, self.scale, self.plus = pair, multiples, scratch, scale, plus

    def __add__(self, n):
        return Linear(self.pair, self.multiples, self.scratch, self.scale, self.plus + n)

    def __sub__(self, n):
        return self + -n

    def __mul__(self, n):
        return Linear(self.pair, self.multiples, self.scratch, self.scale * n, self.plus * n)

    __radd__, __rmul__ = __add__, __mul__

    def value(self):
        return self.pair * self.scale + self.plus

    def count(self, eng):
        if self.plus == 0:
            return self.multiples[self.scale]
        eng.reg_add(self.scratch, self.multiples[self.scale], self.plus)
        return self.scratch


def number(n):
    return n.value() if isinstance(n, Linear) else n


def conv_attention_hybrid_kernel(
    nc: bass.Bass,
    x: bass.AP,
    L0_conv_gamma: bass.AP,
    L0_conv_beta: bass.AP,
    L0_conv_run_mean: bass.AP,
    L0_conv_run_var: bass.AP,
    L0_conv_qkv_w: bass.AP,
    L0_conv_qkv_b: bass.AP,
    L0_conv_out_w: bass.AP,
    L0_conv_out_b: bass.AP,
    L1_attn_kln_weight: bass.AP,
    L1_attn_kln_bias: bass.AP,
    L1_attn_vln_weight: bass.AP,
    L1_attn_vln_bias: bass.AP,
    L1_ffn_gate_w: bass.AP,
    L1_ffn_gate_b: bass.AP,
    L1_ffn_W1: bass.AP,
    L1_ffn_b1: bass.AP,
    L1_ffn_W2: bass.AP,
    L1_ffn_b2: bass.AP,
    out: bass.AP,
):
    B, C, IMH, IMW = x.shape
    N = IMH * IMW
    BLK = N // P
    NH = 4
    HD = C // NH
    HALF = N // 2
    NKB = N // P
    G16 = L1_attn_kln_weight.shape[2]
    NG = C // G16
    E, _, HID = L1_ffn_W1.shape
    HC = HID // P
    assert C == P and HD == 32 and N == 1024 and B % 2 == 0

    STEPS, QUARTERS = 8, 32
    FIRST, LAST = -1, B + 1
    LOOP_FROM, LOOP_PAIRS = 2, (B - 4) // 2

    x_v = x.rearrange("b c h w -> b c (h w)")
    out_v = out.rearrange("b c h w -> b c (h w)")

    SCALES = (2, 4, 8, 10, 12, 16, 24, 26, 32, 64, 128, 768)

    SHARED = {}
    for s in range(STEPS):
        SHARED[f"mrow{s}"] = (4 * s + 2, 0 if s < 4 else 1)
    SHARED.update({
        "q0": (1, 1), "k0": (2, 1), "q1": (4, 1), "k1": (5, 1), "v0": (6, 1), "v1": (7, 1),
        "proj0": (8, -1), "proj1": (9, -1), "zT0": (17, -1), "zT1": (18, -1),
        "gram": (28, -1), "usum": (29, -1),
        "t2_0": (2, -2), "t2_1": (3, -2), "z2T0": (11, -2), "z2T1": (12, -2), "logits": (15, -2),
    })
    ORDER = sorted(SHARED, key=lambda n: SHARED[n][0])
    BANK = {n: i % 2 for i, n in enumerate(ORDER)}

    def in_range(lag, pair, p):
        return not isinstance(pair, int) or 0 <= 2 * pair + p + lag < B

    def image(lag, pair, p):
        return 2 * (pair + (p + lag) // 2) + (p + lag) % 2, pair + (p + lag) // 2, (p + lag) % 2

    def turn(name, pair, p):
        bank = BANK[name]
        mine = [n for n in ORDER if BANK[n] == bank]
        if isinstance(pair, int):
            it = 2 * pair + p
            done = sum(in_range(SHARED[n][1], 0, k) for k in range(FIRST, it) for n in mine)
            return done + sum(in_range(SHARED[n][1], 0, it) for n in mine[:mine.index(name)])
        before = sum(in_range(SHARED[n][1], 0, k) for k in range(FIRST, LOOP_FROM) for n in mine)
        return 2 * len(mine) * pair + (before + len(mine) * (p - LOOP_FROM) + mine.index(name))

    def at_quarter(q, pair, p):
        return [n for n in ORDER if SHARED[n][0] == q and in_range(SHARED[n][1], pair, p)]

    def iterations(eng, body):
        for it in range(FIRST, LOOP_FROM):
            body(it // 2, it % 2)
        multiples = {m: eng.alloc_register(f"pair_times_{m}") for m in SCALES}
        scratch = eng.alloc_register("wait_value")
        with eng.Fori(LOOP_FROM // 2, LOOP_FROM // 2 + LOOP_PAIRS) as register:
            for scale, multiple in multiples.items():
                eng.reg_mul(multiple, register, scale)
            pair = Linear(register, multiples, scratch)
            body(pair, 0)
            body(pair, 1)
        for it in range(LOOP_FROM + 2 * LOOP_PAIRS, LAST + 1):
            body(it // 2, it % 2)

    def positive(value):
        return not isinstance(value, int) or value > 0

    def count(eng, value):
        return value.count(eng) if isinstance(value, Linear) else value

    def apart(eng, value):
        if isinstance(value, Linear):
            eng.sem_inc(waits_passed, 1)

    ctx = ExitStack()
    with ctx:
        def sb(name, shape, dt=F32):
            return ctx.enter_context(nc.sbuf_tensor(name, shape, dt))

        def sem(name):
            return ctx.enter_context(nc.semaphore(name))

        t2_dram = nc.dram_tensor("t2_scratch", [B, P, BLK, C], F32, kind="Internal").ap()
        z2T_dram = nc.dram_tensor("z2T_scratch", [B, C, N], F32, kind="Internal").ap()

        ident = sb("ident", [P, P])
        identb = sb("identb", [P, P], BF16)
        ones = sb("ones", [P, P])
        headmask = sb("headmask", [P, P])
        wload = sb("wload", [P, 3, C])
        woload = sb("woload", [P, C])
        wqkvT = sb("wqkvT", [P, 3, NH, HD])
        woT = sb("woT", [P, C])
        bn = sb("bn", [P, 4])
        bn_scale = sb("bn_scale", [P, 1])
        bn_shift = sb("bn_shift", [P, 1])
        bn_tmp = sb("bn_tmp", [P, 2])
        bqk = sb("bqk", [P, 2])
        bv_row = sb("bv_row", [P, NH, HD])
        bo = sb("bo", [P, 1])
        kcol = sb("kcol", [P, 2])
        kb_n = sb("kb_n", [P, 1])
        vrow = sb("vrow", [P, 2, C])
        gate_w = sb("gate_w_sb", [P, E])
        gate_b = sb("gate_b_sb", [P, E])
        b1 = sb("b1_sb", [P, E, HC])
        b1_rows = sb("b1_rows", [E * HC, P])
        b2 = sb("b2_sb", [E, C])
        rank_w = sb("rank_w", [P, E])
        power = sb("power", [P, 2, BLK * NG])

        x_in = sb("x_in", [P, 2, N])
        xn = sb("xn", [P, N])
        part = sb("part", [P, 3, 2, N], BF16)
        rest = sb("rest", [P, 2, HALF])
        qs1 = sb("qs1", [P, 2, NH, N], BF16)
        ks1 = sb("ks1", [P, 2, NH, N], BF16)
        qs2 = sb("qs2", [P, 2, NH, N], BF16)
        ks2 = sb("ks2", [P, 2, NH, N], BF16)
        v_sb = sb("v_sb", [P, 2, BLK, C])
        rowmax = sb("rowmax", [P, 2, 2, 4])
        rowm = sb("rowm", [P, 2, 4])
        negm = sb("negm", [P, 2, 4, 2], BF16)
        probs = sb("probs", [P, 16, HALF])
        rden = sb("rden", [P, HALF])
        avn = sb("avn", [P, N])

        x_res = sb("x_res", [P, N])
        xr = sb("xr", [P, N])
        t1 = sb("t1", [P, BLK, C])
        stats = sb("stats", [P, 2, BLK, 6])
        mv = sb("mv", [P, 2, BLK, 2])
        rstd = sb("rstd", [P, 2, 3, BLK])
        z = sb("z", [P, BLK, C])
        gsum = sb("gsum", [P, BLK * NG])
        d16 = sb("d16", [P, BLK, C])
        sq16 = sb("sq16", [P, BLK, C])
        ss16 = sb("ss16", [P, 3, BLK * NG])
        rs16 = sb("rs16", [P, 2, BLK * NG])
        u = sb("u", [P, BLK, C + 1])
        usum = sb("usum_sb", [P, 1])
        udiag = sb("udiag", [P, P])
        kvw = sb("kvw", [P, 5, P])
        kcc = sb("kcc", [P, 1])
        bd = sb("bd", [P, P])
        zT = sb("zT", [P, N])
        t2 = sb("t2", [P, BLK, C])
        z2 = sb("z2", [P, BLK, C])
        z2T = sb("z2T", [P, N])
        lg = sb("lg", [P, 9, BLK, E])
        lred = sb("lred", [P, 7, BLK])
        cw = sb("cw", [P, B, BLK, E])

        ring = probs[:, :, :]
        w1 = qs1[:, 0, :, :].rearrange("p h n -> p (h n)").bitcast(F32).rearrange("p (e i) -> p e i", e=E)
        w2 = qs1[:, 1, :, :].rearrange("p h n -> p (h n)").bitcast(F32)\
            .rearrange("p (e j c) -> p e j c", e=E, j=HC)
        z2T_t = [ring[:, i, :] for i in (0, 1)]
        t2_t = [ring[:, i, :].rearrange("p (k c) -> p k c", c=C) for i in (2, 3)]
        acc = [ring[:, i, :].rearrange("p (k c) -> p k c", c=C) for i in (4, 5)]
        outT = [ring[:, i, :] for i in (6, 7)]
        hid = [[ring[:, 8 + 2 * i + j, :] for j in range(HC)] for i in (0, 1)]
        cw_t = [ring[:, 14 + i, 0:4 * E].rearrange("p (k e) -> p k e", e=E) for i in (0, 1)]
        cwT = [ring[0:E, 12 + i, :] for i in (0, 1)]

        bank = [ctx.enter_context(nc.psum_tensor(f"bank{i}", [P, 512], F32)) for i in range(8)]
        row_ps, st_ps, av_ps, den_ps, shared_ps = bank[0:2], bank[2:4], bank[4], bank[5], bank[6:8]

        waits_passed = sem("waits_passed")
        weights_in = sem("weights_in")
        pool_const = sem("pool_const")
        dve_const = sem("dve_const")
        bn_step = sem("bn_step")
        wT_ps = sem("wT_ps")
        wT_ready = sem("wT_ready")
        ones_rows = sem("ones_rows")
        x_loaded = [sem(f"x_loaded{i}") for i in (0, 1)]
        xn_ready = sem("xn_ready")
        shared_ready = [sem(f"shared_ready{i}") for i in (0, 1)]
        high_ready = sem("high_ready")
        rest_ready = sem("rest_ready")
        mid_ready = sem("mid_ready")
        low_ready = sem("low_ready")
        stacked = [sem(f"stacked{i}") for i in (0, 1)]
        v_ready = sem("v_ready")
        row_ready = sem("row_ready")
        row_used = sem("row_used")
        max_step = sem("max_step")
        negm_ready = sem("negm_ready")
        mrow_ready = sem("mrow_ready")
        st_ready = sem("st_ready")
        exp_done = sem("exp_done")
        probs_used = sem("probs_used")
        rden_ready = sem("rden_ready")
        norm_done = sem("norm_done")
        xres_loaded = sem("xres_loaded")
        xr_ready = sem("xr_ready")
        t1_ready = sem("t1_ready")
        stats_done = [sem(f"stats_done{i}") for i in (0, 1)]
        mv_ready = [sem(f"mv_ready{i}") for i in (0, 1)]
        rstd_step = [sem(f"rstd_step{i}") for i in (0, 1)]
        z_ready = sem("z_ready")
        z2_ready = sem("z2_ready")
        zT_ready = sem("zT_ready")
        gsum_ready = sem("gsum_ready")
        d_ready = sem("d_ready")
        sq_ready = sem("sq_ready")
        ss_ready = sem("ss_ready")
        std_step = sem("std_step")
        std_ready = sem("std_ready")
        rs_step = sem("rs_step")
        u_ready = sem("u_ready")
        kv_step = sem("kv_step")
        udiag_ready = sem("udiag_ready")
        bd_ready = sem("bd_ready")
        t2_ready = sem("t2_ready")
        z2T_ready = sem("z2T_ready")
        lmax_step = sem("lmax_step")
        lsub_ready = sem("lsub_ready")
        gexp_ready = sem("gexp_ready")
        gate_step = sem("gate_step")
        cw_ready = sem("cw_ready")
        t2_stored = sem("t2_stored")
        z2T_stored = sem("z2T_stored")
        experts_in = sem("experts_in")
        tile_loaded = [sem(f"tile_loaded{i}") for i in (0, 1)]
        cw_copied = sem("cw_copied")
        cwT_ps = sem("cwT_ps")
        cwT_ready = sem("cwT_ready")
        bias_ps = sem("bias_ps")
        acc_step = sem("acc_step")
        hid_ps = sem("hid_ps")
        hid_ready = sem("hid_ready")
        y_ps = sem("y_ps")
        y_used = sem("y_used")
        outT_ps = sem("outT_ps")
        outT_ready = sem("outT_ready")
        out_stored = [sem(f"out_stored{i}") for i in (0, 1)]

        N_WEIGHT_DMAS = 3 + 1 + 4 + 2 * NH + 1 + NH + 2 + 2 + 2 + 1 + 1
        STACK_DMAS = 12 * NH
        block = ctx.enter_context(nc.Block())

        @block.sync
        def _(sp):
            n = [0]

            def load(dst, src):
                sp.dma_start(dst, src).then_inc(weights_in, 16)
                n[0] += 1

            for j in range(3):
                load(wload[:, j, :], L0_conv_qkv_w[j * P:(j + 1) * P, :])
            load(woload[:, :], L0_conv_out_w)
            for j, v in enumerate((L0_conv_gamma, L0_conv_beta, L0_conv_run_mean, L0_conv_run_var)):
                load(bn[:, j:j + 1], v.rearrange("(c a) -> c a", a=1))
            qkv_b = L0_conv_qkv_b.rearrange("(n j d) -> n j d", n=NH, j=3)
            for h in range(NH):
                for j in range(2):
                    load(bqk[HD * h:HD * h + HD, j:j + 1], qkv_b[h, j, :].rearrange("(d a) -> d a", a=1))
            load(bo[:, :], L0_conv_out_b.rearrange("(c a) -> c a", a=1))
            for h in range(NH):
                load(bv_row[:, h, :], qkv_b[h, 2, :].rearrange("(a d) -> a d", a=1).broadcast_to([P, HD]))
            for j, v in enumerate((L1_attn_kln_weight, L1_attn_kln_bias)):
                load(kcol[:, j:j + 1], v.rearrange("h a d -> (h d) a"))
            for j, v in enumerate((L1_attn_vln_weight, L1_attn_vln_bias)):
                load(vrow[:, j, :], v.rearrange("h a d -> a (h d)").broadcast_to([P, C]))
            load(gate_w[:, :], L1_ffn_gate_w)
            load(gate_b[:, :], L1_ffn_gate_b.rearrange("(a e) -> a e", a=1).broadcast_to([P, E]))
            load(b1_rows[:, :], L1_ffn_b1.rearrange("e (j p) -> (e j) p", p=P))
            load(b2[:, :], L1_ffn_b2)
            assert n[0] == N_WEIGHT_DMAS, n[0]

            def iteration(pair, p):
                if in_range(1, pair, p):
                    b, pr, par = image(1, pair, p)
                    if isinstance(pair, int) and 2 * pair + p == FIRST:
                        sp.dma_start(x_in[:, par, :], x_v[number(b)]).then_inc(x_loaded[par], 16)
                    if in_range(2, pair, p):
                        bn_, _, par2 = image(2, pair, p)
                        if positive(bn_ - 1):
                            sp.wait_ge(xn_ready, count(sp, bn_ - 1))
                            apart(sp, bn_ - 1)
                        sp.dma_start(x_in[:, par2, :], x_v[number(bn_)]).then_inc(x_loaded[par2], 16)
                    if positive(64 * (b - 1)):
                        sp.wait_ge(exp_done, count(sp, 64 * (b - 1)))
                        apart(sp, 64 * (b - 1))
                    sp.wait_ge(high_ready, count(sp, 4 * b + 4))
                    apart(sp, 4 * b + 4)
                    sp.wait_ge(mid_ready, count(sp, 4 * b + 4))
                    apart(sp, 4 * b + 4)
                    sp.wait_ge(low_ready, count(sp, 4 * b + 4))
                    apart(sp, 4 * b + 4)
                    HI, MI, LO = 0, 1, 2
                    for h in range(NH):
                        src = slice(HD * h, HD * h + HD)
                        for which, s1, s2 in ((0, qs1, qs2), (1, ks1, ks2)):
                            first = (HI, HI, MI, MI) if which == 0 else (HI, MI, HI, MI)
                            second = (HI, LO) if which == 0 else (LO, HI)
                            for g, k in enumerate(first):
                                sp.dma_start(s1[HD * g:HD * g + HD, par, h, :],
                                             part[src, k, which, :]).then_inc(stacked[par], 16)
                            for g, k in enumerate(second):
                                sp.dma_start(s2[HD * g:HD * g + HD, par, h, :],
                                             part[src, k, which, :]).then_inc(stacked[par], 16)
                if in_range(0, pair, p):
                    b, _, _ = image(0, pair, p)
                    if positive(b):
                        sp.wait_ge(xr_ready, count(sp, b))
                        apart(sp, b)
                    sp.dma_start(x_res[:, :], x_v[number(b)]).then_inc(xres_loaded, 16)
                if in_range(-2, pair, p):
                    b, _, _ = image(-2, pair, p)
                    sp.wait_ge(t2_ready, count(sp, 2 * b + 2))
                    apart(sp, 2 * b + 2)
                    sp.dma_start(t2_dram[number(b)], t2[:, :, :]).then_inc(t2_stored, 16)
                    sp.wait_ge(z2T_ready, count(sp, 2 * b + 2))
                    apart(sp, 2 * b + 2)
                    sp.dma_start(z2T_dram[number(b)], z2T[:, :]).then_inc(z2T_stored, 16)

            iterations(sp, iteration)

            sp.wait_ge(t2_stored, 16 * B)
            sp.wait_ge(z2T_stored, 16 * B)
            sp.wait_ge(probs_used, 8 * B)
            sp.dma_start(w1, L1_ffn_W1.rearrange("e c h -> c e h")).then_inc(experts_in, 16)
            sp.dma_start(w2, L1_ffn_W2.rearrange("e (j p) c -> p e j c", p=P)).then_inc(experts_in, 16)

            def load_tile(b, half, k):
                if positive((k - 1) * (1 + E)):
                    sp.wait_ge(acc_step, count(sp, (k - 1) * (1 + E)))
                sp.dma_start(z2T_t[half], z2T_dram[b, :, half * HALF:(half + 1) * HALF])\
                  .then_inc(tile_loaded[half], 16)
                sp.dma_start(t2_t[half], t2_dram[b, :, 4 * half:4 * half + 4, :])\
                  .then_inc(tile_loaded[half], 16)

            def store_tile(b, half, k):
                sp.wait_ge(outT_ready, count(sp, k + 1))
                sp.dma_start(out_v[b, :, half * HALF:(half + 1) * HALF], outT[half])\
                  .then_inc(out_stored[half], 16)

            load_tile(0, 0, 0)
            load_tile(0, 1, 1)
            with sp.Fori(1, B) as b:
                for half in range(2):
                    load_tile(b, half, 2 * b + half)
                    store_tile(b - 1, half, 2 * b - 2 + half)
            for half in range(2):
                store_tile(B - 1, half, 2 * B - 2 + half)
            for half in range(2):
                sp.wait_ge(out_stored[half], 16 * B)

        @block.gpsimd
        def _(pool):
            g = nc.gpsimd
            g.memset(ident[:, :], 0.0).then_inc(pool_const, 1)
            g.memset(ones[:, :], 1.0).then_inc(pool_const, 1)
            g.memset(headmask[:, :], 1.0 / N).then_inc(pool_const, 1)
            g.memset(power[:, 0, :], -0.5).then_inc(pool_const, 1)
            g.memset(power[:, 1, :], 0.5).then_inc(pool_const, 1)
            pool.wait_ge(pool_const, 5)
            g.affine_select(out=ident[:, :], in_=ident[:, :], compare_op=ALU.not_equal, fill=1.0,
                            base=0, pattern=[[-1, P]], channel_multiplier=1).then_inc(pool_const, 1)
            hm = headmask[:, :].rearrange("p (g d) -> p g d", d=G16)
            g.affine_select(out=hm, in_=hm, compare_op=ALU.is_ge, fill=0.0, base=0,
                            pattern=[[-G16, NG], [0, G16]], channel_multiplier=1).then_inc(pool_const, 1)
            pool.wait_ge(pool_const, 7)
            g.affine_select(out=hm, in_=hm, compare_op=ALU.is_ge, fill=0.0, base=G16 - 1,
                            pattern=[[G16, NG], [0, G16]], channel_multiplier=-1).then_inc(pool_const, 1)
            for e in range(E):
                g.memset(rank_w[:, e:e + 1], float(E - e)).then_inc(pool_const, 1)
            g.memset(u[:, :, C:C + 1], 1.0).then_inc(pool_const, 1)
            pool.wait_ge(pool_const, 9 + E)
            pool.wait_ge(weights_in, 16 * N_WEIGHT_DMAS)
            g.tensor_scalar(bn_tmp[:, 0:1], bn[:, 3:4], EPS_BN, 1.0, ALU.add, ALU.mult).then_inc(bn_step, 1)
            pool.wait_ge(bn_step, 1)
            g.tensor_tensor(bn_tmp[:, 1:2], bn_tmp[:, 0:1], power[:, 0, 0:1], ALU.pow).then_inc(bn_step, 1)

            def split_ml(b, c):
                half, which = c // 2, c % 2
                cols = slice(half * HALF, (half + 1) * HALF)
                pool.wait_ge(rest_ready, count(pool, 4 * b + c + 1))
                apart(pool, 4 * b + c + 1)
                g.tensor_scalar(part[:, 1, which, cols], rest[:, c % 2, :], 1.0, 0.0, ALU.mult, ALU.add)\
                 .then_inc(mid_ready, 1)
                pool.wait_ge(mid_ready, count(pool, 4 * b + c + 1))
                apart(pool, 4 * b + c + 1)
                g.tensor_tensor(part[:, 2, which, cols], rest[:, c % 2, :], part[:, 1, which, cols],
                                ALU.subtract).then_inc(low_ready, 1)

            def normalise(b, which, src, dst, done):
                step = rstd_step[which]
                pool.wait_ge(mv_ready[which], count(pool, b + 1))
                apart(pool, b + 1)
                r = rstd[:, which, :, :]
                g.tensor_scalar(r[:, 0, :], mv[:, which, :, 1], EPS_LN, 1.0, ALU.add, ALU.mult)\
                 .then_inc(step, 1)
                pool.wait_ge(step, count(pool, 4 * b + 1))
                apart(pool, 4 * b + 1)
                g.tensor_tensor(r[:, 1, :], r[:, 0, :], power[:, 0, 0:BLK], ALU.pow).then_inc(step, 1)
                pool.wait_ge(step, count(pool, 4 * b + 2))
                apart(pool, 4 * b + 2)
                g.tensor_tensor(r[:, 2, :], mv[:, which, :, 0], r[:, 1, :], ALU.mult).then_inc(step, 1)
                pool.wait_ge(step, count(pool, 4 * b + 3))
                apart(pool, 4 * b + 3)
                g.tensor_scalar(r[:, 0, :], r[:, 2, :], -1.0, 0.0, ALU.mult, ALU.add).then_inc(step, 1)
                pool.wait_ge(step, count(pool, 4 * b + 4))
                apart(pool, 4 * b + 4)
                for k in range(BLK):
                    g.tensor_scalar(dst[:, k, :], src[:, k, :], r[:, 1, k:k + 1], r[:, 0, k:k + 1],
                                    ALU.mult, ALU.add).then_inc(done, 1)

            def iteration(pair, p):
                if in_range(1, pair, p):
                    b, _, _ = image(1, pair, p)
                    if True:
                        bp, prp, parp = image(0, pair, p)
                        pool.wait_ge(stacked[parp], count(pool, 16 * STACK_DMAS * (prp + 1)))
                        apart(pool, 16 * STACK_DMAS * (prp + 1))
                    for c in range(4):
                        split_ml(b, c)
                if in_range(-1, pair, p):
                    b, _, _ = image(-1, pair, p)
                    pool.wait_ge(xres_loaded, count(pool, 16 * b + 16))
                    apart(pool, 16 * b + 16)
                    g.tensor_scalar(xr[:, :], x_res[:, :], bo[:, :], 1.0, ALU.add, ALU.mult)\
                     .then_inc(xr_ready, 1)
                if in_range(-2, pair, p):
                    b, _, _ = image(-2, pair, p)
                    normalise(b, 1, t2, z2, z2_ready)
                if in_range(-1, pair, p):
                    b, _, _ = image(-1, pair, p)
                    normalise(b, 0, t1, z, z_ready)
                    pool.wait_ge(ss_ready, count(pool, b + 1))
                    apart(pool, b + 1)
                    g.tensor_scalar(ss16[:, 1, :], ss16[:, 0, :], 1.0 / (G16 - 1), 0.0, ALU.mult, ALU.add)\
                     .then_inc(std_step, 1)
                    pool.wait_ge(std_step, count(pool, b + 1))
                    apart(pool, b + 1)
                    g.tensor_tensor(ss16[:, 2, :], ss16[:, 1, :], power[:, 1, :], ALU.pow)\
                     .then_inc(std_ready, 1)

            iterations(pool, iteration)

        @block.scalar
        def _(act):
            a = nc.scalar
            act.wait_ge(weights_in, 16 * N_WEIGHT_DMAS)
            act.wait_ge(pool_const, 9 + E)

            def from_shared(name, pair, p):
                act.wait_ge(shared_ready[BANK[name]], count(act, turn(name, pair, p) + 1))
                return shared_ps[BANK[name]]

            def piece(name, pair, p):
                b, _, par = image(SHARED[name][1], pair, p)
                if name[:4] == "mrow":
                    s = int(name[4:])
                    half, h = (1, s) if s < 4 else (0, s - 4)
                    ps = from_shared(name, pair, p)
                    a.activation(qs2[64:66, par, h, half * HALF:(half + 1) * HALF], ps[64:66, :], ACT.Copy)\
                     .then_inc(mrow_ready, 1)
                elif name in ("q0", "k0", "q1", "k1"):
                    which, half = "qk".index(name[0]), int(name[1])
                    ps = from_shared(name, pair, p)
                    if name == "q0":
                        _, prp, parp = image(0, pair, p)
                        act.wait_ge(stacked[parp], count(act, 16 * STACK_DMAS * (prp + 1)))
                    a.activation(part[:, 0, which, half * HALF:(half + 1) * HALF], ps[:, :], ACT.Identity,
                                 bias=bqk[:, which:which + 1]).then_inc(high_ready, 1)
                elif name[:4] == "proj":
                    half = int(name[4])
                    ps = from_shared(name, pair, p)
                    if positive(2 * b):
                        act.wait_ge(t2_ready, count(act, 2 * b))
                    a.activation(t1[:, 4 * half:4 * half + 4, :].rearrange("p k c -> p (k c)"), ps[:, :],
                                 ACT.Copy).then_inc(t1_ready, 1)
                elif name[:2] == "zT":
                    half = int(name[2])
                    ps = from_shared(name, pair, p)
                    a.activation(zT[:, half * HALF:(half + 1) * HALF], ps[:, :], ACT.Copy)\
                     .then_inc(zT_ready, 1)
                elif name[:3] == "z2T":
                    half = int(name[3])
                    ps = from_shared(name, pair, p)
                    if positive(16 * b):
                        act.wait_ge(z2T_stored, count(act, 16 * b))
                    a.activation(z2T[:, half * HALF:(half + 1) * HALF], ps[:, :], ACT.Copy)\
                     .then_inc(z2T_ready, 1)

            def iteration(pair, p):
                for q in range(QUARTERS):
                    s, j = divmod(q, 4)
                    if in_range(0, pair, p):
                        b, _, par = image(0, pair, p)
                        for t in (2 * j, 2 * j + 1):
                            tile = 64 * b + 8 * s + t
                            if t == 0:
                                if positive(8 * b + s - 1):
                                    act.wait_ge(probs_used, count(act, 8 * b + s - 1))
                            act.wait_ge(st_ready, count(act, tile + 1))
                            a.activation(probs[:, 8 * (s % 2) + t, :], st_ps[t % 2][:, :], ACT.Exp,
                                         scale=float(C) ** -0.5).then_inc(exp_done, 1)
                    for name in at_quarter(q, pair, p):
                        piece(name, pair, p)
                    if q == 20 and in_range(-1, pair, p):
                        b, _, _ = image(-1, pair, p)
                        act.wait_ge(d_ready, count(act, b + 1))
                        a.activation(sq16[:, :, :], d16[:, :, :], ACT.Square).then_inc(sq_ready, 1)
                    if q == 17 and in_range(-2, pair, p):
                        b, _, _ = image(-2, pair, p)
                        act.wait_ge(lsub_ready, count(act, b + 1))
                        a.activation(lg[:, 1, :, :], lg[:, 0, :, :], ACT.Exp).then_inc(gexp_ready, 1)

            iterations(act, iteration)

            def hidden(k, e, half):
                n = E * k + e
                for j in range(HC):
                    act.wait_ge(hid_ps, count(act, HC * n + j + 1))
                    if j == 0:
                        if positive(n - 1):
                            act.wait_ge(y_ps, count(act, n - 1))
                    a.activation(hid[e % 2][j], bank[2 * (e % 2) + j][:, :], ACT.Gelu,
                                 bias=b1[:, e, j:j + 1]).then_inc(hid_ready, 1)

            def write_out(b, half):
                k = 2 * b + half
                act.wait_ge(outT_ps, count(act, k + 1))
                if positive(16 * b):
                    act.wait_ge(out_stored[half], count(act, 16 * b))
                a.activation(outT[half], bank[7][:, :], ACT.Copy).then_inc(outT_ready, 1)

            def tile(b, half, first):
                k = 2 * b + half
                act.wait_ge(cwT_ps, count(act, k + 1))
                a.activation(cwT[half], bank[6][0:E, :], ACT.Copy).then_inc(cwT_ready, 1)
                for e in range(E):
                    hidden(k, e, half)
                    if e == 2 and not first:
                        write_out(b - 1 if half == 0 else b, 1 - half)

            tile(0, 0, True)
            tile(0, 1, False)
            with act.Fori(1, B) as b:
                for half in range(2):
                    tile(b, half, False)
            write_out(B - 1, 1)

        @block.vector
        def _(dve):
            v = nc.vector
            dve.wait_ge(weights_in, 16 * N_WEIGHT_DMAS)
            dve.wait_ge(pool_const, 9 + E)
            v.tensor_copy(identb[:, :], ident[:, :]).then_inc(dve_const, 1)
            v.tensor_scalar(kb_n[:, :], kcol[:, 1:2], float(N), None, ALU.mult).then_inc(dve_const, 1)
            for par in range(2):
                v.memset(ks2[64:66, par, :, :], 1.0).then_inc(ones_rows, 1)
            dve.wait_ge(bn_step, 2)
            v.tensor_tensor(bn_scale[:, :], bn_tmp[:, 1:2], bn[:, 0:1], ALU.mult).then_inc(bn_step, 1)
            dve.wait_ge(bn_step, 3)
            v.tensor_tensor(bn_tmp[:, 0:1], bn_scale[:, :], bn[:, 2:3], ALU.mult).then_inc(bn_step, 1)
            dve.wait_ge(bn_step, 4)
            v.tensor_tensor(bn_shift[:, :], bn[:, 1:2], bn_tmp[:, 0:1], ALU.subtract).then_inc(bn_step, 1)
            for j in range(3):
                dve.wait_ge(wT_ps, count(dve, j + 1))
                for blk in range(4):
                    h, kind = divmod(4 * j + blk, 3)
                    v.tensor_copy(wqkvT[:, kind, h, :], bank[j][:, HD * blk:HD * blk + HD]).then_inc(wT_ready, 1)
            dve.wait_ge(wT_ps, 4)
            v.tensor_copy(woT[:, :], bank[3][:, 0:P]).then_inc(wT_ready, 1)
            dve.wait_ge(wT_ps, 5)
            v.tensor_copy(b1[:, :, :].rearrange("p e j -> p (e j)"), bank[4][:, 0:E * HC]).then_inc(wT_ready, 1)
            dve.wait_ge(bn_step, 5)
            dve.wait_ge(dve_const, 2)

            def from_shared(name, pair, p):
                dve.wait_ge(shared_ready[BANK[name]], count(dve, turn(name, pair, p) + 1))
                return shared_ps[BANK[name]]

            def norm(b, half):
                dve.wait_ge(probs_used, count(dve, 8 * b + 4 * half + 4))
                v.reciprocal(rden[:, :], den_ps[:, :]).then_inc(rden_ready, 1)
                dve.wait_ge(rden_ready, count(dve, 2 * b + half + 1))
                if positive(2 * b):
                    dve.wait_ge(t1_ready, count(dve, 2 * b))
                v.tensor_tensor(avn[:, half * HALF:(half + 1) * HALF], av_ps[:, :], rden[:, :], ALU.mult)\
                 .then_inc(norm_done, 1)

            def layer_stats(b, which, src, half):
                blocks = range(4 * half, 4 * half + 4)
                for k in blocks:
                    v.bn_stats(stats[:, which, k, :], src[:, k, :]).then_inc(stats_done[which], 1)
                if half == 1:
                    dve.wait_ge(stats_done[which], count(dve, BLK * b + BLK))
                    apart(dve, BLK * b + BLK)
                    for k in range(BLK):
                        m = v.bn_aggr(mv[:, which, k, :], stats[:, which, k, :])
                    m.then_inc(mv_ready[which], 1)

            def piece(name, pair, p):
                b, _, par = image(SHARED[name][1], pair, p)
                if name in ("q0", "k0", "q1", "k1"):
                    which, half = "qk".index(name[0]), int(name[1])
                    c = 2 * half + which
                    ps = from_shared(name, pair, p)
                    dve.wait_ge(high_ready, count(dve, 4 * b + c + 1))
                    if positive(4 * b + c - 1):
                        dve.wait_ge(low_ready, count(dve, 4 * b + c - 1))
                    v.scalar_tensor_tensor(rest[:, c % 2, :], ps[:, :], bqk[:, which:which + 1],
                                           part[:, 0, which, half * HALF:(half + 1) * HALF],
                                           ALU.add, ALU.subtract).then_inc(rest_ready, 1)
                elif name in ("v0", "v1"):
                    half = int(name[1])
                    ps = from_shared(name, pair, p)
                    bias = bv_row[:, :, :].rearrange("p n d -> p (n d)").unsqueeze(1).broadcast_to([P, 4, C])
                    v.tensor_tensor(v_sb[:, par, 4 * half:4 * half + 4, :],
                                    ps[:, :].rearrange("p (k c) -> p k c", c=C), bias, ALU.add)\
                     .then_inc(v_ready, 1)
                elif name == "gram":
                    ps = from_shared(name, pair, p)
                    v.tensor_copy(usum[:, :], ps[:, C:C + 1]).then_inc(kv_step, 1)
                    dve.wait_ge(kv_step, count(dve, 6 * b + 1))
                    v.tensor_scalar(udiag[:, :], ident[:, :], usum[:, :], None, ALU.mult).then_inc(udiag_ready, 1)
                    v.tensor_scalar(kvw[:, 0, :], ps[:, 0:C], kcol[:, 0:1], None, ALU.mult).then_inc(kv_step, 1)
                    v.scalar_tensor_tensor(kcc[:, :], usum[:, :], kcol[:, 0:1], kb_n[:, :], ALU.mult, ALU.add)\
                     .then_inc(kv_step, 1)
                elif name == "usum":
                    ps = from_shared(name, pair, p)
                    dve.wait_ge(kv_step, count(dve, 6 * b + 3))
                    v.scalar_tensor_tensor(kvw[:, 1, :], ps[:, 0:C], kcol[:, 1:2], kvw[:, 0, :],
                                           ALU.mult, ALU.add).then_inc(kv_step, 1)
                    dve.wait_ge(kv_step, count(dve, 6 * b + 4))
                    v.tensor_tensor(kvw[:, 2, :], kvw[:, 1, :], vrow[:, 0, :], ALU.mult).then_inc(kv_step, 1)
                    dve.wait_ge(kv_step, count(dve, 6 * b + 5))
                    v.scalar_tensor_tensor(kvw[:, 3, :], vrow[:, 1, :], kcc[:, :], kvw[:, 2, :],
                                           ALU.mult, ALU.add).then_inc(kv_step, 1)
                    dve.wait_ge(kv_step, count(dve, 6 * b + 6))
                    v.tensor_tensor(kvw[:, 4, :], kvw[:, 3, :], headmask[:, :], ALU.mult).then_inc(bd_ready, 1)
                    dve.wait_ge(bd_ready, count(dve, 2 * b + 1))
                    v.tensor_tensor(bd[:, :], kvw[:, 4, :], ident[:, :], ALU.add).then_inc(bd_ready, 1)
                elif name[:3] == "t2_":
                    half = int(name[3])
                    ps = from_shared(name, pair, p)
                    if positive(16 * b):
                        dve.wait_ge(t2_stored, count(dve, 16 * b))
                    if positive(BLK * b):
                        dve.wait_ge(z2_ready, count(dve, BLK * b))
                    v.tensor_tensor(t2[:, 4 * half:4 * half + 4, :], ps[:, :].rearrange("p (k c) -> p k c", c=C),
                                    t1[:, 4 * half:4 * half + 4, :], ALU.add).then_inc(t2_ready, 1)
                    dve.wait_ge(t2_ready, count(dve, 2 * b + half + 1))
                    layer_stats(b, 1, t2, half)
                elif name == "logits":
                    ps = from_shared(name, pair, p)
                    pl = ps[:, 0:BLK * E].rearrange("p (k e) -> p k e", e=E)
                    v.tensor_tensor(lg[:, 2, :, :], pl, gate_b[:, :].unsqueeze(1).broadcast_to([P, BLK, E]),
                                    ALU.add).then_inc(lmax_step, 1)
                    dve.wait_ge(lmax_step, count(dve, 2 * b + 1))
                    v.tensor_reduce(lred[:, 0, :], lg[:, 2, :, :], AX.X, ALU.max).then_inc(lmax_step, 1)
                    dve.wait_ge(lmax_step, count(dve, 2 * b + 2))
                    v.tensor_tensor(lg[:, 0, :, :], lg[:, 2, :, :],
                                    lred[:, 0, :].unsqueeze(2).broadcast_to([P, BLK, E]), ALU.subtract)\
                     .then_inc(lsub_ready, 1)

            def gate(b):
                steps = [0]

                def then(ins):
                    steps[0] += 1
                    ins.then_inc(gate_step, 1)
                    dve.wait_ge(gate_step, count(dve, 16 * b + steps[0]))

                def wide(r):
                    return lred[:, r, :].unsqueeze(2).broadcast_to([P, BLK, E])

                rank = rank_w[:, :].unsqueeze(1).broadcast_to([P, BLK, E])
                ex, pr, pr2 = lg[:, 1, :, :], lg[:, 3, :, :], lg[:, 4, :, :]
                w, sel1, sel2, eq = lg[:, 5, :, :], lg[:, 6, :, :], lg[:, 7, :, :], lg[:, 8, :, :]
                dve.wait_ge(gexp_ready, count(dve, b + 1))
                then(v.tensor_reduce(lred[:, 1, :], ex, AX.X, ALU.add))
                then(v.reciprocal(lred[:, 2, :], lred[:, 1, :]))
                then(v.tensor_tensor(pr, ex, wide(2), ALU.mult))
                then(v.tensor_reduce(lred[:, 3, :], pr, AX.X, ALU.max))
                then(v.tensor_tensor(eq, pr, wide(3), ALU.is_equal))
                then(v.tensor_tensor(w, eq, rank, ALU.mult))
                then(v.tensor_reduce(lred[:, 4, :], w, AX.X, ALU.max))
                then(v.tensor_tensor(sel1, w, wide(4), ALU.is_equal))
                then(v.scalar_tensor_tensor(pr2, sel1, -2.0, pr, ALU.mult, ALU.add))
                then(v.tensor_reduce(lred[:, 5, :], pr2, AX.X, ALU.max))
                then(v.tensor_tensor(eq, pr2, wide(5), ALU.is_equal))
                then(v.tensor_tensor(w, eq, rank, ALU.mult))
                then(v.tensor_reduce(lred[:, 6, :], w, AX.X, ALU.max))
                then(v.tensor_tensor(sel2, w, wide(6), ALU.is_equal))
                then(v.tensor_tensor(eq, sel1, sel2, ALU.add))
                assert steps[0] == 15
                v.tensor_tensor(cw[:, number(b), :, :], pr, eq, ALU.mult).then_inc(gate_step, 1)

            def row_target(r):
                return (0, 1, r) if r < 4 else (1, 0, r - 4) if r < 8 else (1, 1, 0)

            def iteration(pair, p):
                for q in range(QUARTERS):
                    s, j = divmod(q, 4)
                    lag, half, h = row_target(s + 1)
                    if in_range(lag, pair, p):
                        b, _, _ = image(lag, pair, p)
                        for kh in range(2):
                            n = 64 * b + 32 * half + 8 * h + 2 * j + kh
                            dve.wait_ge(row_ready, count(dve, n + 1))
                            v.tensor_reduce(rowmax[:, h % 2, kh, j:j + 1], row_ps[kh][:, :], AX.X, ALU.max)\
                             .then_inc(row_used, 1)
                        if j == 3:
                            g = 8 * b + 4 * half + h
                            dve.wait_ge(row_used, count(dve, 8 * g + 8))
                            v.tensor_tensor(rowm[:, h % 2, :], rowmax[:, h % 2, 0, :], rowmax[:, h % 2, 1, :],
                                            ALU.max).then_inc(max_step, 1)
                            dve.wait_ge(max_step, count(dve, 2 * g + 1))
                            if positive(g - 1):
                                dve.wait_ge(mrow_ready, count(dve, g - 1))
                            v.tensor_scalar(negm[:, h % 2, :, 0], rowm[:, h % 2, :], -1.0, None, ALU.mult)\
                             .then_inc(max_step, 1)
                            dve.wait_ge(max_step, count(dve, 2 * g + 2))
                            v.scalar_tensor_tensor(negm[:, h % 2, :, 1], rowm[:, h % 2, :], -1.0,
                                                   negm[:, h % 2, :, 0], ALU.mult, ALU.subtract)\
                             .then_inc(negm_ready, 1)
                    if q == 0 and in_range(1, pair, p):
                        b, pr, par = image(1, pair, p)
                        dve.wait_ge(x_loaded[par], count(dve, 16 * (pr + 1)))
                        v.tensor_scalar(xn[:, :], x_in[:, par, :], bn_scale[:, :], bn_shift[:, :],
                                        ALU.mult, ALU.add).then_inc(xn_ready, 1)
                    if q == 4 and in_range(-1, pair, p):
                        norm(image(-1, pair, p)[0], 1)
                    if q == 20 and in_range(0, pair, p):
                        norm(image(0, pair, p)[0], 0)
                    for name in at_quarter(q, pair, p):
                        piece(name, pair, p)
                    if in_range(-1, pair, p):
                        b, _, _ = image(-1, pair, p)
                        if q in (11, 12):
                            half1 = q - 11
                            dve.wait_ge(t1_ready, count(dve, 2 * b + half1 + 1))
                            layer_stats(b, 0, t1, half1)
                        if q == 18:
                            dve.wait_ge(z_ready, count(dve, BLK * b + BLK))
                            v.tensor_reduce(gsum[:, :], z[:, :, :].rearrange("p k (g d) -> p (k g) d", d=G16),
                                            AX.X, ALU.add).then_inc(gsum_ready, 1)
                            dve.wait_ge(gsum_ready, count(dve, b + 1))
                            v.scalar_tensor_tensor(
                                d16[:, :, :].rearrange("p k (g d) -> p (k g) d", d=G16),
                                gsum[:, :].unsqueeze(2).broadcast_to([P, BLK * NG, G16]), -1.0 / G16,
                                z[:, :, :].rearrange("p k (g d) -> p (k g) d", d=G16),
                                ALU.mult, ALU.add).then_inc(d_ready, 1)
                        if q == 22:
                            dve.wait_ge(sq_ready, count(dve, b + 1))
                            v.tensor_reduce(ss16[:, 0, :], sq16[:, :, :].rearrange("p k (g d) -> p (k g) d", d=G16),
                                            AX.X, ALU.add).then_inc(ss_ready, 1)
                        if q == 27:
                            dve.wait_ge(std_ready, count(dve, b + 1))
                            v.tensor_scalar(rs16[:, 0, :], ss16[:, 2, :], EPS_HEAD, None, ALU.add)\
                             .then_inc(rs_step, 1)
                            dve.wait_ge(rs_step, count(dve, 2 * b + 1))
                            v.reciprocal(rs16[:, 1, :], rs16[:, 0, :]).then_inc(rs_step, 1)
                            dve.wait_ge(rs_step, count(dve, 2 * b + 2))
                            v.tensor_tensor(u[:, :, 0:C].rearrange("p k (g d) -> p k g d", d=G16),
                                            d16[:, :, :].rearrange("p k (g d) -> p k g d", d=G16),
                                            rs16[:, 1, :].rearrange("p (k g) -> p k g", g=NG).unsqueeze(3)
                                            .broadcast_to([P, BLK, NG, G16]), ALU.mult).then_inc(u_ready, 1)
                    if q == 19 and in_range(-2, pair, p):
                        gate(image(-2, pair, p)[0])

            iterations(dve, iteration)

            def tile(b, half, last_tile=False):
                k = 2 * b + half
                dve.wait_ge(cw_copied, count(dve, k + 1))
                dve.wait_ge(tile_loaded[half], count(dve, 32 * b + 32))
                dve.wait_ge(bias_ps, count(dve, k + 1))
                if positive(k - 1):
                    dve.wait_ge(outT_ps, count(dve, k - 1))
                v.tensor_tensor(acc[half], bank[6][:, :].rearrange("p (k c) -> p k c", c=C), t2_t[half],
                                ALU.add).then_inc(acc_step, 1)
                dve.wait_ge(acc_step, count(dve, (1 + E) * k + 1))
                if half == 0:
                    v.tensor_copy(cw_t[1], cw[:, b, 4:8, :]).then_inc(cw_copied, 1)
                elif not last_tile:
                    v.tensor_copy(cw_t[0], cw[:, b + 1, 0:4, :]).then_inc(cw_copied, 1)
                for e in range(E):
                    n = E * k + e
                    dve.wait_ge(y_ps, count(dve, n + 1))
                    dve.wait_ge(acc_step, count(dve, (1 + E) * k + e + 1))
                    for i in range(4):
                        last = v.scalar_tensor_tensor(
                            acc[half][:, i, :], bank[4 + e % 2][:, i * C:(i + 1) * C],
                            cw_t[half][:, i, e:e + 1], acc[half][:, i, :], ALU.mult, ALU.add)
                    last.then_inc(acc_step, 1)

            dve.wait_ge(gate_step, 16 * B)
            dve.wait_ge(probs_used, 8 * B)
            v.tensor_copy(cw_t[0], cw[:, 0, 0:4, :]).then_inc(cw_copied, 1)
            tile(0, 0)
            tile(0, 1)
            with dve.Fori(1, B - 1) as b:
                tile(b, 0)
                tile(b, 1)
            tile(B - 1, 0)
            tile(B - 1, 1, last_tile=True)

        @block.tensor
        def _(pe):
            t_ = nc.tensor
            pe.wait_ge(weights_in, 16 * N_WEIGHT_DMAS)
            pe.wait_ge(pool_const, 9 + E)
            for j in range(3):
                t_.transpose(bank[j][:, 0:P], wload[:, j, :], ident[:, :]).then_inc(wT_ps, 1)
            t_.transpose(bank[3][:, 0:P], woload[:, :], ident[:, :]).then_inc(wT_ps, 1)
            t_.transpose(bank[4][:, 0:E * HC], b1_rows[:, :], ident[0:E * HC, 0:E * HC]).then_inc(wT_ps, 1)
            pe.wait_ge(wT_ready, 14)
            pe.wait_ge(ones_rows, 2)
            pe.wait_ge(dve_const, 2)

            def piece(name, pair, p):
                b, _, par = image(SHARED[name][1], pair, p)
                bk = BANK[name]
                ps = shared_ps[bk]
                if name in ("q0", "k0", "q1", "k1"):
                    which, half = "qk".index(name[0]), int(name[1])
                    pe.wait_ge(xn_ready, count(pe, b + 1))
                    free_shared(name, pair, p)
                    last = t_.matmul(ps[:, :], wqkvT[:, which, :, :].rearrange("p n d -> p (n d)"),
                                     xn[:, half * HALF:(half + 1) * HALF], start=True, stop=True)
                elif name in ("v0", "v1"):
                    free_shared(name, pair, p)
                    half = int(name[1])
                    for i in range(4):
                        k = 4 * half + i
                        last = t_.matmul(ps[:, i * C:(i + 1) * C], xn[:, k * P:(k + 1) * P],
                                         wqkvT[:, 2, :, :].rearrange("p n d -> p (n d)"), start=True, stop=True)
                elif name[:4] == "mrow":
                    s = int(name[4:])
                    half, h = (1, s) if s < 4 else (0, s - 4)
                    pe.wait_ge(negm_ready, count(pe, 8 * b + 4 * half + h + 1))
                    free_shared(name, pair, p)
                    for i in range(4):
                        last = t_.matmul(ps[64:66, i * P:(i + 1) * P], negm[:, h % 2, i, :], identb[:, :],
                                         start=True, stop=True)
                elif name[:4] == "proj":
                    half = int(name[4])
                    pe.wait_ge(xr_ready, count(pe, b + 1))
                    pe.wait_ge(norm_done, count(pe, 2 * b + half + 1))
                    free_shared(name, pair, p)
                    for i in range(4):
                        k = 4 * half + i
                        o = ps[:, i * C:(i + 1) * C]
                        t_.matmul(o, avn[:, k * P:(k + 1) * P], woT[:, :], start=True, stop=False)
                        last = t_.matmul(o, xr[:, k * P:(k + 1) * P], ident[:, :], start=False, stop=True)
                elif name[:2] == "zT":
                    half = int(name[2])
                    pe.wait_ge(z_ready, count(pe, BLK * b + 4 * half + 4))
                    free_shared(name, pair, p)
                    for i in range(4):
                        last = t_.transpose(ps[:, i * P:(i + 1) * P], z[:, 4 * half + i, :], ident[:, :])
                elif name == "gram":
                    pe.wait_ge(u_ready, count(pe, b + 1))
                    free_shared(name, pair, p)
                    for k in range(BLK):
                        last = t_.matmul(ps[:, 0:C + 1], u[:, k, 0:C], u[:, k, :],
                                         start=(k == 0), stop=(k == BLK - 1))
                elif name == "usum":
                    pe.wait_ge(udiag_ready, count(pe, b + 1))
                    free_shared(name, pair, p)
                    last = t_.matmul(ps[:, 0:C], ones[:, :], udiag[:, :], start=True, stop=True)
                elif name[:3] == "t2_":
                    half = int(name[3])
                    pe.wait_ge(zT_ready, count(pe, 2 * b + half + 1))
                    pe.wait_ge(bd_ready, count(pe, 2 * b + 2))
                    free_shared(name, pair, p)
                    for i in range(4):
                        k = 4 * half + i
                        last = t_.matmul(ps[:, i * C:(i + 1) * C], zT[:, k * P:(k + 1) * P], bd[:, :],
                                         start=True, stop=True)
                elif name[:3] == "z2T":
                    half = int(name[3])
                    pe.wait_ge(z2_ready, count(pe, BLK * b + 4 * half + 4))
                    free_shared(name, pair, p)
                    for i in range(4):
                        last = t_.transpose(ps[:, i * P:(i + 1) * P], z2[:, 4 * half + i, :], ident[:, :])
                elif name == "logits":
                    pe.wait_ge(z2T_ready, count(pe, 2 * b + 2))
                    free_shared(name, pair, p)
                    for k in range(BLK):
                        last = t_.matmul(ps[:, k * E:(k + 1) * E], z2T[:, k * P:(k + 1) * P], gate_w[:, :],
                                         start=True, stop=True)
                last.then_inc(shared_ready[bk], 1)

            def free_shared(name, pair, p):
                prev_name, prev_pair, prev_p = previous(name, pair, p)
                if prev_name is None:
                    return
                b = image(SHARED[prev_name][1], prev_pair, prev_p)[0]
                if prev_name in ("q0", "k0", "q1", "k1"):
                    pe.wait_ge(rest_ready, count(pe, 4 * b + 2 * int(prev_name[1]) + "qk".index(prev_name[0]) + 1))
                elif prev_name in ("v0", "v1"):
                    pe.wait_ge(v_ready, count(pe, 2 * b + int(prev_name[1]) + 1))
                elif prev_name[:4] == "mrow":
                    s = int(prev_name[4:])
                    half, h = (1, s) if s < 4 else (0, s - 4)
                    pe.wait_ge(mrow_ready, count(pe, 8 * b + 4 * half + h + 1))
                elif prev_name[:4] == "proj":
                    pe.wait_ge(t1_ready, count(pe, 2 * b + int(prev_name[4]) + 1))
                elif prev_name[:2] == "zT":
                    pe.wait_ge(zT_ready, count(pe, 2 * b + int(prev_name[2]) + 1))
                elif prev_name == "gram":
                    pe.wait_ge(kv_step, count(pe, 6 * b + 3))
                elif prev_name == "usum":
                    pe.wait_ge(kv_step, count(pe, 6 * b + 4))
                elif prev_name[:3] == "t2_":
                    pe.wait_ge(t2_ready, count(pe, 2 * b + int(prev_name[3]) + 1))
                elif prev_name[:3] == "z2T":
                    pe.wait_ge(z2T_ready, count(pe, 2 * b + int(prev_name[3]) + 1))
                elif prev_name == "logits":
                    pe.wait_ge(lmax_step, count(pe, 2 * b + 1))

            def previous(name, pair, p):
                mine = [n for n in ORDER if BANK[n] == BANK[name]]
                i = mine.index(name)
                while True:
                    i -= 1
                    if i < 0:
                        i = len(mine) - 1
                        pair, p = (pair, 0) if p == 1 else (pair - 1, 1)
                        if isinstance(pair, int) and 2 * pair + p < FIRST:
                            return None, None, None
                    if in_range(SHARED[mine[i]][1], pair, p):
                        return mine[i], pair, p

            def row_target(r):
                return (0, 1, r) if r < 4 else (1, 0, r - 4) if r < 8 else (1, 1, 0)

            def iteration(pair, p):
                for q in range(QUARTERS):
                    s, j = divmod(q, 4)
                    if in_range(0, pair, p):
                        b, _, par = image(0, pair, p)
                        half = s // 4
                        for t in (2 * j, 2 * j + 1):
                            kb, h = 2 * (s % 4) + t // 4, t % 4
                            keys = slice(kb * P, (kb + 1) * P)
                            queries = slice(half * HALF, (half + 1) * HALF)
                            tile = 64 * b + 8 * s + t
                            if s % 4 == 0 and t < 4:
                                pe.wait_ge(mrow_ready, count(pe, 8 * b + 4 * half + h + 1))
                            if positive(tile - 1):
                                pe.wait_ge(exp_done, count(pe, tile - 1))
                            t_.matmul(st_ps[t % 2][:, :], ks1[:, par, h, keys], qs1[:, par, h, queries],
                                      start=True, stop=False)
                            t_.matmul(st_ps[t % 2][:, :], ks2[0:66, par, h, keys], qs2[0:66, par, h, queries],
                                      start=False, stop=True).then_inc(st_ready, 1)
                    lag, half, h = row_target(s + 1)
                    if in_range(lag, pair, p):
                        b, pr, par = image(lag, pair, p)
                        if half == 0 and h == 0 and j == 0:
                            pe.wait_ge(stacked[par], count(pe, 16 * STACK_DMAS * (pr + 1)))
                        for kh in range(2):
                            n = 64 * b + 32 * half + 8 * h + 2 * j + kh
                            if positive(n - 1):
                                pe.wait_ge(row_used, count(pe, n - 1))
                            qb = 4 * half + j
                            t_.matmul(row_ps[kh][:, :], qs1[:, par, h, qb * P:(qb + 1) * P],
                                      ks1[:, par, h, kh * HALF:(kh + 1) * HALF], start=True, stop=True)\
                              .then_inc(row_ready, 1)
                    lag, sv = (0, s - 1) if s > 0 else (-1, STEPS - 1)
                    if in_range(lag, pair, p) and j > 0:
                        b, _, par = image(lag, pair, p)
                        half, slot = sv // 4, 8 * (sv % 2)
                        first, last_kb = 2 * (sv % 4), 2 * (sv % 4) + 1
                        if j < 3:
                            kb = first + j - 1
                            pe.wait_ge(exp_done, count(pe, 64 * b + 8 * sv + 4 * j))
                            if kb == 0:
                                if positive(2 * b + half):
                                    pe.wait_ge(norm_done, count(pe, 2 * b + half))
                                pe.wait_ge(v_ready, count(pe, 2 * b + 2))
                            for h in range(NH):
                                rows = slice(HD * h, HD * h + HD)
                                t_.matmul(av_ps[rows, :], v_sb[:, par, kb, rows], probs[:, slot + 4 * (j - 1) + h, :],
                                          start=(kb == 0), stop=(kb == NKB - 1))
                        else:
                            for kb in (first, last_kb):
                                for h in range(NH):
                                    rows = slice(HD * h, HD * h + HD)
                                    mm = t_.matmul(den_ps[rows, :], ones[:, 0:HD],
                                                   probs[:, slot + 4 * (kb - first) + h, :],
                                                   start=(kb == 0), stop=(kb == NKB - 1))
                            mm.then_inc(probs_used, 1)
                    for name in at_quarter(q, pair, p):
                        piece(name, pair, p)

            iterations(pe, iteration)

            pe.wait_ge(experts_in, 32)
            pe.wait_ge(gate_step, 16 * B)

            def prepare(b, half):
                k = 2 * b + half
                pe.wait_ge(cw_copied, count(pe, k + 1))
                if positive((1 + E) * (k - 1) + 1):
                    pe.wait_ge(acc_step, count(pe, (1 + E) * (k - 1) + 1))
                for i in range(4):
                    last = t_.transpose(bank[6][0:E, i * P:(i + 1) * P], cw_t[half][:, i, :], ident[:, :])
                last.then_inc(cwT_ps, 1)

            def bias_term(b, half):
                k = 2 * b + half
                pe.wait_ge(cwT_ready, count(pe, k + 1))
                for i in range(4):
                    last = t_.matmul(bank[6][:, i * C:(i + 1) * C], cwT[half][:, i * P:(i + 1) * P], b2[:, :],
                                     start=True, stop=True)
                last.then_inc(bias_ps, 1)

            def up(b, half, e):
                k = 2 * b + half
                n = E * k + e
                if e == 0:
                    pe.wait_ge(tile_loaded[half], count(pe, 32 * b + 32))
                if positive(HC * (n - 1)):
                    pe.wait_ge(hid_ready, count(pe, HC * (n - 1)))
                for j in range(HC):
                    t_.matmul(bank[2 * (e % 2) + j][:, :], w1[:, e, j * P:(j + 1) * P], z2T_t[half],
                              start=True, stop=True).then_inc(hid_ps, 1)

            def down(b, half, e):
                k = 2 * b + half
                n = E * k + e
                pe.wait_ge(hid_ready, count(pe, HC * (n + 1)))
                if e >= 2:
                    if positive((1 + E) * k + e):
                        pe.wait_ge(acc_step, count(pe, (1 + E) * k + e))
                else:
                    if positive((1 + E) * (k - 1) + E + e):
                        pe.wait_ge(acc_step, count(pe, (1 + E) * (k - 1) + E + e))
                for i in range(4):
                    for j in range(HC):
                        last = t_.matmul(bank[4 + e % 2][:, i * C:(i + 1) * C],
                                         hid[e % 2][j][:, i * P:(i + 1) * P], w2[:, e, j, :],
                                         start=(j == 0), stop=(j == HC - 1))
                last.then_inc(y_ps, 1)

            def turn_out(b, half):
                k = 2 * b + half
                pe.wait_ge(acc_step, count(pe, (1 + E) * (k + 1)))
                if positive(k):
                    pe.wait_ge(outT_ready, count(pe, k))
                for i in range(4):
                    last = t_.transpose(bank[7][:, i * P:(i + 1) * P], acc[half][:, i, :], ident[:, :])
                last.then_inc(outT_ps, 1)

            def tile(b, half, first):
                prepare(b, half)
                up(b, half, 0)
                bias_term(b, half)
                for e in range(1, E):
                    up(b, half, e)
                    down(b, half, e - 1)
                    if e == 2 and not first:
                        turn_out(b - 1 if half == 0 else b, 1 - half)
                down(b, half, E - 1)

            tile(0, 0, True)
            tile(0, 1, False)
            with pe.Fori(1, B) as b:
                tile(b, 0, False)
                tile(b, 1, False)
            turn_out(B - 1, 1)


_INS = ['x', 'L0_conv_gamma', 'L0_conv_beta', 'L0_conv_run_mean', 'L0_conv_run_var', 'L0_conv_qkv_w',
        'L0_conv_qkv_b', 'L0_conv_out_w', 'L0_conv_out_b', 'L1_attn_kln_weight', 'L1_attn_kln_bias',
        'L1_attn_vln_weight', 'L1_attn_vln_bias', 'L1_ffn_gate_w', 'L1_ffn_gate_b', 'L1_ffn_W1',
        'L1_ffn_b1', 'L1_ffn_W2', 'L1_ffn_b2']
_OUTS = [((16, 128, 32, 32), 'float32')]


def kernel(**inputs):
    import numpy as _np
    import concourse.bacc as _bacc
    from concourse import mybir as _mybir
    from concourse.bass_utils import run_bass_kernel_spmd as _run

    nc = _bacc.Bacc("TRN2", target_bir_lowering=False, num_devices=1)
    arrays, args = {}, []
    for name in _INS:
        a = _np.ascontiguousarray(inputs[name])
        arrays[f"in_{name}_dram"] = a
        args.append(nc.dram_tensor(f"in_{name}_dram", a.shape, _mybir.dt.from_np(a.dtype), kind="ExternalInput").ap())
    for i, (shape, dtype) in enumerate(_OUTS):
        dt = _mybir.dt.from_np(_np.dtype(dtype))
        args.append(nc.dram_tensor(f"out_{i}_dram", shape, dt, kind="ExternalOutput").ap())
    conv_attention_hybrid_kernel(nc, *args)
    r = _run(nc, [arrays], core_ids=[0])
    got = tuple(r.results[0][f"out_{i}_dram"] for i in range(len(_OUTS)))
    return got[0]
```

```python
from contextlib import ExitStack

import concourse.bass as bass
from concourse import mybir

P = 128
EPS_BN = 1e-5
EPS_LN = 1e-5
EPS_HEAD = 1e-5

ALU = mybir.AluOpType
ACT = mybir.ActivationFunctionType
AX = mybir.AxisListType
F32 = mybir.dt.float32
BF16 = mybir.dt.bfloat16


class Linear:

    def __init__(self, pair, multiples, scratch, scale=1, plus=0):
        self.pair, self.multiples, self.scratch, self.scale, self.plus = pair, multiples, scratch, scale, plus

    def __add__(self, n):
        return Linear(self.pair, self.multiples, self.scratch, self.scale, self.plus + n)

    def __sub__(self, n):
        return self + -n

    def __mul__(self, n):
        return Linear(self.pair, self.multiples, self.scratch, self.scale * n, self.plus * n)

    __radd__, __rmul__ = __add__, __mul__

    def value(self):
        return self.pair * self.scale + self.plus

    def count(self, eng):
        if self.plus == 0:
            return self.multiples[self.scale]
        eng.reg_add(self.scratch, self.multiples[self.scale], self.plus)
        return self.scratch


def number(n):
    return n.value() if isinstance(n, Linear) else n


def conv_attention_hybrid_kernel(
    nc: bass.Bass,
    x: bass.AP,
    L0_conv_gamma: bass.AP,
    L0_conv_beta: bass.AP,
    L0_conv_run_mean: bass.AP,
    L0_conv_run_var: bass.AP,
    L0_conv_qkv_w: bass.AP,
    L0_conv_qkv_b: bass.AP,
    L0_conv_out_w: bass.AP,
    L0_conv_out_b: bass.AP,
    L1_attn_kln_weight: bass.AP,
    L1_attn_kln_bias: bass.AP,
    L1_attn_vln_weight: bass.AP,
    L1_attn_vln_bias: bass.AP,
    L1_ffn_gate_w: bass.AP,
    L1_ffn_gate_b: bass.AP,
    L1_ffn_W1: bass.AP,
    L1_ffn_b1: bass.AP,
    L1_ffn_W2: bass.AP,
    L1_ffn_b2: bass.AP,
    out: bass.AP,
):
    B, C, IMH, IMW = x.shape
    N = IMH * IMW
    BLK = N // P
    NH = 4
    HD = C // NH
    HALF = N // 2
    NKB = N // P
    G16 = L1_attn_kln_weight.shape[2]
    NG = C // G16
    E, _, HID = L1_ffn_W1.shape
    HC = HID // P
    assert C == P and HD == 32 and N == 1024 and B % 2 == 0

    STEPS, QUARTERS = 8, 32
    FIRST, LAST = -1, B + 1
    LOOP_FROM, LOOP_PAIRS = 2, (B - 4) // 2

    x_v = x.rearrange("b c h w -> b c (h w)")
    out_v = out.rearrange("b c h w -> b c (h w)")

    SCALES = (2, 4, 8, 10, 12, 16, 24, 26, 32, 64, 128, 192)

    SHARED = {}
    for s in range(STEPS):
        SHARED[f"mrow{s}"] = (4 * s + 2, 0 if s < 4 else 1)
    SHARED.update({
        "q0": (1, 1), "k0": (2, 1), "q1": (4, 1), "k1": (5, 1), "v0": (6, 1), "v1": (7, 1),
        "proj0": (8, -1), "proj1": (11, -1), "zT0": (19, -1), "zT1": (20, -1),
        "gram": (29, -1), "usum": (30, -1),
        "t2_0": (3, -2), "t2_1": (4, -2), "z2T0": (12, -2), "z2T1": (13, -2), "logits": (16, -2),
    })
    ORDER = sorted(SHARED, key=lambda n: SHARED[n][0])
    BANK = {n: i % 2 for i, n in enumerate(ORDER)}

    def in_range(lag, pair, p):
        return not isinstance(pair, int) or 0 <= 2 * pair + p + lag < B

    def image(lag, pair, p):
        return 2 * (pair + (p + lag) // 2) + (p + lag) % 2, pair + (p + lag) // 2, (p + lag) % 2

    def turn(name, pair, p):
        bank = BANK[name]
        mine = [n for n in ORDER if BANK[n] == bank]
        if isinstance(pair, int):
            it = 2 * pair + p
            done = sum(in_range(SHARED[n][1], 0, k) for k in range(FIRST, it) for n in mine)
            return done + sum(in_range(SHARED[n][1], 0, it) for n in mine[:mine.index(name)])
        before = sum(in_range(SHARED[n][1], 0, k) for k in range(FIRST, LOOP_FROM) for n in mine)
        return 2 * len(mine) * pair + (before + len(mine) * (p - LOOP_FROM) + mine.index(name))

    def at_quarter(q, pair, p):
        return [n for n in ORDER if SHARED[n][0] == q and in_range(SHARED[n][1], pair, p)]

    def iterations(eng, body):
        for it in range(FIRST, LOOP_FROM):
            body(it // 2, it % 2)
        multiples = {m: eng.alloc_register(f"pair_times_{m}") for m in SCALES}
        scratch = eng.alloc_register("wait_value")
        with eng.Fori(LOOP_FROM // 2, LOOP_FROM // 2 + LOOP_PAIRS) as register:
            for scale, multiple in multiples.items():
                eng.reg_mul(multiple, register, scale)
            pair = Linear(register, multiples, scratch)
            body(pair, 0)
            body(pair, 1)
        for it in range(LOOP_FROM + 2 * LOOP_PAIRS, LAST + 1):
            body(it // 2, it % 2)

    def positive(value):
        return not isinstance(value, int) or value > 0

    def count(eng, value):
        return value.count(eng) if isinstance(value, Linear) else value

    def apart(eng, value):
        if isinstance(value, Linear):
            eng.sem_inc(waits_passed, 1)

    def grouped(t):
        return t.rearrange("p k (g d) -> p k g d", d=G16)

    def wide16(r):
        return r.rearrange("p (k g) -> p k g", g=NG).unsqueeze(3).broadcast_to([P, BLK, NG, G16])

    def row_target(r):
        return (0, 1, r) if r < 4 else (1, 0, r - 4) if r < 8 else (1, 1, 0)

    ctx = ExitStack()
    with ctx:
        def sb(name, shape, dt=F32):
            return ctx.enter_context(nc.sbuf_tensor(name, shape, dt))

        def sem(name):
            return ctx.enter_context(nc.semaphore(name))

        t2_dram = nc.dram_tensor("t2_scratch", [B, P, BLK, C], F32, kind="Internal").ap()
        z2T_dram = nc.dram_tensor("z2T_scratch", [B, C, N], F32, kind="Internal").ap()

        ident = sb("ident", [P, P])
        identb = sb("identb", [P, P], BF16)
        ones = sb("ones", [P, P])
        headmask = sb("headmask", [P, P])
        wload = sb("wload", [P, 3, C])
        woload = sb("woload", [P, C])
        wqkvT = sb("wqkvT", [P, 3, NH, HD])
        woT = sb("woT", [P, C])
        bn = sb("bn", [P, 4])
        bn_scale = sb("bn_scale", [P, 1])
        bn_shift = sb("bn_shift", [P, 1])
        bn_tmp = sb("bn_tmp", [P, 2])
        bqk = sb("bqk", [P, 2])
        bv = sb("bv", [P, 1])
        bo = sb("bo", [P, 1])
        kcol = sb("kcol", [P, 2])
        kb_n = sb("kb_n", [P, 1])
        vrow = sb("vrow", [P, 2, C])
        gate_w = sb("gate_w_sb", [P, E])
        gate_b = sb("gate_b_sb", [P, E])
        b1 = sb("b1_sb", [P, E, HC])
        b1_rows = sb("b1_rows", [E * HC, P])
        b2 = sb("b2_sb", [E, C])
        rank_w = sb("rank_w", [P, E])
        power = sb("power", [P, 2, BLK * NG])

        x_in = sb("x_in", [P, 2, N])
        xn = sb("xn", [P, N])
        part = sb("part", [P, 3, 2, N], BF16)
        raw = sb("raw", [P, 2, HALF])
        rest = sb("rest", [P, 2, HALF])
        qs1 = sb("qs1", [P, 2, NH, N], BF16)
        ks1 = sb("ks1", [P, 2, NH, N], BF16)
        qs2 = sb("qs2", [P, 2, NH, N], BF16)
        ks2 = sb("ks2", [P, 2, NH, N], BF16)
        v_sb = sb("v_sb", [P, 2, BLK, C])
        rowmax = sb("rowmax", [P, 2, 2, 4])
        rowm = sb("rowm", [P, 2, 4])
        negm = sb("negm", [P, 2, 4, 2], BF16)
        probs = sb("probs", [P, 16, HALF])
        rden = sb("rden", [P, HALF])
        avn = sb("avn", [P, N])

        x_res = sb("x_res", [P, N])
        xr = sb("xr", [P, N])
        t1 = sb("t1", [P, BLK, C])
        stats = sb("stats", [P, 2, BLK, 6])
        mv = sb("mv", [P, 2, BLK, 2])
        rstd = sb("rstd", [P, 2, 3, BLK])
        z = sb("z", [P, BLK, C])
        gsum = sb("gsum", [P, 2, BLK * NG])
        d16 = sb("d16", [P, BLK, C])
        sq16 = sb("sq16", [P, BLK, C])
        ss16 = sb("ss16", [P, 3, BLK * NG])
        rs16 = sb("rs16", [P, 2, BLK * NG])
        u = sb("u", [P, BLK, C + 1])
        usum = sb("usum_sb", [P, 1])
        udiag = sb("udiag", [P, P])
        kvw = sb("kvw", [P, 5, P])
        kcc = sb("kcc", [P, 1])
        bd = sb("bd", [P, P])
        zT = sb("zT", [P, N])
        t2 = sb("t2", [P, BLK, C])
        z2 = sb("z2", [P, BLK, C])
        z2T = sb("z2T", [P, N])
        lg = sb("lg", [P, 9, BLK, E])
        lred = sb("lred", [P, 7, BLK])
        cw = sb("cw", [P, B, BLK, E])

        ring = probs[:, :, :]
        w1 = qs1[:, 0, :, :].rearrange("p h n -> p (h n)").bitcast(F32).rearrange("p (e i) -> p e i", e=E)
        w2 = qs1[:, 1, :, :].rearrange("p h n -> p (h n)").bitcast(F32)\
            .rearrange("p (e j c) -> p e j c", e=E, j=HC)
        z2T_t = [ring[:, i, :] for i in (0, 1)]
        t2_t = [ring[:, i, :].rearrange("p (k c) -> p k c", c=C) for i in (2, 3)]
        acc = [ring[:, i, :].rearrange("p (k c) -> p k c", c=C) for i in (4, 5)]
        outT = [ring[:, i, :] for i in (6, 7)]
        hid = [[ring[:, 8 + 2 * i + j, :] for j in range(HC)] for i in (0, 1)]
        cw_t = [ring[:, 14 + i, 0:4 * E].rearrange("p (k e) -> p k e", e=E) for i in (0, 1)]
        cwT = [ring[0:E, 12 + i, :] for i in (0, 1)]

        bank = [ctx.enter_context(nc.psum_tensor(f"bank{i}", [P, 512], F32)) for i in range(8)]
        row_ps, st_ps, av_ps, den_ps, shared_ps = bank[0:2], bank[2:4], bank[4], bank[5], bank[6:8]

        waits_passed = sem("waits_passed")
        weights_in = sem("weights_in")
        pool_const = sem("pool_const")
        dve_const = sem("dve_const")
        bn_step = sem("bn_step")
        wT_ps = sem("wT_ps")
        wT_ready = sem("wT_ready")
        ones_rows = sem("ones_rows")
        x_loaded = [sem(f"x_loaded{i}") for i in (0, 1)]
        xn_ready = sem("xn_ready")
        shared_ready = [sem(f"shared_ready{i}") for i in (0, 1)]
        high_ready = sem("high_ready")
        raw_ready = sem("raw_ready")
        rest_ready = sem("rest_ready")
        mid_ready = sem("mid_ready")
        low_ready = sem("low_ready")
        stacked1 = [[sem(f"stacked1_{i}_{h}") for h in range(NH)] for i in (0, 1)]
        stacked2 = [sem(f"stacked2_{i}") for i in (0, 1)]
        v_ready = sem("v_ready")
        row_ready = sem("row_ready")
        row_used = sem("row_used")
        max_step = sem("max_step")
        negm_ready = sem("negm_ready")
        mrow_ready = sem("mrow_ready")
        st_ready = sem("st_ready")
        exp_done = sem("exp_done")
        probs_used = sem("probs_used")
        av_out = sem("av_out")
        rden_ready = sem("rden_ready")
        norm_step = sem("norm_step")
        norm_done = sem("norm_done")
        xres_loaded = sem("xres_loaded")
        xr_ready = sem("xr_ready")
        t1_ready = sem("t1_ready")
        stats_done = [sem(f"stats_done{i}") for i in (0, 1)]
        mv_ready = [sem(f"mv_ready{i}") for i in (0, 1)]
        rstd_step = [sem(f"rstd_step{i}") for i in (0, 1)]
        z_ready = sem("z_ready")
        z2_ready = sem("z2_ready")
        zT_ready = sem("zT_ready")
        gsum_ready = sem("gsum_ready")
        d_ready = sem("d_ready")
        sq_ready = sem("sq_ready")
        ss_ready = sem("ss_ready")
        std_step = sem("std_step")
        std_ready = sem("std_ready")
        rs_step = sem("rs_step")
        u_ready = sem("u_ready")
        kv_step = sem("kv_step")
        udiag_ready = sem("udiag_ready")
        bd_ready = sem("bd_ready")
        t2_ready = sem("t2_ready")
        z2T_ready = sem("z2T_ready")
        lmax_step = sem("lmax_step")
        lsub_ready = sem("lsub_ready")
        gexp_ready = sem("gexp_ready")
        gate_step = sem("gate_step")
        cw_ready = sem("cw_ready")
        t2_stored = sem("t2_stored")
        z2T_stored = sem("z2T_stored")
        experts_in = sem("experts_in")
        tile_loaded = [sem(f"tile_loaded{i}") for i in (0, 1)]
        cw_copied = sem("cw_copied")
        cwT_ps = sem("cwT_ps")
        cwT_ready = sem("cwT_ready")
        bias_ps = sem("bias_ps")
        acc_step = sem("acc_step")
        hid_ps = sem("hid_ps")
        hid_ready = sem("hid_ready")
        y_ps = sem("y_ps")
        y_used = sem("y_used")
        outT_ps = sem("outT_ps")
        outT_ready = sem("outT_ready")
        out_stored = [sem(f"out_stored{i}") for i in (0, 1)]

        N_WEIGHT_DMAS = 3 + 1 + 4 + 2 * NH + 1 + NH + 2 + 2 + 2 + 1 + 1
        STACK1_DMAS = 4
        STACK2_DMAS = 3 * NH
        block = ctx.enter_context(nc.Block())

        @block.sync
        def _(sp):
            n = [0]

            def load(dst, src):
                sp.dma_start(dst, src).then_inc(weights_in, 16)
                n[0] += 1

            for j in range(3):
                load(wload[:, j, :], L0_conv_qkv_w[j * P:(j + 1) * P, :])
            load(woload[:, :], L0_conv_out_w)
            for j, v in enumerate((L0_conv_gamma, L0_conv_beta, L0_conv_run_mean, L0_conv_run_var)):
                load(bn[:, j:j + 1], v.rearrange("(c a) -> c a", a=1))
            qkv_b = L0_conv_qkv_b.rearrange("(n j d) -> n j d", n=NH, j=3)
            for h in range(NH):
                for j in range(2):
                    load(bqk[HD * h:HD * h + HD, j:j + 1], qkv_b[h, j, :].rearrange("(d a) -> d a", a=1))
            load(bo[:, :], L0_conv_out_b.rearrange("(c a) -> c a", a=1))
            for h in range(NH):
                load(bv[HD * h:HD * h + HD, :], qkv_b[h, 2, :].rearrange("(d a) -> d a", a=1))
            for j, v in enumerate((L1_attn_kln_weight, L1_attn_kln_bias)):
                load(kcol[:, j:j + 1], v.rearrange("h a d -> (h d) a"))
            for j, v in enumerate((L1_attn_vln_weight, L1_attn_vln_bias)):
                load(vrow[:, j, :], v.rearrange("h a d -> a (h d)").broadcast_to([P, C]))
            load(gate_w[:, :], L1_ffn_gate_w)
            load(gate_b[:, :], L1_ffn_gate_b.rearrange("(a e) -> a e", a=1).broadcast_to([P, E]))
            load(b1_rows[:, :], L1_ffn_b1.rearrange("e (j p) -> (e j) p", p=P))
            load(b2[:, :], L1_ffn_b2)
            assert n[0] == N_WEIGHT_DMAS, n[0]

            def iteration(pair, p):
                if in_range(1, pair, p):
                    b, pr, par = image(1, pair, p)
                    if isinstance(pair, int) and 2 * pair + p == FIRST:
                        sp.dma_start(x_in[:, par, :], x_v[number(b)]).then_inc(x_loaded[par], 16)
                    if in_range(2, pair, p):
                        bn_, _, par2 = image(2, pair, p)
                        if positive(bn_ - 1):
                            sp.wait_ge(xn_ready, count(sp, bn_ - 1))
                            apart(sp, bn_ - 1)
                        sp.dma_start(x_in[:, par2, :], x_v[number(bn_)]).then_inc(x_loaded[par2], 16)
                    if positive(64 * (b - 1)):
                        sp.wait_ge(exp_done, count(sp, 64 * (b - 1)))
                        apart(sp, 64 * (b - 1))
                    sp.wait_ge(high_ready, count(sp, 4 * b + 4))
                    apart(sp, 4 * b + 4)
                    sp.wait_ge(mid_ready, count(sp, 4 * b + 4))
                    apart(sp, 4 * b + 4)
                    for h in range(NH):
                        src = slice(HD * h, HD * h + HD)
                        for r in range(2):
                            rows = slice(2 * HD * r, 2 * HD * r + 2 * HD)
                            sp.dma_start(qs1[rows, par, h, :],
                                         part[src, r, 0, :].unsqueeze(1).broadcast_to([HD, 2, N]))\
                              .then_inc(stacked1[par][h], 16)
                            sp.dma_start(ks1[rows, par, h, :], part[src, 0:2, 1, :])\
                              .then_inc(stacked1[par][h], 16)
                    sp.wait_ge(low_ready, count(sp, 4 * b + 4))
                    apart(sp, 4 * b + 4)
                    for h in range(NH):
                        src = slice(HD * h, HD * h + HD)
                        sp.dma_start(qs2[0:2 * HD, par, h, :], part[src, 0:3:2, 0, :])\
                          .then_inc(stacked2[par], 16)
                        for g, k in enumerate((2, 0)):
                            sp.dma_start(ks2[g:2 * HD:2, par, h, :], part[src, k, 1, :])\
                              .then_inc(stacked2[par], 16)
                if in_range(0, pair, p):
                    b, _, _ = image(0, pair, p)
                    if positive(b):
                        sp.wait_ge(xr_ready, count(sp, b))
                        apart(sp, b)
                    sp.dma_start(x_res[:, :], x_v[number(b)]).then_inc(xres_loaded, 16)
                if in_range(-2, pair, p):
                    b, _, _ = image(-2, pair, p)
                    sp.wait_ge(t2_ready, count(sp, 2 * b + 2))
                    apart(sp, 2 * b + 2)
                    sp.dma_start(t2_dram[number(b)], t2[:, :, :]).then_inc(t2_stored, 16)
                    sp.wait_ge(z2T_ready, count(sp, 2 * b + 2))
                    apart(sp, 2 * b + 2)
                    sp.dma_start(z2T_dram[number(b)], z2T[:, :]).then_inc(z2T_stored, 16)

            iterations(sp, iteration)

            sp.wait_ge(t2_stored, 16 * B)
            sp.wait_ge(z2T_stored, 16 * B)
            sp.wait_ge(probs_used, 8 * B)
            sp.dma_start(w1, L1_ffn_W1.rearrange("e c h -> c e h")).then_inc(experts_in, 16)
            sp.dma_start(w2, L1_ffn_W2.rearrange("e (j p) c -> p e j c", p=P)).then_inc(experts_in, 16)

            def load_tile(b, half, k):
                if positive((k - 1) * (1 + E)):
                    sp.wait_ge(acc_step, count(sp, (k - 1) * (1 + E)))
                sp.dma_start(z2T_t[half], z2T_dram[b, :, half * HALF:(half + 1) * HALF])\
                  .then_inc(tile_loaded[half], 16)
                sp.dma_start(t2_t[half], t2_dram[b, :, 4 * half:4 * half + 4, :])\
                  .then_inc(tile_loaded[half], 16)

            def store_tile(b, half, k):
                sp.wait_ge(outT_ready, count(sp, k + 1))
                sp.dma_start(out_v[b, :, half * HALF:(half + 1) * HALF], outT[half])\
                  .then_inc(out_stored[half], 16)

            load_tile(0, 0, 0)
            load_tile(0, 1, 1)
            with sp.Fori(1, B) as b:
                for half in range(2):
                    load_tile(b, half, 2 * b + half)
                    store_tile(b - 1, half, 2 * b - 2 + half)
            for half in range(2):
                store_tile(B - 1, half, 2 * B - 2 + half)
            for half in range(2):
                sp.wait_ge(out_stored[half], 16 * B)

        @block.gpsimd
        def _(pool):
            g = nc.gpsimd
            g.memset(ident[:, :], 0.0).then_inc(pool_const, 1)
            g.memset(ones[:, :], 1.0).then_inc(pool_const, 1)
            g.memset(headmask[:, :], 1.0 / N).then_inc(pool_const, 1)
            g.memset(power[:, 0, :], -0.5).then_inc(pool_const, 1)
            g.memset(power[:, 1, :], 0.5).then_inc(pool_const, 1)
            pool.wait_ge(pool_const, 5)
            g.affine_select(out=ident[:, :], in_=ident[:, :], compare_op=ALU.not_equal, fill=1.0,
                            base=0, pattern=[[-1, P]], channel_multiplier=1).then_inc(pool_const, 1)
            hm = headmask[:, :].rearrange("p (g d) -> p g d", d=G16)
            g.affine_select(out=hm, in_=hm, compare_op=ALU.is_ge, fill=0.0, base=0,
                            pattern=[[-G16, NG], [0, G16]], channel_multiplier=1).then_inc(pool_const, 1)
            pool.wait_ge(pool_const, 7)
            g.affine_select(out=hm, in_=hm, compare_op=ALU.is_ge, fill=0.0, base=G16 - 1,
                            pattern=[[G16, NG], [0, G16]], channel_multiplier=-1).then_inc(pool_const, 1)
            for e in range(E):
                g.memset(rank_w[:, e:e + 1], float(E - e)).then_inc(pool_const, 1)
            g.memset(u[:, :, C:C + 1], 1.0).then_inc(pool_const, 1)
            pool.wait_ge(pool_const, 9 + E)
            pool.wait_ge(weights_in, 16 * N_WEIGHT_DMAS)
            g.tensor_scalar(bn_tmp[:, 0:1], bn[:, 3:4], EPS_BN, 1.0, ALU.add, ALU.mult).then_inc(bn_step, 1)
            pool.wait_ge(bn_step, 1)
            g.tensor_tensor(bn_tmp[:, 1:2], bn_tmp[:, 0:1], power[:, 0, 0:1], ALU.pow).then_inc(bn_step, 1)

            def split_ml(b, c):
                half, which = c // 2, c % 2
                cols = slice(half * HALF, (half + 1) * HALF)
                pool.wait_ge(high_ready, count(pool, 4 * b + c + 1))
                apart(pool, 4 * b + c + 1)
                pool.wait_ge(raw_ready, count(pool, 4 * b + c + 1))
                apart(pool, 4 * b + c + 1)
                g.tensor_tensor(rest[:, c % 2, :], raw[:, c % 2, :], part[:, 0, which, cols], ALU.subtract)\
                 .then_inc(rest_ready, 1)
                pool.wait_ge(rest_ready, count(pool, 4 * b + c + 1))
                apart(pool, 4 * b + c + 1)
                g.tensor_scalar(part[:, 1, which, cols], rest[:, c % 2, :], 1.0, 0.0, ALU.mult, ALU.add)\
                 .then_inc(mid_ready, 1)
                pool.wait_ge(mid_ready, count(pool, 4 * b + c + 1))
                apart(pool, 4 * b + c + 1)
                g.tensor_tensor(part[:, 2, which, cols], rest[:, c % 2, :], part[:, 1, which, cols],
                                ALU.subtract).then_inc(low_ready, 1)

            def normalise(b, which, src, dst, done):
                step = rstd_step[which]
                pool.wait_ge(mv_ready[which], count(pool, b + 1))
                apart(pool, b + 1)
                r = rstd[:, which, :, :]
                g.tensor_scalar(r[:, 0, :], mv[:, which, :, 1], EPS_LN, 1.0, ALU.add, ALU.mult)\
                 .then_inc(step, 1)
                pool.wait_ge(step, count(pool, 4 * b + 1))
                apart(pool, 4 * b + 1)
                g.tensor_tensor(r[:, 1, :], r[:, 0, :], power[:, 0, 0:BLK], ALU.pow).then_inc(step, 1)
                pool.wait_ge(step, count(pool, 4 * b + 2))
                apart(pool, 4 * b + 2)
                g.tensor_tensor(r[:, 2, :], mv[:, which, :, 0], r[:, 1, :], ALU.mult).then_inc(step, 1)
                pool.wait_ge(step, count(pool, 4 * b + 3))
                apart(pool, 4 * b + 3)
                g.tensor_scalar(r[:, 0, :], r[:, 2, :], -1.0, 0.0, ALU.mult, ALU.add).then_inc(step, 1)
                pool.wait_ge(step, count(pool, 4 * b + 4))
                apart(pool, 4 * b + 4)
                for k in range(BLK):
                    g.tensor_scalar(dst[:, k, :], src[:, k, :], r[:, 1, k:k + 1], r[:, 0, k:k + 1],
                                    ALU.mult, ALU.add).then_inc(done, 1)

            def norm(b, half):
                a = avn[:, half * HALF:(half + 1) * HALF]
                pool.wait_ge(rden_ready, count(pool, 8 * b + 4 * half + 4))
                apart(pool, 8 * b + 4 * half + 4)
                g.tensor_tensor(a, a, rden[:, :], ALU.mult).then_inc(norm_step, 1)
                pool.wait_ge(norm_step, count(pool, 2 * b + half + 1))
                apart(pool, 2 * b + half + 1)
                g.tensor_scalar(a, a, bv[:, :], 1.0, ALU.add, ALU.mult).then_inc(norm_done, 1)

            def iteration(pair, p):
                if in_range(-1, pair, p):
                    b, _, _ = image(-1, pair, p)
                    pool.wait_ge(xres_loaded, count(pool, 16 * b + 16))
                    apart(pool, 16 * b + 16)
                    g.tensor_scalar(xr[:, :], x_res[:, :], bo[:, :], 1.0, ALU.add, ALU.mult)\
                     .then_inc(xr_ready, 1)
                if in_range(1, pair, p):
                    b, _, _ = image(1, pair, p)
                    _, prp, parp = image(0, pair, p)
                    if positive(prp + 1):
                        for h in range(NH):
                            pool.wait_ge(stacked1[parp][h], count(pool, 16 * STACK1_DMAS * (prp + 1)))
                            apart(pool, prp)
                        pool.wait_ge(stacked2[parp], count(pool, 16 * STACK2_DMAS * (prp + 1)))
                        apart(pool, prp)
                    for c in range(4):
                        split_ml(b, c)
                if in_range(-1, pair, p):
                    norm(image(-1, pair, p)[0], 1)
                if in_range(-2, pair, p):
                    b, _, _ = image(-2, pair, p)
                    normalise(b, 1, t2, z2, z2_ready)
                if in_range(-1, pair, p):
                    b, _, _ = image(-1, pair, p)
                    normalise(b, 0, t1, z, z_ready)
                    pool.wait_ge(gsum_ready, count(pool, 2 * b + 2))
                    apart(pool, 2 * b + 2)
                    g.tensor_tensor(grouped(d16[:, :, :]), grouped(z[:, :, :]), wide16(gsum[:, 1, :]),
                                    ALU.subtract).then_inc(d_ready, 1)
                    pool.wait_ge(ss_ready, count(pool, b + 1))
                    apart(pool, b + 1)
                    g.tensor_scalar(ss16[:, 1, :], ss16[:, 0, :], 1.0 / (G16 - 1), 0.0, ALU.mult, ALU.add)\
                     .then_inc(std_step, 1)
                    pool.wait_ge(std_step, count(pool, b + 1))
                    apart(pool, b + 1)
                    g.tensor_tensor(ss16[:, 2, :], ss16[:, 1, :], power[:, 1, :], ALU.pow)\
                     .then_inc(std_ready, 1)
                    pool.wait_ge(rs_step, count(pool, 2 * b + 2))
                    apart(pool, 2 * b + 2)
                    g.tensor_tensor(grouped(u[:, :, 0:C]), grouped(d16[:, :, :]), wide16(rs16[:, 1, :]),
                                    ALU.mult).then_inc(u_ready, 1)
                if in_range(0, pair, p):
                    norm(image(0, pair, p)[0], 0)

            iterations(pool, iteration)

        @block.scalar
        def _(act):
            a = nc.scalar
            act.wait_ge(weights_in, 16 * N_WEIGHT_DMAS)
            act.wait_ge(pool_const, 9 + E)

            def from_shared(name, pair, p):
                act.wait_ge(shared_ready[BANK[name]], count(act, turn(name, pair, p) + 1))
                return shared_ps[BANK[name]]

            def piece(name, pair, p):
                b, _, par = image(SHARED[name][1], pair, p)
                if name[:4] == "mrow":
                    s = int(name[4:])
                    half, h = (1, s) if s < 4 else (0, s - 4)
                    ps = from_shared(name, pair, p)
                    a.activation(qs2[64:66, par, h, half * HALF:(half + 1) * HALF], ps[64:66, :], ACT.Copy)\
                     .then_inc(mrow_ready, 1)
                elif name in ("q0", "k0", "q1", "k1"):
                    which, half = "qk".index(name[0]), int(name[1])
                    ps = from_shared(name, pair, p)
                    if name == "q0":
                        _, prp, parp = image(0, pair, p)
                        if positive(prp + 1):
                            for h in range(NH):
                                act.wait_ge(stacked1[parp][h], count(act, 16 * STACK1_DMAS * (prp + 1)))
                                apart(act, prp)
                            act.wait_ge(stacked2[parp], count(act, 16 * STACK2_DMAS * (prp + 1)))
                    a.activation(part[:, 0, which, half * HALF:(half + 1) * HALF], ps[:, :], ACT.Identity,
                                 bias=bqk[:, which:which + 1]).then_inc(high_ready, 1)
                    c = 2 * half + which
                    if positive(4 * b + c - 1):
                        act.wait_ge(rest_ready, count(act, 4 * b + c - 1))
                    a.activation(raw[:, c % 2, :], ps[:, :], ACT.Identity,
                                 bias=bqk[:, which:which + 1]).then_inc(raw_ready, 1)
                elif name in ("v0", "v1"):
                    half = int(name[1])
                    ps = from_shared(name, pair, p)
                    a.activation(v_sb[:, par, 4 * half:4 * half + 4, :].rearrange("p k c -> p (k c)"), ps[:, :],
                                 ACT.Copy).then_inc(v_ready, 1)
                elif name[:4] == "proj":
                    half = int(name[4])
                    ps = from_shared(name, pair, p)
                    if positive(2 * b):
                        act.wait_ge(t2_ready, count(act, 2 * b))
                    a.activation(t1[:, 4 * half:4 * half + 4, :].rearrange("p k c -> p (k c)"), ps[:, :],
                                 ACT.Copy).then_inc(t1_ready, 1)
                elif name[:2] == "zT":
                    half = int(name[2])
                    ps = from_shared(name, pair, p)
                    a.activation(zT[:, half * HALF:(half + 1) * HALF], ps[:, :], ACT.Copy)\
                     .then_inc(zT_ready, 1)
                elif name[:3] == "z2T":
                    half = int(name[3])
                    ps = from_shared(name, pair, p)
                    if positive(16 * b):
                        act.wait_ge(z2T_stored, count(act, 16 * b))
                    a.activation(z2T[:, half * HALF:(half + 1) * HALF], ps[:, :], ACT.Copy)\
                     .then_inc(z2T_ready, 1)

            def out_of_psum(b, half):
                act.wait_ge(probs_used, count(act, 8 * b + 4 * half + 4))
                if half == 0 and positive(2 * b):
                    act.wait_ge(t1_ready, count(act, 2 * b))
                a.activation(avn[:, half * HALF:(half + 1) * HALF], av_ps[:, :], ACT.Copy).then_inc(av_out, 1)
                if positive(2 * b + half):
                    act.wait_ge(norm_step, count(act, 2 * b + half))
                a.activation(rden[:, :], den_ps[:, :], ACT.Copy).then_inc(av_out, 1)

            def iteration(pair, p):
                for q in range(QUARTERS):
                    s, j = divmod(q, 4)
                    if q == 4 and in_range(-1, pair, p):
                        out_of_psum(image(-1, pair, p)[0], 1)
                    if q == 20 and in_range(0, pair, p):
                        out_of_psum(image(0, pair, p)[0], 0)
                    if in_range(0, pair, p):
                        b, _, par = image(0, pair, p)
                        for t in (2 * j, 2 * j + 1):
                            tile = 64 * b + 8 * s + t
                            if t == 0:
                                if positive(8 * b + s - 1):
                                    act.wait_ge(probs_used, count(act, 8 * b + s - 1))
                            act.wait_ge(st_ready, count(act, tile + 1))
                            a.activation(probs[:, 8 * (s % 2) + t, :], st_ps[t % 2][:, :], ACT.Exp,
                                         scale=float(C) ** -0.5).then_inc(exp_done, 1)
                    for name in at_quarter(q, pair, p):
                        piece(name, pair, p)
                    if q == 19 and in_range(-1, pair, p):
                        b, _, _ = image(-1, pair, p)
                        act.wait_ge(d_ready, count(act, b + 1))
                        a.activation(sq16[:, :, :], d16[:, :, :], ACT.Square).then_inc(sq_ready, 1)
                    if q == 18 and in_range(-2, pair, p):
                        b, _, _ = image(-2, pair, p)
                        act.wait_ge(lsub_ready, count(act, b + 1))
                        a.activation(lg[:, 1, :, :], lg[:, 0, :, :], ACT.Exp).then_inc(gexp_ready, 1)

            iterations(act, iteration)

            def hidden(k, e, half):
                n = E * k + e
                for j in range(HC):
                    act.wait_ge(hid_ps, count(act, HC * n + j + 1))
                    if j == 0:
                        if positive(n - 1):
                            act.wait_ge(y_ps, count(act, n - 1))
                    a.activation(hid[e % 2][j], bank[2 * (e % 2) + j][:, :], ACT.Gelu,
                                 bias=b1[:, e, j:j + 1]).then_inc(hid_ready, 1)

            def write_out(b, half):
                k = 2 * b + half
                act.wait_ge(outT_ps, count(act, k + 1))
                if positive(16 * b):
                    act.wait_ge(out_stored[half], count(act, 16 * b))
                a.activation(outT[half], bank[7][:, :], ACT.Copy).then_inc(outT_ready, 1)

            def tile(b, half, first):
                k = 2 * b + half
                act.wait_ge(cwT_ps, count(act, k + 1))
                a.activation(cwT[half], bank[6][0:E, :], ACT.Copy).then_inc(cwT_ready, 1)
                for e in range(E):
                    hidden(k, e, half)
                    if e == 2 and not first:
                        write_out(b - 1 if half == 0 else b, 1 - half)

            tile(0, 0, True)
            tile(0, 1, False)
            with act.Fori(1, B) as b:
                for half in range(2):
                    tile(b, half, False)
            write_out(B - 1, 1)

        @block.vector
        def _(dve):
            v = nc.vector
            dve.wait_ge(weights_in, 16 * N_WEIGHT_DMAS)
            dve.wait_ge(pool_const, 9 + E)
            v.tensor_copy(identb[:, :], ident[:, :]).then_inc(dve_const, 1)
            v.tensor_scalar(kb_n[:, :], kcol[:, 1:2], float(N), None, ALU.mult).then_inc(dve_const, 1)
            for par in range(2):
                v.memset(ks2[64:66, par, :, :], 1.0).then_inc(ones_rows, 1)
            dve.wait_ge(bn_step, 2)
            v.tensor_tensor(bn_scale[:, :], bn_tmp[:, 1:2], bn[:, 0:1], ALU.mult).then_inc(bn_step, 1)
            dve.wait_ge(bn_step, 3)
            v.tensor_tensor(bn_tmp[:, 0:1], bn_scale[:, :], bn[:, 2:3], ALU.mult).then_inc(bn_step, 1)
            dve.wait_ge(bn_step, 4)
            v.tensor_tensor(bn_shift[:, :], bn[:, 1:2], bn_tmp[:, 0:1], ALU.subtract).then_inc(bn_step, 1)
            for j in range(3):
                dve.wait_ge(wT_ps, count(dve, j + 1))
                for blk in range(4):
                    h, kind = divmod(4 * j + blk, 3)
                    v.tensor_copy(wqkvT[:, kind, h, :], bank[j][:, HD * blk:HD * blk + HD]).then_inc(wT_ready, 1)
            dve.wait_ge(wT_ps, 4)
            v.tensor_copy(woT[:, :], bank[3][:, 0:P]).then_inc(wT_ready, 1)
            dve.wait_ge(wT_ps, 5)
            v.tensor_copy(b1[:, :, :].rearrange("p e j -> p (e j)"), bank[4][:, 0:E * HC]).then_inc(wT_ready, 1)
            dve.wait_ge(bn_step, 5)
            dve.wait_ge(dve_const, 2)

            def from_shared(name, pair, p):
                dve.wait_ge(shared_ready[BANK[name]], count(dve, turn(name, pair, p) + 1))
                return shared_ps[BANK[name]]

            def reciprocals(b, half, i):
                dve.wait_ge(av_out, count(dve, 4 * b + 2 * half + 2))
                r = rden[:, i * P:(i + 1) * P]
                v.reciprocal(r, r).then_inc(rden_ready, 1)

            def layer_stats(b, which, src, half):
                blocks = range(4 * half, 4 * half + 4)
                for k in blocks:
                    v.bn_stats(stats[:, which, k, :], src[:, k, :]).then_inc(stats_done[which], 1)
                if half == 1:
                    dve.wait_ge(stats_done[which], count(dve, BLK * b + BLK))
                    apart(dve, BLK * b + BLK)
                    for k in range(BLK):
                        m = v.bn_aggr(mv[:, which, k, :], stats[:, which, k, :])
                    m.then_inc(mv_ready[which], 1)

            def piece(name, pair, p):
                b, _, par = image(SHARED[name][1], pair, p)
                if name == "gram":
                    ps = from_shared(name, pair, p)
                    v.tensor_copy(usum[:, :], ps[:, C:C + 1]).then_inc(kv_step, 1)
                    dve.wait_ge(kv_step, count(dve, 6 * b + 1))
                    v.tensor_scalar(udiag[:, :], ident[:, :], usum[:, :], None, ALU.mult).then_inc(udiag_ready, 1)
                    v.tensor_scalar(kvw[:, 0, :], ps[:, 0:C], kcol[:, 0:1], None, ALU.mult).then_inc(kv_step, 1)
                    v.scalar_tensor_tensor(kcc[:, :], usum[:, :], kcol[:, 0:1], kb_n[:, :], ALU.mult, ALU.add)\
                     .then_inc(kv_step, 1)
                elif name[:3] == "t2_":
                    half = int(name[3])
                    ps = from_shared(name, pair, p)
                    if positive(16 * b):
                        dve.wait_ge(t2_stored, count(dve, 16 * b))
                    if positive(BLK * b):
                        dve.wait_ge(z2_ready, count(dve, BLK * b))
                    v.tensor_tensor(t2[:, 4 * half:4 * half + 4, :], ps[:, :].rearrange("p (k c) -> p k c", c=C),
                                    t1[:, 4 * half:4 * half + 4, :], ALU.add).then_inc(t2_ready, 1)
                    dve.wait_ge(t2_ready, count(dve, 2 * b + half + 1))
                    layer_stats(b, 1, t2, half)
                elif name == "logits":
                    ps = from_shared(name, pair, p)
                    pl = ps[:, 0:BLK * E].rearrange("p (k e) -> p k e", e=E)
                    v.tensor_tensor(lg[:, 2, :, :], pl, gate_b[:, :].unsqueeze(1).broadcast_to([P, BLK, E]),
                                    ALU.add).then_inc(lmax_step, 1)
                    dve.wait_ge(lmax_step, count(dve, 2 * b + 1))
                    v.tensor_reduce(lred[:, 0, :], lg[:, 2, :, :], AX.X, ALU.max).then_inc(lmax_step, 1)
                    dve.wait_ge(lmax_step, count(dve, 2 * b + 2))
                    v.tensor_tensor(lg[:, 0, :, :], lg[:, 2, :, :],
                                    lred[:, 0, :].unsqueeze(2).broadcast_to([P, BLK, E]), ALU.subtract)\
                     .then_inc(lsub_ready, 1)

            def kv_product(b, which, pair=None, p=None):
                if which == 0:
                    ps = from_shared("usum", pair, p)
                    dve.wait_ge(kv_step, count(dve, 6 * b + 3))
                    v.scalar_tensor_tensor(kvw[:, 1, :], ps[:, 0:C], kcol[:, 1:2], kvw[:, 0, :],
                                           ALU.mult, ALU.add).then_inc(kv_step, 1)
                elif which == 1:
                    dve.wait_ge(kv_step, count(dve, 6 * b + 4))
                    v.tensor_tensor(kvw[:, 2, :], kvw[:, 1, :], vrow[:, 0, :], ALU.mult).then_inc(kv_step, 1)
                elif which == 2:
                    dve.wait_ge(kv_step, count(dve, 6 * b + 5))
                    v.scalar_tensor_tensor(kvw[:, 3, :], vrow[:, 1, :], kcc[:, :], kvw[:, 2, :],
                                           ALU.mult, ALU.add).then_inc(kv_step, 1)
                else:
                    dve.wait_ge(kv_step, count(dve, 6 * b + 6))
                    v.tensor_tensor(kvw[:, 4, :], kvw[:, 3, :], headmask[:, :], ALU.mult).then_inc(bd_ready, 1)
                    dve.wait_ge(bd_ready, count(dve, 2 * b + 1))
                    v.tensor_tensor(bd[:, :], kvw[:, 4, :], ident[:, :], ALU.add).then_inc(bd_ready, 1)

            def gate(b, steps):
                def wide(r):
                    return lred[:, r, :].unsqueeze(2).broadcast_to([P, BLK, E])

                rank = rank_w[:, :].unsqueeze(1).broadcast_to([P, BLK, E])
                ex, pr, pr2 = lg[:, 1, :, :], lg[:, 3, :, :], lg[:, 4, :, :]
                w, sel1, sel2, eq = lg[:, 5, :, :], lg[:, 6, :, :], lg[:, 7, :, :], lg[:, 8, :, :]
                for step in steps:
                    if step == 0:
                        dve.wait_ge(gexp_ready, count(dve, b + 1))
                    else:
                        dve.wait_ge(gate_step, count(dve, 16 * b + step))
                    if step == 0:
                        ins = v.tensor_reduce(lred[:, 1, :], ex, AX.X, ALU.add)
                    elif step == 1:
                        ins = v.reciprocal(lred[:, 2, :], lred[:, 1, :])
                    elif step == 2:
                        ins = v.tensor_tensor(pr, ex, wide(2), ALU.mult)
                    elif step == 3:
                        ins = v.tensor_reduce(lred[:, 3, :], pr, AX.X, ALU.max)
                    elif step == 4:
                        ins = v.tensor_tensor(eq, pr, wide(3), ALU.is_equal)
                    elif step == 5:
                        ins = v.tensor_tensor(w, eq, rank, ALU.mult)
                    elif step == 6:
                        ins = v.tensor_reduce(lred[:, 4, :], w, AX.X, ALU.max)
                    elif step == 7:
                        ins = v.tensor_tensor(sel1, w, wide(4), ALU.is_equal)
                    elif step == 8:
                        ins = v.scalar_tensor_tensor(pr2, sel1, -2.0, pr, ALU.mult, ALU.add)
                    elif step == 9:
                        ins = v.tensor_reduce(lred[:, 5, :], pr2, AX.X, ALU.max)
                    elif step == 10:
                        ins = v.tensor_tensor(eq, pr2, wide(5), ALU.is_equal)
                    elif step == 11:
                        ins = v.tensor_tensor(w, eq, rank, ALU.mult)
                    elif step == 12:
                        ins = v.tensor_reduce(lred[:, 6, :], w, AX.X, ALU.max)
                    elif step == 13:
                        ins = v.tensor_tensor(sel2, w, wide(6), ALU.is_equal)
                    elif step == 14:
                        ins = v.tensor_tensor(eq, sel1, sel2, ALU.add)
                    else:
                        ins = v.tensor_tensor(cw[:, number(b), :, :], pr, eq, ALU.mult)
                    ins.then_inc(gate_step, 1)

            def iteration(pair, p):
                for q in range(QUARTERS):
                    s, j = divmod(q, 4)
                    lag, half, h = row_target(s + 1)
                    if in_range(lag, pair, p):
                        b, _, _ = image(lag, pair, p)
                        for kh in range(2):
                            n = 64 * b + 32 * half + 8 * h + 2 * j + kh
                            dve.wait_ge(row_ready, count(dve, n + 1))
                            v.tensor_reduce(rowmax[:, h % 2, kh, j:j + 1], row_ps[kh][:, :], AX.X, ALU.max)\
                             .then_inc(row_used, 1)
                    lag, half, h = row_target(s)
                    if j < 2 and in_range(lag, pair, p):
                        b, _, _ = image(lag, pair, p)
                        g = 8 * b + 4 * half + h
                        if j == 0:
                            dve.wait_ge(row_used, count(dve, 8 * g + 8))
                            v.tensor_tensor(rowm[:, h % 2, :], rowmax[:, h % 2, 0, :], rowmax[:, h % 2, 1, :],
                                            ALU.max).then_inc(max_step, 1)
                            dve.wait_ge(max_step, count(dve, 2 * g + 1))
                            if positive(g - 1):
                                dve.wait_ge(mrow_ready, count(dve, g - 1))
                            v.tensor_scalar(negm[:, h % 2, :, 0], rowm[:, h % 2, :], -1.0, None, ALU.mult)\
                             .then_inc(max_step, 1)
                        else:
                            dve.wait_ge(max_step, count(dve, 2 * g + 2))
                            v.scalar_tensor_tensor(negm[:, h % 2, :, 1], rowm[:, h % 2, :], -1.0,
                                                   negm[:, h % 2, :, 0], ALU.mult, ALU.subtract)\
                             .then_inc(negm_ready, 1)
                    if q == 0 and in_range(1, pair, p):
                        b, pr, par = image(1, pair, p)
                        dve.wait_ge(x_loaded[par], count(dve, 16 * (pr + 1)))
                        v.tensor_scalar(xn[:, :], x_in[:, par, :], bn_scale[:, :], bn_shift[:, :],
                                        ALU.mult, ALU.add).then_inc(xn_ready, 1)
                    if q < 3 and in_range(-2, pair, p):
                        kv_product(image(-2, pair, p)[0], q + 1)
                    if q in (5, 6, 7, 8) and in_range(-1, pair, p):
                        reciprocals(image(-1, pair, p)[0], 1, q - 5)
                    if q in (21, 22, 23, 24) and in_range(0, pair, p):
                        reciprocals(image(0, pair, p)[0], 0, q - 21)
                    for name in at_quarter(q, pair, p):
                        piece(name, pair, p)
                    if in_range(-1, pair, p):
                        b, _, _ = image(-1, pair, p)
                        if q in (10, 13):
                            half1 = (q - 10) // 3
                            dve.wait_ge(t1_ready, count(dve, 2 * b + half1 + 1))
                            layer_stats(b, 0, t1, half1)
                        if q == 17:
                            dve.wait_ge(z_ready, count(dve, BLK * b + BLK))
                            v.tensor_reduce(gsum[:, 0, :], z[:, :, :].rearrange("p k (g d) -> p (k g) d", d=G16),
                                            AX.X, ALU.add).then_inc(gsum_ready, 1)
                            dve.wait_ge(gsum_ready, count(dve, 2 * b + 1))
                            v.tensor_scalar(gsum[:, 1, :], gsum[:, 0, :], 1.0 / G16, None, ALU.mult)\
                             .then_inc(gsum_ready, 1)
                        if q == 20:
                            dve.wait_ge(sq_ready, count(dve, b + 1))
                            v.tensor_reduce(ss16[:, 0, :], sq16[:, :, :].rearrange("p k (g d) -> p (k g) d", d=G16),
                                            AX.X, ALU.add).then_inc(ss_ready, 1)
                        if q == 27:
                            dve.wait_ge(std_ready, count(dve, b + 1))
                            v.tensor_scalar(rs16[:, 0, :], ss16[:, 2, :], EPS_HEAD, None, ALU.add)\
                             .then_inc(rs_step, 1)
                            dve.wait_ge(rs_step, count(dve, 2 * b + 1))
                            v.reciprocal(rs16[:, 1, :], rs16[:, 0, :]).then_inc(rs_step, 1)
                        if q == 31:
                            kv_product(b, 0, pair, p)
                    if in_range(-2, pair, p):
                        b, _, _ = image(-2, pair, p)
                        if 20 <= q < 28:
                            gate(b, (2 * (q - 20), 2 * (q - 20) + 1))

            iterations(dve, iteration)

            def tile(b, half, last_tile=False):
                k = 2 * b + half
                dve.wait_ge(cw_copied, count(dve, k + 1))
                dve.wait_ge(tile_loaded[half], count(dve, 32 * b + 32))
                dve.wait_ge(bias_ps, count(dve, k + 1))
                if positive(k - 1):
                    dve.wait_ge(outT_ps, count(dve, k - 1))
                v.tensor_tensor(acc[half], bank[6][:, :].rearrange("p (k c) -> p k c", c=C), t2_t[half],
                                ALU.add).then_inc(acc_step, 1)
                dve.wait_ge(acc_step, count(dve, (1 + E) * k + 1))
                if half == 0:
                    v.tensor_copy(cw_t[1], cw[:, b, 4:8, :]).then_inc(cw_copied, 1)
                elif not last_tile:
                    v.tensor_copy(cw_t[0], cw[:, b + 1, 0:4, :]).then_inc(cw_copied, 1)
                for e in range(E):
                    n = E * k + e
                    dve.wait_ge(y_ps, count(dve, n + 1))
                    dve.wait_ge(acc_step, count(dve, (1 + E) * k + e + 1))
                    for i in range(4):
                        last = v.scalar_tensor_tensor(
                            acc[half][:, i, :], bank[4 + e % 2][:, i * C:(i + 1) * C],
                            cw_t[half][:, i, e:e + 1], acc[half][:, i, :], ALU.mult, ALU.add)
                    last.then_inc(acc_step, 1)

            dve.wait_ge(gate_step, 16 * B)
            dve.wait_ge(probs_used, 8 * B)
            v.tensor_copy(cw_t[0], cw[:, 0, 0:4, :]).then_inc(cw_copied, 1)
            tile(0, 0)
            tile(0, 1)
            with dve.Fori(1, B - 1) as b:
                tile(b, 0)
                tile(b, 1)
            tile(B - 1, 0)
            tile(B - 1, 1, last_tile=True)

        @block.tensor
        def _(pe):
            t_ = nc.tensor
            pe.wait_ge(weights_in, 16 * N_WEIGHT_DMAS)
            pe.wait_ge(pool_const, 9 + E)
            for j in range(3):
                t_.transpose(bank[j][:, 0:P], wload[:, j, :], ident[:, :]).then_inc(wT_ps, 1)
            t_.transpose(bank[3][:, 0:P], woload[:, :], ident[:, :]).then_inc(wT_ps, 1)
            t_.transpose(bank[4][:, 0:E * HC], b1_rows[:, :], ident[0:E * HC, 0:E * HC]).then_inc(wT_ps, 1)
            pe.wait_ge(wT_ready, 14)
            pe.wait_ge(ones_rows, 2)
            pe.wait_ge(dve_const, 2)

            def piece(name, pair, p):
                b, _, par = image(SHARED[name][1], pair, p)
                bk = BANK[name]
                ps = shared_ps[bk]
                if name in ("q0", "k0", "q1", "k1"):
                    which, half = "qk".index(name[0]), int(name[1])
                    pe.wait_ge(xn_ready, count(pe, b + 1))
                    free_shared(name, pair, p)
                    last = t_.matmul(ps[:, :], wqkvT[:, which, :, :].rearrange("p n d -> p (n d)"),
                                     xn[:, half * HALF:(half + 1) * HALF], start=True, stop=True)
                elif name in ("v0", "v1"):
                    free_shared(name, pair, p)
                    half = int(name[1])
                    for i in range(4):
                        k = 4 * half + i
                        last = t_.matmul(ps[:, i * C:(i + 1) * C], xn[:, k * P:(k + 1) * P],
                                         wqkvT[:, 2, :, :].rearrange("p n d -> p (n d)"), start=True, stop=True)
                elif name[:4] == "mrow":
                    s = int(name[4:])
                    half, h = (1, s) if s < 4 else (0, s - 4)
                    pe.wait_ge(negm_ready, count(pe, 8 * b + 4 * half + h + 1))
                    free_shared(name, pair, p)
                    for i in range(4):
                        last = t_.matmul(ps[64:66, i * P:(i + 1) * P], negm[:, h % 2, i, :], identb[:, :],
                                         start=True, stop=True)
                elif name[:4] == "proj":
                    half = int(name[4])
                    pe.wait_ge(xr_ready, count(pe, b + 1))
                    pe.wait_ge(norm_done, count(pe, 2 * b + half + 1))
                    free_shared(name, pair, p)
                    for i in range(4):
                        k = 4 * half + i
                        o = ps[:, i * C:(i + 1) * C]
                        t_.matmul(o, avn[:, k * P:(k + 1) * P], woT[:, :], start=True, stop=False)
                        last = t_.matmul(o, xr[:, k * P:(k + 1) * P], ident[:, :], start=False, stop=True)
                elif name[:2] == "zT":
                    half = int(name[2])
                    pe.wait_ge(z_ready, count(pe, BLK * b + 4 * half + 4))
                    free_shared(name, pair, p)
                    for i in range(4):
                        last = t_.transpose(ps[:, i * P:(i + 1) * P], z[:, 4 * half + i, :], ident[:, :])
                elif name == "gram":
                    pe.wait_ge(u_ready, count(pe, b + 1))
                    free_shared(name, pair, p)
                    for k in range(BLK):
                        last = t_.matmul(ps[:, 0:C + 1], u[:, k, 0:C], u[:, k, :],
                                         start=(k == 0), stop=(k == BLK - 1))
                elif name == "usum":
                    pe.wait_ge(udiag_ready, count(pe, b + 1))
                    free_shared(name, pair, p)
                    last = t_.matmul(ps[:, 0:C], ones[:, :], udiag[:, :], start=True, stop=True)
                elif name[:3] == "t2_":
                    half = int(name[3])
                    pe.wait_ge(zT_ready, count(pe, 2 * b + half + 1))
                    pe.wait_ge(bd_ready, count(pe, 2 * b + 2))
                    free_shared(name, pair, p)
                    for i in range(4):
                        k = 4 * half + i
                        last = t_.matmul(ps[:, i * C:(i + 1) * C], zT[:, k * P:(k + 1) * P], bd[:, :],
                                         start=True, stop=True)
                elif name[:3] == "z2T":
                    half = int(name[3])
                    pe.wait_ge(z2_ready, count(pe, BLK * b + 4 * half + 4))
                    free_shared(name, pair, p)
                    for i in range(4):
                        last = t_.transpose(ps[:, i * P:(i + 1) * P], z2[:, 4 * half + i, :], ident[:, :])
                elif name == "logits":
                    pe.wait_ge(z2T_ready, count(pe, 2 * b + 2))
                    free_shared(name, pair, p)
                    for k in range(BLK):
                        last = t_.matmul(ps[:, k * E:(k + 1) * E], z2T[:, k * P:(k + 1) * P], gate_w[:, :],
                                         start=True, stop=True)
                last.then_inc(shared_ready[bk], 1)

            def free_shared(name, pair, p):
                prev_name, prev_pair, prev_p = previous(name, pair, p)
                if prev_name is None:
                    return
                b = image(SHARED[prev_name][1], prev_pair, prev_p)[0]
                if prev_name in ("q0", "k0", "q1", "k1"):
                    pe.wait_ge(raw_ready, count(pe, 4 * b + 2 * int(prev_name[1]) + "qk".index(prev_name[0]) + 1))
                elif prev_name in ("v0", "v1"):
                    pe.wait_ge(v_ready, count(pe, 2 * b + int(prev_name[1]) + 1))
                elif prev_name[:4] == "mrow":
                    s = int(prev_name[4:])
                    half, h = (1, s) if s < 4 else (0, s - 4)
                    pe.wait_ge(mrow_ready, count(pe, 8 * b + 4 * half + h + 1))
                elif prev_name[:4] == "proj":
                    pe.wait_ge(t1_ready, count(pe, 2 * b + int(prev_name[4]) + 1))
                elif prev_name[:2] == "zT":
                    pe.wait_ge(zT_ready, count(pe, 2 * b + int(prev_name[2]) + 1))
                elif prev_name == "gram":
                    pe.wait_ge(kv_step, count(pe, 6 * b + 3))
                elif prev_name == "usum":
                    pe.wait_ge(kv_step, count(pe, 6 * b + 4))
                elif prev_name[:3] == "t2_":
                    pe.wait_ge(t2_ready, count(pe, 2 * b + int(prev_name[3]) + 1))
                elif prev_name[:3] == "z2T":
                    pe.wait_ge(z2T_ready, count(pe, 2 * b + int(prev_name[3]) + 1))
                elif prev_name == "logits":
                    pe.wait_ge(lmax_step, count(pe, 2 * b + 1))

            def previous(name, pair, p):
                mine = [n for n in ORDER if BANK[n] == BANK[name]]
                i = mine.index(name)
                while True:
                    i -= 1
                    if i < 0:
                        i = len(mine) - 1
                        pair, p = (pair, 0) if p == 1 else (pair - 1, 1)
                        if isinstance(pair, int) and 2 * pair + p < FIRST:
                            return None, None, None
                    if in_range(SHARED[mine[i]][1], pair, p):
                        return mine[i], pair, p

            def iteration(pair, p):
                for q in range(QUARTERS):
                    s, j = divmod(q, 4)
                    if in_range(0, pair, p):
                        b, pr, par = image(0, pair, p)
                        half = s // 4
                        for t in (2 * j, 2 * j + 1):
                            kb, h = 2 * (s % 4) + t // 4, t % 4
                            keys = slice(kb * P, (kb + 1) * P)
                            queries = slice(half * HALF, (half + 1) * HALF)
                            tile = 64 * b + 8 * s + t
                            if s % 4 == 0 and t < 4:
                                pe.wait_ge(mrow_ready, count(pe, 8 * b + 4 * half + h + 1))
                            if s == 0 and t == 0:
                                pe.wait_ge(stacked2[par], count(pe, 16 * STACK2_DMAS * (pr + 1)))
                            if positive(tile - 1):
                                pe.wait_ge(exp_done, count(pe, tile - 1))
                            t_.matmul(st_ps[t % 2][:, :], ks1[:, par, h, keys], qs1[:, par, h, queries],
                                      start=True, stop=False)
                            t_.matmul(st_ps[t % 2][:, :], ks2[0:66, par, h, keys], qs2[0:66, par, h, queries],
                                      start=False, stop=True).then_inc(st_ready, 1)
                    lag, half, h = row_target(s + 1)
                    if in_range(lag, pair, p):
                        b, pr, par = image(lag, pair, p)
                        if half == 0 and j == 0:
                            pe.wait_ge(stacked1[par][h], count(pe, 16 * STACK1_DMAS * (pr + 1)))
                        for kh in range(2):
                            n = 64 * b + 32 * half + 8 * h + 2 * j + kh
                            if positive(n - 1):
                                pe.wait_ge(row_used, count(pe, n - 1))
                            qb = 4 * half + j
                            t_.matmul(row_ps[kh][:, :], qs1[:, par, h, qb * P:(qb + 1) * P],
                                      ks1[:, par, h, kh * HALF:(kh + 1) * HALF], start=True, stop=True)\
                              .then_inc(row_ready, 1)
                    lag, sv = (0, s - 1) if s > 0 else (-1, STEPS - 1)
                    if in_range(lag, pair, p) and j > 0:
                        b, _, par = image(lag, pair, p)
                        half, slot = sv // 4, 8 * (sv % 2)
                        first, last_kb = 2 * (sv % 4), 2 * (sv % 4) + 1
                        if j < 3:
                            kb = first + j - 1
                            pe.wait_ge(exp_done, count(pe, 64 * b + 8 * sv + 4 * j))
                            if kb == 0:
                                if positive(4 * b + 2 * half):
                                    pe.wait_ge(av_out, count(pe, 4 * b + 2 * half))
                                pe.wait_ge(v_ready, count(pe, 2 * b + 2))
                            for h in range(NH):
                                rows = slice(HD * h, HD * h + HD)
                                t_.matmul(av_ps[rows, :], v_sb[:, par, kb, rows], probs[:, slot + 4 * (j - 1) + h, :],
                                          start=(kb == 0), stop=(kb == NKB - 1))
                        else:
                            for kb in (first, last_kb):
                                for h in range(NH):
                                    rows = slice(HD * h, HD * h + HD)
                                    mm = t_.matmul(den_ps[rows, :], ones[:, 0:HD],
                                                   probs[:, slot + 4 * (kb - first) + h, :],
                                                   start=(kb == 0), stop=(kb == NKB - 1))
                            mm.then_inc(probs_used, 1)
                    for name in at_quarter(q, pair, p):
                        piece(name, pair, p)

            iterations(pe, iteration)

            pe.wait_ge(experts_in, 32)
            pe.wait_ge(gate_step, 16 * B)

            def prepare(b, half):
                k = 2 * b + half
                pe.wait_ge(cw_copied, count(pe, k + 1))
                if positive((1 + E) * (k - 1) + 1):
                    pe.wait_ge(acc_step, count(pe, (1 + E) * (k - 1) + 1))
                for i in range(4):
                    last = t_.transpose(bank[6][0:E, i * P:(i + 1) * P], cw_t[half][:, i, :], ident[:, :])
                last.then_inc(cwT_ps, 1)

            def bias_term(b, half):
                k = 2 * b + half
                pe.wait_ge(cwT_ready, count(pe, k + 1))
                for i in range(4):
                    last = t_.matmul(bank[6][:, i * C:(i + 1) * C], cwT[half][:, i * P:(i + 1) * P], b2[:, :],
                                     start=True, stop=True)
                last.then_inc(bias_ps, 1)

            def up(b, half, e):
                k = 2 * b + half
                n = E * k + e
                if e == 0:
                    pe.wait_ge(tile_loaded[half], count(pe, 32 * b + 32))
                if positive(HC * (n - 1)):
                    pe.wait_ge(hid_ready, count(pe, HC * (n - 1)))
                for j in range(HC):
                    t_.matmul(bank[2 * (e % 2) + j][:, :], w1[:, e, j * P:(j + 1) * P], z2T_t[half],
                              start=True, stop=True).then_inc(hid_ps, 1)

            def down(b, half, e):
                k = 2 * b + half
                n = E * k + e
                pe.wait_ge(hid_ready, count(pe, HC * (n + 1)))
                if e >= 2:
                    if positive((1 + E) * k + e):
                        pe.wait_ge(acc_step, count(pe, (1 + E) * k + e))
                else:
                    if positive((1 + E) * (k - 1) + E + e):
                        pe.wait_ge(acc_step, count(pe, (1 + E) * (k - 1) + E + e))
                for i in range(4):
                    for j in range(HC):
                        last = t_.matmul(bank[4 + e % 2][:, i * C:(i + 1) * C],
                                         hid[e % 2][j][:, i * P:(i + 1) * P], w2[:, e, j, :],
                                         start=(j == 0), stop=(j == HC - 1))
                last.then_inc(y_ps, 1)

            def turn_out(b, half):
                k = 2 * b + half
                pe.wait_ge(acc_step, count(pe, (1 + E) * (k + 1)))
                if positive(k):
                    pe.wait_ge(outT_ready, count(pe, k))
                for i in range(4):
                    last = t_.transpose(bank[7][:, i * P:(i + 1) * P], acc[half][:, i, :], ident[:, :])
                last.then_inc(outT_ps, 1)

            def tile(b, half, first):
                prepare(b, half)
                up(b, half, 0)
                bias_term(b, half)
                for e in range(1, E):
                    up(b, half, e)
                    down(b, half, e - 1)
                    if e == 2 and not first:
                        turn_out(b - 1 if half == 0 else b, 1 - half)
                down(b, half, E - 1)

            tile(0, 0, True)
            tile(0, 1, False)
            with pe.Fori(1, B) as b:
                tile(b, 0, False)
                tile(b, 1, False)
            turn_out(B - 1, 1)


_INS = ['x', 'L0_conv_gamma', 'L0_conv_beta', 'L0_conv_run_mean', 'L0_conv_run_var', 'L0_conv_qkv_w',
        'L0_conv_qkv_b', 'L0_conv_out_w', 'L0_conv_out_b', 'L1_attn_kln_weight', 'L1_attn_kln_bias',
        'L1_attn_vln_weight', 'L1_attn_vln_bias', 'L1_ffn_gate_w', 'L1_ffn_gate_b', 'L1_ffn_W1',
        'L1_ffn_b1', 'L1_ffn_W2', 'L1_ffn_b2']
_OUTS = [((16, 128, 32, 32), 'float32')]


def kernel(**inputs):
    import numpy as _np
    import concourse.bacc as _bacc
    from concourse import mybir as _mybir
    from concourse.bass_utils import run_bass_kernel_spmd as _run

    nc = _bacc.Bacc("TRN2", target_bir_lowering=False, num_devices=1)
    arrays, args = {}, []
    for name in _INS:
        a = _np.ascontiguousarray(inputs[name])
        arrays[f"in_{name}_dram"] = a
        args.append(nc.dram_tensor(f"in_{name}_dram", a.shape, _mybir.dt.from_np(a.dtype), kind="ExternalInput").ap())
    for i, (shape, dtype) in enumerate(_OUTS):
        dt = _mybir.dt.from_np(_np.dtype(dtype))
        args.append(nc.dram_tensor(f"out_{i}_dram", shape, dt, kind="ExternalOutput").ap())
    conv_attention_hybrid_kernel(nc, *args)
    r = _run(nc, [arrays], core_ids=[0])
    got = tuple(r.results[0][f"out_{i}_dram"] for i in range(len(_OUTS)))
    return got[0]
```

```python
from contextlib import ExitStack

import concourse.bass as bass
from concourse import mybir

P = 128
EPS_BN = 1e-5
EPS_LN = 1e-5
EPS_HEAD = 1e-5

ALU = mybir.AluOpType
ACT = mybir.ActivationFunctionType
AX = mybir.AxisListType
F32 = mybir.dt.float32
BF16 = mybir.dt.bfloat16
I32 = mybir.dt.int32
U32 = mybir.dt.uint32


class Linear:

    def __init__(self, pair, multiples, scratch, scale=1, plus=0):
        self.pair, self.multiples, self.scratch, self.scale, self.plus = pair, multiples, scratch, scale, plus

    def __add__(self, n):
        return Linear(self.pair, self.multiples, self.scratch, self.scale, self.plus + n)

    def __sub__(self, n):
        return self + -n

    def __mul__(self, n):
        return Linear(self.pair, self.multiples, self.scratch, self.scale * n, self.plus * n)

    __radd__, __rmul__ = __add__, __mul__

    def value(self):
        return self.pair * self.scale + self.plus

    def count(self, eng):
        if self.plus == 0:
            return self.multiples[self.scale]
        eng.reg_add(self.scratch, self.multiples[self.scale], self.plus)
        return self.scratch


def number(n):
    return n.value() if isinstance(n, Linear) else n


def conv_attention_hybrid_kernel(
    nc: bass.Bass,
    x: bass.AP,
    L0_conv_gamma: bass.AP,
    L0_conv_beta: bass.AP,
    L0_conv_run_mean: bass.AP,
    L0_conv_run_var: bass.AP,
    L0_conv_qkv_w: bass.AP,
    L0_conv_qkv_b: bass.AP,
    L0_conv_out_w: bass.AP,
    L0_conv_out_b: bass.AP,
    L1_attn_kln_weight: bass.AP,
    L1_attn_kln_bias: bass.AP,
    L1_attn_vln_weight: bass.AP,
    L1_attn_vln_bias: bass.AP,
    L1_ffn_gate_w: bass.AP,
    L1_ffn_gate_b: bass.AP,
    L1_ffn_W1: bass.AP,
    L1_ffn_b1: bass.AP,
    L1_ffn_W2: bass.AP,
    L1_ffn_b2: bass.AP,
    out: bass.AP,
):
    B, C, IMH, IMW = x.shape
    N = IMH * IMW
    BLK = N // P
    NH = 4
    HD = C // NH
    HALF = N // 2
    NKB = N // P
    G16 = L1_attn_kln_weight.shape[2]
    NG = C // G16
    E, _, HID = L1_ffn_W1.shape
    HC = HID // P

    TOKENS = B * N
    TILE = 2 * P
    CAP = TOKENS + TILE
    UNROLL = 8
    DEPTH = 4
    TILES = -(-(2 * TOKENS // TILE + E - 1) // UNROLL) * UNROLL
    ROUNDS = TILES // UNROLL
    SPARE = TILES - 2 * TOKENS // TILE
    MOST = TOKENS // TILE
    WAT, DAT, ROW = C, C + E, C + 2 * E
    assert TOKENS % TILE == 0 and UNROLL == 2 * DEPTH and ROUNDS > B // 2
    assert C == P and HD == 32 and N == 1024 and B % 2 == 0

    STEPS, QUARTERS = 8, 32
    FIRST, LAST = -1, B + 2
    LOOP_FROM, LOOP_PAIRS = 4, (B - 6) // 2

    x_v = x.rearrange("b c h w -> b c (h w)")
    out_v = out.rearrange("b c h w -> b c (h w)")

    SCALES = (2, 4, 8, 12, 16, 26, 28, 32, 64, 128, 192, 256)

    SHARED = {}
    for s in range(STEPS):
        SHARED[f"mrow{s}"] = (4 * s + 2, 0 if s < 4 else 1)
    SHARED.update({
        "q0": (1, 1), "k0": (2, 1), "q1": (4, 1), "k1": (5, 1), "v0": (6, 1), "v1": (7, 1),
        "proj0": (8, -1), "proj1": (13, -1), "zT0": (19, -1), "zT1": (20, -1),
        "gram": (30, -1), "usum": (31, -1),
        "t2_0": (3, -2), "t2_1": (4, -2), "z2T0": (9, -2), "z2T1": (10, -2), "logits": (12, -2),
        "rank": (2, -3), "total": (10, -3),
    })
    ORDER = sorted(SHARED, key=lambda n: SHARED[n][0])
    BANK = {n: i % 2 for i, n in enumerate(ORDER)}

    def in_range(lag, pair, p):
        return not isinstance(pair, int) or 0 <= 2 * pair + p + lag < B

    def image(lag, pair, p):
        return 2 * (pair + (p + lag) // 2) + (p + lag) % 2, pair + (p + lag) // 2, (p + lag) % 2

    def turn(name, pair, p):
        bank = BANK[name]
        mine = [n for n in ORDER if BANK[n] == bank]
        if isinstance(pair, int):
            it = 2 * pair + p
            done = sum(in_range(SHARED[n][1], 0, k) for k in range(FIRST, it) for n in mine)
            return done + sum(in_range(SHARED[n][1], 0, it) for n in mine[:mine.index(name)])
        before = sum(in_range(SHARED[n][1], 0, k) for k in range(FIRST, LOOP_FROM) for n in mine)
        return 2 * len(mine) * pair + (before + len(mine) * (p - LOOP_FROM) + mine.index(name))

    def at_quarter(q, pair, p):
        return [n for n in ORDER if SHARED[n][0] == q and in_range(SHARED[n][1], pair, p)]

    def iterations(eng, body):
        for it in range(FIRST, LOOP_FROM):
            body(it // 2, it % 2)
        multiples = {m: eng.alloc_register(f"pair_times_{m}") for m in SCALES}
        scratch = eng.alloc_register("wait_value")
        with eng.Fori(LOOP_FROM // 2, LOOP_FROM // 2 + LOOP_PAIRS) as register:
            for scale, multiple in multiples.items():
                eng.reg_mul(multiple, register, scale)
            pair = Linear(register, multiples, scratch)
            body(pair, 0)
            body(pair, 1)
        for it in range(LOOP_FROM + 2 * LOOP_PAIRS, LAST + 1):
            body(it // 2, it % 2)

    def positive(value):
        return not isinstance(value, int) or value > 0

    def count(eng, value):
        return value.count(eng) if isinstance(value, Linear) else value

    def apart(eng, value):
        if isinstance(value, Linear):
            eng.sem_inc(waits_passed, 1)

    def grouped(t):
        return t.rearrange("p k (g d) -> p k g d", d=G16)

    def wide16(r):
        return r.rearrange("p (k g) -> p k g", g=NG).unsqueeze(3).broadcast_to([P, BLK, NG, G16])

    def row_target(r):
        return (0, 1, r) if r < 4 else (1, 0, r - 4) if r < 8 else (1, 1, 0)

    def steps_before(s, n):
        return (0, s - n) if s >= n else (-1, STEPS + s - n)

    ctx = ExitStack()
    with ctx:
        def sb(name, shape, dt=F32):
            return ctx.enter_context(nc.sbuf_tensor(name, shape, dt))

        def sem(name):
            return ctx.enter_context(nc.semaphore(name))

        POOL_HEADS = 2

        t2_dram = nc.dram_tensor("t2_scratch", [B, P, BLK, C], F32, kind="Internal").ap()
        sorted_dram = nc.dram_tensor("sorted_scratch", [E * CAP + SPARE * TILE, ROW], F32, kind="Internal").ap()
        y_dram = nc.dram_tensor("y_scratch", [2 * TOKENS, C], F32, kind="Internal").ap()

        ident = sb("ident", [P, P])
        identb = sb("identb", [P, P], BF16)
        ones = sb("ones", [P, P])
        headmask = sb("headmask", [P, P])
        wqkvT = sb("wqkvT", [P, 3, NH, HD])
        woT = sb("woT", [P, C])
        bn = sb("bn", [P, 4])
        bn_scale = sb("bn_scale", [P, 1])
        bn_shift = sb("bn_shift", [P, 1])
        bn_tmp = sb("bn_tmp", [P, 2])
        bqk = sb("bqk", [P, 2])
        bv = sb("bv", [P, 1])
        bo = sb("bo", [P, 1])
        kcol = sb("kcol", [P, 2])
        kb_n = sb("kb_n", [P, 1])
        vrow = sb("vrow", [P, 2, C])
        gate_w = sb("gate_w_sb", [P, E])
        gate_b = sb("gate_b_sb", [P, E])
        b1 = sb("b1_sb", [P, E, HC])
        tri = sb("tri", [P, P])
        emask = sb("emask", [P, E, E])
        counting = sb("counting", [P, TILES + MOST + BLK], I32)
        tile_no = sb("tile_no", [P, TILES])
        filled = sb("filled", [P, MOST])
        token = sb("token", [P, BLK])
        region = sb("region", [P, E])
        base = sb("base", [P, E])
        pad_row = sb("pad_row", [P, ROW])
        tile_expert = sb("tile_expert", [P, TILES], I32)
        tile_row = sb("tile_row", [P, TILES], I32)
        region_end = sb("region_end", [P, E], I32)
        rank_w = sb("rank_w", [P, E])
        power = sb("power", [P, 2, BLK * NG])

        x_in = sb("x_in", [P, N])
        xn = sb("xn", [P, N])
        part = sb("part", [P, 3, 2, N], BF16)
        raw = sb("raw", [P, 2, HALF])
        rest = sb("rest", [P, 2, HALF])
        stacks = sb("stacks", [P, 4, 2, NH, N], BF16)
        qs1, ks1, qs2, ks2 = (stacks[:, i, :, :, :] for i in range(4))
        v_sb = sb("v_sb", [P, 2, BLK, C])
        rowmax = sb("rowmax", [P, 2, 2, 4])
        rowm = sb("rowm", [P, 2, 4])
        negm = sb("negm", [P, 2, 4, 2], BF16)
        probs = sb("probs", [P, 16, HALF])
        pairs = sb("pairs", [P, NH, HALF])
        rden = sb("rden", [P, HALF])
        avn = sb("avn", [P, N])

        x_res = sb("x_res", [P, N])
        t1 = sb("t1", [P, BLK, C])
        stats = sb("stats", [P, 2, BLK, 6])
        mv = sb("mv", [P, 2, BLK, 2])
        rstd = sb("rstd", [P, 2, 3, BLK])
        z = sb("z", [P, BLK, C])
        gsum = sb("gsum", [P, 2, BLK * NG])
        d16 = sb("d16", [P, BLK, C])
        ss16 = sb("ss16", [P, 3, BLK * NG])
        rs16 = sb("rs16", [P, 2, BLK * NG])
        u = sb("u", [P, BLK, C + 1])
        usum = sb("usum_sb", [P, 1])
        udiag = sb("udiag", [P, P])
        kvw = sb("kvw", [P, 5, P])
        kcc = sb("kcc", [P, 1])
        bd = sb("bd", [P, P])
        zT = sb("zT", [P, N])
        t2 = sb("t2", [P, BLK, C])
        rows = sb("rows", [P, 2, BLK, ROW])
        z2T = sb("z2T", [P, N])
        sq16 = z2T[:, :].rearrange("p (k c) -> p k c", c=C)
        lg = sb("lg", [P, 9, BLK, E])
        lred = sb("lred", [P, 7, BLK])
        before = sb("before", [P, BLK + 1, E])
        slot = sb("slot", [P, 3, BLK, E])
        slot_of = sb("slot_of", [P, 2, BLK])
        slot_idx = sb("slot_idx", [P, 2, 2 * BLK], U32)

        wload = probs[:, 0:3, 0:C]
        woload = probs[:, 3, 0:C]
        b1_rows = probs[0:E * HC, 4, 0:P]

        ring = probs[:, :, :].rearrange("p s n -> p (s n)")
        w1 = ring[:, 0:E * HID].rearrange("p (e i) -> p e i", e=E)
        w2 = ring[:, E * HID:2 * E * HID].rearrange("p (e j c) -> p e j c", e=E, j=HC)
        b2 = ring[:, 2 * E * HID:2 * E * HID + E * C].rearrange("p (e c) -> p e c", e=E)
        tables = ring[:, 2 * E * HID + E * C:]
        hid = [ring[:, (14 + i) * 512:(15 + i) * 512].rearrange("p (j n) -> p j n", j=HC) for i in (0, 1)]
        z_rows = [pairs[:, i, 0:2 * ROW].rearrange("p (k c) -> p k c", k=2)
                  for i in range(DEPTH)]
        y_out = [(xn, avn)[i // 4][:, i % 4 * TILE:(i % 4 + 1) * TILE].rearrange("p (k c) -> p k c", k=2)
                 for i in range(UNROLL)]
        w1_tile = [raw[:, i, 0:HID] for i in (0, 1)]
        y_sum = [raw[:, i, HID:2 * HID].rearrange("p (k c) -> p k c", k=2) for i in (0, 1)]
        zT_tile = [rest[:, i, 0:TILE] for i in (0, 1)]
        b2_tile = [rest[:, i // 2, TILE + i % 2 * C:TILE + (i % 2 + 1) * C] for i in range(4)]
        b1_tile = sb("b1_tile", [P, 2, HC])
        w_tile = sb("w_tile", [P, UNROLL, 2])
        d_tile = sb("d_tile", [P, UNROLL, 2], U32)
        t2_all = stacks[:, :, :, :, :].rearrange("p i a h n -> p (i a h n)").bitcast(F32)\
            .rearrange("p (b k c) -> p b k c", b=B, k=BLK)
        y_in = [[ring[:, (2 * i + c) * 512:(2 * i + c + 1) * 512].rearrange("p (k c) -> p k c", c=C)
                 for c in (0, 1)] for i in range(4)]
        outT = [ring[:, (8 + i) * 512:(9 + i) * 512] for i in range(4)]

        bank = [ctx.enter_context(nc.psum_tensor(f"bank{i}", [P, 512], F32)) for i in range(8)]
        row_ps, st_ps, av_ps, den_ps, shared_ps = bank[0:2], bank[2:4], bank[4], bank[5], bank[6:8]

        waits_passed = sem("waits_passed")
        weights_in = sem("weights_in")
        pool_const = sem("pool_const")
        dve_const = sem("dve_const")
        bn_step = sem("bn_step")
        wT_ps = sem("wT_ps")
        wT_ready = sem("wT_ready")
        ones_rows = sem("ones_rows")
        x_loaded = sem("x_loaded")
        xn_ready = sem("xn_ready")
        shared_ready = [sem(f"shared_ready{i}") for i in (0, 1)]
        high_ready = sem("high_ready")
        raw_ready = sem("raw_ready")
        rest_ready = sem("rest_ready")
        mid_ready = sem("mid_ready")
        low_ready = sem("low_ready")
        stacked1 = [[sem(f"stacked1_{i}_{h}") for h in range(NH)] for i in (0, 1)]
        stacked2 = [sem(f"stacked2_{i}") for i in (0, 1)]
        v_ready = sem("v_ready")
        row_ready = sem("row_ready")
        row_used = sem("row_used")
        max_step = sem("max_step")
        negm_ready = sem("negm_ready")
        mrow_ready = sem("mrow_ready")
        st_ready = sem("st_ready")
        exp_done = sem("exp_done")
        pairs_pool = sem("pairs_pool")
        pairs_dve = sem("pairs_dve")
        probs_used = sem("probs_used")
        den_done = sem("den_done")
        av_out = sem("av_out")
        rden_ready = sem("rden_ready")
        norm_step = sem("norm_step")
        norm_done = sem("norm_done")
        xres_loaded = sem("xres_loaded")
        xr_ready = sem("xr_ready")
        t1_ready = sem("t1_ready")
        stats_done = [sem(f"stats_done{i}") for i in (0, 1)]
        mv_ready = [sem(f"mv_ready{i}") for i in (0, 1)]
        rstd_step = [sem(f"rstd_step{i}") for i in (0, 1)]
        z_ready = sem("z_ready")
        z2_ready = sem("z2_ready")
        zT_ready = sem("zT_ready")
        gsum_ready = sem("gsum_ready")
        d_ready = sem("d_ready")
        sq_ready = sem("sq_ready")
        ss_ready = sem("ss_ready")
        std_step = sem("std_step")
        std_ready = sem("std_ready")
        rs_step = sem("rs_step")
        u_ready = sem("u_ready")
        kv_step = sem("kv_step")
        udiag_ready = sem("udiag_ready")
        bd_ready = sem("bd_ready")
        t2_ready = sem("t2_ready")
        z2T_ready = sem("z2T_ready")
        lmax_step = sem("lmax_step")
        lsub_ready = sem("lsub_ready")
        gexp_ready = sem("gexp_ready")
        gate_step = sem("gate_step")
        t2_stored = sem("t2_stored")
        prefix_step = sem("prefix_step")
        slot_step = sem("slot_step")
        idx_ready = sem("idx_ready")
        token_ready = sem("token_ready")
        base_ready = sem("base_ready")
        scattered = [sem(f"scattered{i}") for i in (0, 1)]
        table_step = sem("table_step")
        pads_in = sem("pads_in")
        experts_in = sem("experts_in")
        t2_loaded = sem("t2_loaded")
        z_loaded = [sem(f"z_loaded{i}") for i in range(DEPTH)]
        zT_ps = sem("zT_ps")
        zT_tile_ready = sem("zT_tile_ready")
        w1_tile_ready = sem("w1_tile_ready")
        b1_tile_ready = sem("b1_tile_ready")
        b2_tile_ready = sem("b2_tile_ready")
        w_tile_ready = sem("w_tile_ready")
        d_tile_ready = sem("d_tile_ready")
        hid_ps = sem("hid_ps")
        hid_ready = sem("hid_ready")
        y_ps = sem("y_ps")
        y_sum_ready = sem("y_sum_ready")
        y_out_ready = sem("y_out_ready")
        y_scattered = [sem(f"y_scattered{i}") for i in range(UNROLL)]
        y_in_ready = [sem(f"y_in_ready{i}") for i in range(4)]
        sum_step = sem("sum_step")
        outT_ps = sem("outT_ps")
        outT_ready = sem("outT_ready")
        out_stored = [sem(f"out_stored{i}") for i in range(4)]

        N_WEIGHT_DMAS = 3 + 1 + 4 + 2 * NH + 1 + NH + 2 + 2 + 2 + 1
        POOL_CONSTS = 9 + E + 9 + E
        TABLE_STEPS = 15
        STACK1_DMAS = 4
        STACK2_DMAS = 3 * NH
        block = ctx.enter_context(nc.Block())

        @block.sync
        def _(sp):
            n = [0]

            def load(dst, src):
                sp.dma_start(dst, src).then_inc(weights_in, 16)
                n[0] += 1

            sp.dma_start(x_in[:, :], x_v[0]).then_inc(x_loaded, 16)
            for j in range(3):
                load(wload[:, j, :], L0_conv_qkv_w[j * P:(j + 1) * P, :])
            load(woload, L0_conv_out_w)
            for j, v in enumerate((L0_conv_gamma, L0_conv_beta, L0_conv_run_mean, L0_conv_run_var)):
                load(bn[:, j:j + 1], v.rearrange("(c a) -> c a", a=1))
            qkv_b = L0_conv_qkv_b.rearrange("(n j d) -> n j d", n=NH, j=3)
            for h in range(NH):
                for j in range(2):
                    load(bqk[HD * h:HD * h + HD, j:j + 1], qkv_b[h, j, :].rearrange("(d a) -> d a", a=1))
            load(bo[:, :], L0_conv_out_b.rearrange("(c a) -> c a", a=1))
            for h in range(NH):
                load(bv[HD * h:HD * h + HD, :], qkv_b[h, 2, :].rearrange("(d a) -> d a", a=1))
            for j, v in enumerate((L1_attn_kln_weight, L1_attn_kln_bias)):
                load(kcol[:, j:j + 1], v.rearrange("h a d -> (h d) a"))
            for j, v in enumerate((L1_attn_vln_weight, L1_attn_vln_bias)):
                load(vrow[:, j, :], v.rearrange("h a d -> a (h d)").broadcast_to([P, C]))
            load(gate_w[:, :], L1_ffn_gate_w)
            load(gate_b[:, :], L1_ffn_gate_b.rearrange("(a e) -> a e", a=1).broadcast_to([P, E]))
            load(b1_rows, L1_ffn_b1.rearrange("e (j p) -> (e j) p", p=P))
            assert n[0] == N_WEIGHT_DMAS, n[0]

            def iteration(pair, p):
                if in_range(1, pair, p):
                    b, pr, par = image(1, pair, p)
                    if in_range(2, pair, p):
                        sp.wait_ge(xn_ready, count(sp, b + 1))
                        apart(sp, b)
                        sp.dma_start(x_in[:, :], x_v[number(b + 1)]).then_inc(x_loaded, 16)
                    if positive(64 * (b - 1)):
                        sp.wait_ge(exp_done, count(sp, 64 * (b - 1)))
                        apart(sp, 64 * (b - 1))
                    sp.wait_ge(high_ready, count(sp, 4 * b + 4))
                    apart(sp, 4 * b + 4)
                    sp.wait_ge(mid_ready, count(sp, 4 * b + 4))
                    apart(sp, 4 * b + 4)
                    for h in range(NH):
                        src = slice(HD * h, HD * h + HD)
                        for r in range(2):
                            rows = slice(2 * HD * r, 2 * HD * r + 2 * HD)
                            sp.dma_start(qs1[rows, par, h, :],
                                         part[src, r, 0, :].unsqueeze(1).broadcast_to([HD, 2, N]))\
                              .then_inc(stacked1[par][h], 16)
                            sp.dma_start(ks1[rows, par, h, :], part[src, 0:2, 1, :])\
                              .then_inc(stacked1[par][h], 16)
                    sp.wait_ge(low_ready, count(sp, 4 * b + 4))
                    apart(sp, 4 * b + 4)
                    for h in range(NH):
                        src = slice(HD * h, HD * h + HD)
                        sp.dma_start(qs2[0:2 * HD, par, h, :], part[src, 0:3:2, 0, :])\
                          .then_inc(stacked2[par], 16)
                        for g, k in enumerate((2, 0)):
                            sp.dma_start(ks2[g:2 * HD:2, par, h, :], part[src, k, 1, :])\
                              .then_inc(stacked2[par], 16)
                if in_range(0, pair, p):
                    b, _, _ = image(0, pair, p)
                    if positive(2 * b):
                        sp.wait_ge(t1_ready, count(sp, 2 * b))
                        apart(sp, b)
                    sp.dma_start(x_res[:, :], x_v[number(b)]).then_inc(xres_loaded, 16)
                if in_range(-2, pair, p):
                    b, _, _ = image(-2, pair, p)
                    sp.wait_ge(t2_ready, count(sp, 2 * b + 2))
                    apart(sp, 2 * b + 2)
                    sp.dma_start(t2_dram[number(b)], t2[:, :, :]).then_inc(t2_stored, 16)

            iterations(sp, iteration)

            sp.wait_ge(pool_const, POOL_CONSTS)
            pad_rows = pad_row[:, :].unsqueeze(1).broadcast_to([P, TILE // P, ROW])

            def tile_rows(first):
                return sorted_dram[bass.ds(first, TILE), :].rearrange("(k p) c -> p k c", p=P)

            for i in range(SPARE):
                sp.dma_start(tile_rows(E * CAP + i * TILE), pad_rows).then_inc(pads_in, 16)
            sp.wait_ge(den_done, 8 * B)
            sp.dma_start(w1, L1_ffn_W1.rearrange("e c h -> c e h")).then_inc(experts_in, 16)
            sp.dma_start(w2, L1_ffn_W2.rearrange("e (j p) c -> p e j c", p=P)).then_inc(experts_in, 16)
            sp.dma_start(b2, L1_ffn_b2.rearrange("(a e) c -> a e c", a=1).broadcast_to([P, E, C]))\
              .then_inc(experts_in, 16)
            sp.wait_ge(table_step, TABLE_STEPS)
            for e in range(E):
                end = sp.value_load(region_end[0:1, e:e + 1], min_val=0, max_val=E * CAP)
                sp.dma_start(tile_rows(end), pad_rows).then_inc(pads_in, 16)
            sp.wait_ge(pads_in, 16 * (E + SPARE))
            for i in range(2):
                sp.wait_ge(scattered[i], 32 * BLK * (B // 2))
            sp.wait_ge(xn_ready, B)

            def load_rows(r, i):
                t = r * UNROLL + i
                if positive(t - DEPTH + 1):
                    sp.wait_ge(zT_ps, t - DEPTH + 1)
                    sp.wait_ge(d_tile_ready, t - DEPTH + 1)
                first = sp.value_load(tile_row[0:1, bass.ds(t, 1)], min_val=0, max_val=E * CAP + (SPARE - 1) * TILE)
                sp.dma_start(z_rows[i % DEPTH], tile_rows(first)).then_inc(z_loaded[i % DEPTH], 16)

            for i in range(UNROLL):
                load_rows(0, i)
            sp.wait_ge(exp_done, 64 * B)
            sp.wait_ge(t2_stored, 16 * B)
            with sp.Fori(1, B // 2 + 1) as r:
                for i in range(UNROLL):
                    load_rows(r, i)
                sp.dma_start(t2_all[:, bass.ds(2 * r - 2, 2), :, :],
                             t2_dram[bass.ds(2 * r - 2, 2)].rearrange("b p k c -> p b k c"))\
                  .then_inc(t2_loaded, 16)
            with sp.Fori(B // 2 + 1, ROUNDS) as r:
                for i in range(UNROLL):
                    load_rows(r, i)
            for i in range(UNROLL):
                sp.wait_ge(y_scattered[i], 32 * ROUNDS)
            STEPS2 = B // 2

            def load_y(r, i):
                half = i % 2
                if positive(4 * r):
                    sp.wait_ge(outT_ps, 4 * r + i - 3)
                for c in (0, 1):
                    first = (2 * r + i // 2) * N + (c * TOKENS + half * HALF)
                    sp.dma_start(y_in[i][c], y_dram[bass.ds(first, HALF), :].rearrange("(k p) c -> p k c", p=P))\
                      .then_inc(y_in_ready[i], 16)

            def store(r, i):
                half = i % 2
                sp.wait_ge(outT_ready, 4 * r + i + 1)
                sp.dma_start(out_v[2 * r + i // 2, :, half * HALF:(half + 1) * HALF], outT[i])\
                  .then_inc(out_stored[i], 16)

            for i in range(4):
                load_y(0, i)
            with sp.Fori(1, STEPS2) as r:
                for i in range(4):
                    load_y(r, i)
                    store(r - 1, i)
            for i in range(4):
                store(STEPS2 - 1, i)
            for i in range(4):
                sp.wait_ge(out_stored[i], 16 * STEPS2)

        @block.gpsimd
        def _(pool):
            g = nc.gpsimd
            g.memset(ident[:, :], 0.0).then_inc(pool_const, 1)
            g.memset(ones[:, :], 1.0).then_inc(pool_const, 1)
            g.memset(headmask[:, :], 1.0 / N).then_inc(pool_const, 1)
            g.memset(power[:, 0, :], -0.5).then_inc(pool_const, 1)
            g.memset(power[:, 1, :], 0.5).then_inc(pool_const, 1)
            pool.wait_ge(pool_const, 5)
            g.affine_select(out=ident[:, :], in_=ident[:, :], compare_op=ALU.not_equal, fill=1.0,
                            base=0, pattern=[[-1, P]], channel_multiplier=1).then_inc(pool_const, 1)
            hm = headmask[:, :].rearrange("p (g d) -> p g d", d=G16)
            g.affine_select(out=hm, in_=hm, compare_op=ALU.is_ge, fill=0.0, base=0,
                            pattern=[[-G16, NG], [0, G16]], channel_multiplier=1).then_inc(pool_const, 1)
            pool.wait_ge(pool_const, 7)
            g.affine_select(out=hm, in_=hm, compare_op=ALU.is_ge, fill=0.0, base=G16 - 1,
                            pattern=[[G16, NG], [0, G16]], channel_multiplier=-1).then_inc(pool_const, 1)
            for e in range(E):
                g.memset(rank_w[:, e:e + 1], float(E - e)).then_inc(pool_const, 1)
            g.memset(u[:, :, C:C + 1], 1.0).then_inc(pool_const, 1)
            g.memset(tri[:, :], 1.0).then_inc(pool_const, 1)
            g.memset(emask[:, :, :], 1.0).then_inc(pool_const, 1)
            g.memset(pad_row[:, 0:DAT], 0.0).then_inc(pool_const, 1)
            g.memset(pad_row[:, DAT:ROW], float(4 * TOKENS)).then_inc(pool_const, 1)
            g.iota(counting[:, 0:TILES], pattern=[[1, TILES]], base=0, channel_multiplier=0).then_inc(pool_const, 1)
            g.iota(counting[:, TILES:TILES + MOST], pattern=[[TILE, MOST]], base=1, channel_multiplier=0)\
             .then_inc(pool_const, 1)
            g.iota(counting[:, TILES + MOST:], pattern=[[P, BLK]], base=0, channel_multiplier=1)\
             .then_inc(pool_const, 1)
            for e in range(E):
                g.memset(region[:, e:e + 1], float(e * CAP)).then_inc(pool_const, 1)
            pool.wait_ge(pool_const, POOL_CONSTS - 2)
            g.affine_select(out=tri[:, :], in_=tri[:, :], compare_op=ALU.is_ge, fill=0.0, base=-1,
                            pattern=[[1, P]], channel_multiplier=-1).then_inc(pool_const, 1)
            g.affine_select(out=emask[:, :, :], in_=emask[:, :, :], compare_op=ALU.is_ge, fill=0.0, base=0,
                            pattern=[[1, E], [-1, E]], channel_multiplier=0).then_inc(pool_const, 1)
            pool.wait_ge(pool_const, POOL_CONSTS)
            pool.wait_ge(weights_in, 16 * N_WEIGHT_DMAS)
            g.tensor_scalar(bn_tmp[:, 0:1], bn[:, 3:4], EPS_BN, 1.0, ALU.add, ALU.mult).then_inc(bn_step, 1)
            pool.wait_ge(bn_step, 1)
            g.tensor_tensor(bn_tmp[:, 1:2], bn_tmp[:, 0:1], power[:, 0, 0:1], ALU.pow).then_inc(bn_step, 1)

            def split_ml(b, c):
                half, which = c // 2, c % 2
                cols = slice(half * HALF, (half + 1) * HALF)
                pool.wait_ge(high_ready, count(pool, 4 * b + c + 1))
                apart(pool, 4 * b + c + 1)
                pool.wait_ge(raw_ready, count(pool, 4 * b + c + 1))
                apart(pool, 4 * b + c + 1)
                g.tensor_tensor(rest[:, c % 2, :], raw[:, c % 2, :], part[:, 0, which, cols], ALU.subtract)\
                 .then_inc(rest_ready, 1)
                pool.wait_ge(rest_ready, count(pool, 4 * b + c + 1))
                apart(pool, 4 * b + c + 1)
                g.tensor_scalar(part[:, 1, which, cols], rest[:, c % 2, :], 1.0, 0.0, ALU.mult, ALU.add)\
                 .then_inc(mid_ready, 1)
                pool.wait_ge(mid_ready, count(pool, 4 * b + c + 1))
                apart(pool, 4 * b + c + 1)
                g.tensor_tensor(part[:, 2, which, cols], rest[:, c % 2, :], part[:, 1, which, cols],
                                ALU.subtract).then_inc(low_ready, 1)

            def deviations(b, which):
                step = rstd_step[which]
                pool.wait_ge(mv_ready[which], count(pool, b + 1))
                apart(pool, b + 1)
                r = rstd[:, which, :, :]
                g.tensor_scalar(r[:, 0, :], mv[:, which, :, 1], EPS_LN, 1.0, ALU.add, ALU.mult)\
                 .then_inc(step, 1)
                pool.wait_ge(step, count(pool, 4 * b + 1))
                apart(pool, 4 * b + 1)
                g.tensor_tensor(r[:, 1, :], r[:, 0, :], power[:, 0, 0:BLK], ALU.pow).then_inc(step, 1)
                pool.wait_ge(step, count(pool, 4 * b + 2))
                apart(pool, 4 * b + 2)
                g.tensor_tensor(r[:, 2, :], mv[:, which, :, 0], r[:, 1, :], ALU.mult).then_inc(step, 1)
                pool.wait_ge(step, count(pool, 4 * b + 3))
                apart(pool, 4 * b + 3)
                g.tensor_scalar(r[:, 0, :], r[:, 2, :], -1.0, 0.0, ALU.mult, ALU.add).then_inc(step, 1)
                pool.wait_ge(step, count(pool, 4 * b + 4))
                apart(pool, 4 * b + 4)

            def scatter(b, par, which):
                pool.wait_ge(idx_ready, count(pool, b + 1))
                apart(pool, b)
                pool.wait_ge(slot_step, count(pool, 6 * b + 6))
                apart(pool, b)
                for n in which:
                    g.indirect_dma_start(
                        out=sorted_dram, out_offset=bass.IndirectOffsetOnAxis(ap=slot_idx[:, par, n:n + 1], axis=0),
                        in_=rows[:, par, n % BLK, :], in_offset=None, bounds_check=E * CAP - 1, oob_is_err=False)\
                     .then_inc(scattered[par], 16)

            def norm(b, half):
                a = avn[:, half * HALF:(half + 1) * HALF]
                pool.wait_ge(rden_ready, count(pool, 8 * b + 4 * half + 4))
                apart(pool, 8 * b + 4 * half + 4)
                g.tensor_tensor(a, a, rden[:, :], ALU.mult).then_inc(norm_step, 1)
                pool.wait_ge(norm_step, count(pool, 2 * b + half + 1))
                apart(pool, 2 * b + half + 1)
                g.tensor_scalar(a, a, bv[:, :], 1.0, ALU.add, ALU.mult).then_inc(norm_done, 1)

            SCATTERS = (9, 10, 11, 12, 14, 15, 16, 19)

            def add_pairs(b, s):
                pool.wait_ge(exp_done, count(pool, 64 * b + 8 * s + 8))
                apart(pool, b)
                if positive(8 * b + s):
                    pool.wait_ge(den_done, count(pool, 8 * b + s))
                    apart(pool, b)
                first = 8 * (s % 2)
                g.tensor_tensor(pairs[:, 0:POOL_HEADS, :], probs[:, first:first + POOL_HEADS, :],
                                probs[:, first + 4:first + 4 + POOL_HEADS, :], ALU.add).then_inc(pairs_pool, 1)

            def iteration(pair, p):
                for q in range(QUARTERS):
                    s, j = divmod(q, 4)
                    lag, before_s = steps_before(s, 1)
                    if j == 1 and in_range(lag, pair, p):
                        add_pairs(image(lag, pair, p)[0], before_s)
                    if in_range(1, pair, p):
                        b, _, _ = image(1, pair, p)
                        if q == 2:
                            _, prp, parp = image(0, pair, p)
                            if positive(prp + 1):
                                for h in range(NH):
                                    pool.wait_ge(stacked1[parp][h], count(pool, 16 * STACK1_DMAS * (prp + 1)))
                                    apart(pool, prp)
                                pool.wait_ge(stacked2[parp], count(pool, 16 * STACK2_DMAS * (prp + 1)))
                                apart(pool, prp)
                        if q in (2, 3, 4, 6):
                            split_ml(b, (2, 3, 4, 6).index(q))
                    if in_range(-2, pair, p):
                        b, _, _ = image(-2, pair, p)
                        if q == 4:
                            deviations(b, 1)
                    if q in SCATTERS and in_range(-3, pair, p):
                        b, _, par = image(-3, pair, p)
                        i = SCATTERS.index(q)
                        scatter(b, par, range(2 * i, 2 * i + 2))
                    if in_range(-1, pair, p):
                        b, _, _ = image(-1, pair, p)
                        if q == 12:
                            norm(b, 1)
                        if q == 14:
                            deviations(b, 0)
                        if q == 18:
                            pool.wait_ge(gsum_ready, count(pool, 2 * b + 2))
                            apart(pool, 2 * b + 2)
                            g.tensor_tensor(grouped(d16[:, :, :]), grouped(z[:, :, :]), wide16(gsum[:, 1, :]),
                                            ALU.subtract).then_inc(d_ready, 1)
                        if q == 22:
                            pool.wait_ge(ss_ready, count(pool, b + 1))
                            apart(pool, b + 1)
                            g.tensor_scalar(ss16[:, 1, :], ss16[:, 0, :], 1.0 / (G16 - 1), 0.0, ALU.mult, ALU.add)\
                             .then_inc(std_step, 1)
                            pool.wait_ge(std_step, count(pool, b + 1))
                            apart(pool, b + 1)
                        if q in (23, 26):
                            half_cols = slice(0, BLK * NG // 2) if q == 23 else slice(BLK * NG // 2, BLK * NG)
                            g.tensor_tensor(ss16[:, 2, half_cols], ss16[:, 1, half_cols], power[:, 1, half_cols], ALU.pow)\
                             .then_inc(std_ready, 1)
                        if q == 28:
                            pool.wait_ge(rs_step, count(pool, 2 * b + 2))
                            apart(pool, 2 * b + 2)
                            g.tensor_tensor(grouped(u[:, :, 0:C]), grouped(d16[:, :, :]), wide16(rs16[:, 1, :]),
                                            ALU.mult).then_inc(u_ready, 1)
                    if q == 30 and in_range(0, pair, p):
                        norm(image(0, pair, p)[0], 0)

            iterations(pool, iteration)

            def scatter_y(r, i):
                t = r * UNROLL + i
                pool.wait_ge(y_out_ready, 2 * t + 2)
                pool.sem_inc(waits_passed, 1)
                pool.wait_ge(d_tile_ready, t + 1)
                pool.sem_inc(waits_passed, 1)
                for k in range(2):
                    g.indirect_dma_start(
                        out=y_dram, out_offset=bass.IndirectOffsetOnAxis(ap=d_tile[:, i, k:k + 1], axis=0),
                        in_=y_out[i][:, k, :], in_offset=None, bounds_check=2 * TOKENS - 1, oob_is_err=False)\
                     .then_inc(y_scattered[i], 16)

            with pool.Fori(0, ROUNDS) as r:
                for i in range(UNROLL):
                    scatter_y(r, i)

        @block.scalar
        def _(act):
            a = nc.scalar
            act.wait_ge(weights_in, 16 * N_WEIGHT_DMAS)
            act.wait_ge(pool_const, POOL_CONSTS)

            def from_shared(name, pair, p):
                act.wait_ge(shared_ready[BANK[name]], count(act, turn(name, pair, p) + 1))
                return shared_ps[BANK[name]]

            def piece(name, pair, p):
                b, _, par = image(SHARED[name][1], pair, p)
                if name[:4] == "mrow":
                    s = int(name[4:])
                    half, h = (1, s) if s < 4 else (0, s - 4)
                    ps = from_shared(name, pair, p)
                    a.activation(qs2[64:66, par, h, half * HALF:(half + 1) * HALF], ps[64:66, :], ACT.Copy)\
                     .then_inc(mrow_ready, 1)
                elif name in ("q0", "k0", "q1", "k1"):
                    which, half = "qk".index(name[0]), int(name[1])
                    ps = from_shared(name, pair, p)
                    if name == "q0":
                        _, prp, parp = image(0, pair, p)
                        if positive(prp + 1):
                            for h in range(NH):
                                act.wait_ge(stacked1[parp][h], count(act, 16 * STACK1_DMAS * (prp + 1)))
                                apart(act, prp)
                            act.wait_ge(stacked2[parp], count(act, 16 * STACK2_DMAS * (prp + 1)))
                    a.activation(part[:, 0, which, half * HALF:(half + 1) * HALF], ps[:, :], ACT.Identity,
                                 bias=bqk[:, which:which + 1]).then_inc(high_ready, 1)
                    c = 2 * half + which
                    if positive(4 * b + c - 1):
                        act.wait_ge(rest_ready, count(act, 4 * b + c - 1))
                    a.activation(raw[:, c % 2, :], ps[:, :], ACT.Identity,
                                 bias=bqk[:, which:which + 1]).then_inc(raw_ready, 1)
                elif name in ("v0", "v1"):
                    half = int(name[1])
                    ps = from_shared(name, pair, p)
                    a.activation(v_sb[:, par, 4 * half:4 * half + 4, :].rearrange("p k c -> p (k c)"), ps[:, :],
                                 ACT.Copy).then_inc(v_ready, 1)
                elif name[:4] == "proj":
                    half = int(name[4])
                    ps = from_shared(name, pair, p)
                    if positive(2 * b):
                        act.wait_ge(t2_ready, count(act, 2 * b))
                    a.activation(t1[:, 4 * half:4 * half + 4, :].rearrange("p k c -> p (k c)"), ps[:, :],
                                 ACT.Copy).then_inc(t1_ready, 1)
                elif name[:2] == "zT":
                    half = int(name[2])
                    ps = from_shared(name, pair, p)
                    a.activation(zT[:, half * HALF:(half + 1) * HALF], ps[:, :], ACT.Copy)\
                     .then_inc(zT_ready, 1)
                elif name[:3] == "z2T":
                    half = int(name[3])
                    ps = from_shared(name, pair, p)
                    if positive(b + 1):
                        act.wait_ge(ss_ready, count(act, b + 1))
                    if positive(2 * b):
                        act.wait_ge(lmax_step, count(act, 2 * b))
                    a.activation(z2T[:, half * HALF:(half + 1) * HALF], ps[:, :], ACT.Copy)\
                     .then_inc(z2T_ready, 1)

            def normalise(b, which, src, dst, done):
                act.wait_ge(rstd_step[which], count(act, 4 * b + 4))
                for k in range(BLK):
                    a.activation(dst[:, k, :], src[:, k, :], ACT.Identity, bias=rstd[:, which, 0, k:k + 1],
                                 scale=rstd[:, which, 1, k:k + 1]).then_inc(done, 1)

            def values_out(b, half):
                act.wait_ge(probs_used, count(act, 8 * b + 4 * half + 4))
                if half == 0 and positive(2 * b):
                    act.wait_ge(t1_ready, count(act, 2 * b))
                a.activation(avn[:, half * HALF:(half + 1) * HALF], av_ps[:, :], ACT.Copy).then_inc(av_out, 1)

            def denominators_out(b, half):
                act.wait_ge(den_done, count(act, 8 * b + 4 * half + 4))
                if positive(2 * b + half):
                    act.wait_ge(norm_step, count(act, 2 * b + half))
                a.activation(rden[:, :], den_ps[:, :], ACT.Copy).then_inc(av_out, 1)

            def iteration(pair, p):
                for q in range(QUARTERS):
                    s, j = divmod(q, 4)
                    if q == 4 and in_range(-1, pair, p):
                        values_out(image(-1, pair, p)[0], 1)
                    if q == 5 and in_range(-1, pair, p):
                        denominators_out(image(-1, pair, p)[0], 1)
                    if q == 20 and in_range(0, pair, p):
                        values_out(image(0, pair, p)[0], 0)
                    if q == 21 and in_range(0, pair, p):
                        denominators_out(image(0, pair, p)[0], 0)
                    if in_range(0, pair, p):
                        b, _, par = image(0, pair, p)
                        for t in (2 * j, 2 * j + 1):
                            tile = 64 * b + 8 * s + t
                            if t == 0:
                                if positive(8 * b + s - 1):
                                    act.wait_ge(probs_used, count(act, 8 * b + s - 1))
                                    act.wait_ge(pairs_pool, count(act, 8 * b + s - 1))
                                    act.wait_ge(pairs_dve, count(act, 8 * b + s - 1))
                            act.wait_ge(st_ready, count(act, tile + 1))
                            a.activation(probs[:, 8 * (s % 2) + t, :], st_ps[t % 2][:, :], ACT.Exp,
                                         scale=float(C) ** -0.5).then_inc(exp_done, 1)
                    for name in at_quarter(q, pair, p):
                        piece(name, pair, p)
                    if q == 24 and in_range(0, pair, p):
                        b, _, _ = image(0, pair, p)
                        act.wait_ge(xres_loaded, count(act, 16 * b + 16))
                        a.activation(x_res[:, :], x_res[:, :], ACT.Identity, bias=bo[:, :]).then_inc(xr_ready, 1)
                    if q == 7 and in_range(-2, pair, p):
                        b, pr, _ = image(-2, pair, p)
                        if positive(32 * BLK * pr):
                            act.wait_ge(scattered[p], count(act, 32 * BLK * pr))
                        normalise(b, 1, t2, rows[:, p, :, 0:C], z2_ready)
                    if q == 17 and in_range(-1, pair, p):
                        normalise(image(-1, pair, p)[0], 0, t1, z, z_ready)
                    if q == 20 and in_range(-1, pair, p):
                        b, _, _ = image(-1, pair, p)
                        act.wait_ge(d_ready, count(act, b + 1))
                        a.activation(sq16[:, :, :], d16[:, :, :], ACT.Square).then_inc(sq_ready, 1)
                    if q == 13 and in_range(-2, pair, p):
                        b, _, _ = image(-2, pair, p)
                        act.wait_ge(lsub_ready, count(act, b + 1))
                        a.activation(lg[:, 1, :, :], lg[:, 0, :, :], ACT.Exp).then_inc(gexp_ready, 1)

            iterations(act, iteration)

            def turned(r, i):
                t = r * UNROLL + i
                act.wait_ge(zT_ps, t + 1)
                if positive(t - 1):
                    act.wait_ge(hid_ps, t - 1)
                a.activation(zT_tile[i % 2], bank[2 + i % 2][:, 0:TILE], ACT.Copy).then_inc(zT_tile_ready, 1)

            def hidden(r, i):
                t = r * UNROLL + i
                act.wait_ge(b1_tile_ready, t + 1)
                act.wait_ge(hid_ps, t + 1)
                if positive(t - 1):
                    act.wait_ge(y_ps, t - 1)
                for j in range(HC):
                    a.activation(hid[i % 2][:, j, :], bank[i % 2][:, j * TILE:(j + 1) * TILE], ACT.Gelu,
                                 bias=b1_tile[:, i % 2, j:j + 1]).then_inc(hid_ready, 1)

            def weighted(r, i):
                t = r * UNROLL + i
                act.wait_ge(y_sum_ready, t + 1)
                act.wait_ge(w_tile_ready, t + 1)
                if positive(r):
                    act.wait_ge(y_scattered[i], 32 * r)
                for k in range(2):
                    a.activation(y_out[i][:, k, :], y_sum[i % 2][:, k, :], ACT.Copy,
                                 scale=w_tile[:, i, k:k + 1]).then_inc(y_out_ready, 1)

            act.wait_ge(v_ready, 2 * B)
            act.wait_ge(t1_ready, 2 * B)
            act.wait_ge(low_ready, 4 * B)
            turned(0, 0)
            for i in range(UNROLL):
                turned((i + 1) // UNROLL, (i + 1) % UNROLL)
                hidden(0, i)
                if i > 0:
                    weighted(0, i - 1)
            with act.Fori(1, ROUNDS - 1) as r:
                for i in range(UNROLL):
                    turned(r if i < UNROLL - 1 else r + 1, (i + 1) % UNROLL)
                    hidden(r, i)
                    weighted(r - 1 if i == 0 else r, (i - 1) % UNROLL)
            for i in range(UNROLL):
                if i < UNROLL - 1:
                    turned(ROUNDS - 1, i + 1)
                hidden(ROUNDS - 1, i)
                weighted(ROUNDS - 2 if i == 0 else ROUNDS - 1, (i - 1) % UNROLL)
            weighted(ROUNDS - 1, UNROLL - 1)

            def write_out(r, i):
                act.wait_ge(outT_ps, 4 * r + i + 1)
                if positive(r):
                    act.wait_ge(out_stored[i], 16 * r)
                a.activation(outT[i], bank[i % 2][:, :], ACT.Copy).then_inc(outT_ready, 1)

            for i in range(4):
                write_out(0, i)
            with act.Fori(1, B // 2) as r:
                for i in range(4):
                    write_out(r, i)

        @block.vector
        def _(dve):
            v = nc.vector
            dve.wait_ge(weights_in, 16 * N_WEIGHT_DMAS)
            dve.wait_ge(pool_const, POOL_CONSTS)
            v.tensor_copy(identb[:, :], ident[:, :]).then_inc(dve_const, 1)
            v.tensor_scalar(kb_n[:, :], kcol[:, 1:2], float(N), None, ALU.mult).then_inc(dve_const, 1)
            for par in range(2):
                v.memset(ks2[64:66, par, :, :], 1.0).then_inc(ones_rows, 1)
            v.tensor_copy(tile_no[:, :], counting[:, 0:TILES]).then_inc(dve_const, 1)
            v.tensor_copy(filled[:, :], counting[:, TILES:TILES + MOST]).then_inc(dve_const, 1)
            v.tensor_copy(token[:, :], counting[:, TILES + MOST:]).then_inc(dve_const, 1)
            v.tensor_copy(base[:, :], region[:, :]).then_inc(dve_const, 1)
            v.memset(before[:, 0, :], 0.0).then_inc(dve_const, 1)
            dve.wait_ge(bn_step, 2)
            v.tensor_tensor(bn_scale[:, :], bn_tmp[:, 1:2], bn[:, 0:1], ALU.mult).then_inc(bn_step, 1)
            dve.wait_ge(bn_step, 3)
            v.tensor_tensor(bn_tmp[:, 0:1], bn_scale[:, :], bn[:, 2:3], ALU.mult).then_inc(bn_step, 1)
            dve.wait_ge(bn_step, 4)
            v.tensor_tensor(bn_shift[:, :], bn[:, 1:2], bn_tmp[:, 0:1], ALU.subtract).then_inc(bn_step, 1)
            for j in range(3):
                dve.wait_ge(wT_ps, count(dve, j + 1))
                for blk in range(4):
                    h, kind = divmod(4 * j + blk, 3)
                    v.tensor_copy(wqkvT[:, kind, h, :], bank[j][:, HD * blk:HD * blk + HD]).then_inc(wT_ready, 1)
            dve.wait_ge(wT_ps, 4)
            v.tensor_copy(woT[:, :], bank[3][:, 0:P]).then_inc(wT_ready, 1)
            dve.wait_ge(wT_ps, 5)
            v.tensor_copy(b1[:, :, :].rearrange("p e j -> p (e j)"), bank[4][:, 0:E * HC]).then_inc(wT_ready, 1)
            dve.wait_ge(bn_step, 5)
            dve.wait_ge(dve_const, 7)

            def from_shared(name, pair, p):
                dve.wait_ge(shared_ready[BANK[name]], count(dve, turn(name, pair, p) + 1))
                return shared_ps[BANK[name]]

            def add_pairs(b, s):
                dve.wait_ge(exp_done, count(dve, 64 * b + 8 * s + 8))
                if positive(8 * b + s):
                    dve.wait_ge(den_done, count(dve, 8 * b + s))
                first = 8 * (s % 2)
                v.tensor_tensor(pairs[:, POOL_HEADS:, :], probs[:, first + POOL_HEADS:first + 4, :],
                                probs[:, first + 4 + POOL_HEADS:first + 8, :], ALU.add).then_inc(pairs_dve, 1)

            def reciprocals(b, half, i):
                dve.wait_ge(av_out, count(dve, 4 * b + 2 * half + 2))
                r = rden[:, i * P:(i + 1) * P]
                v.reciprocal(r, r).then_inc(rden_ready, 1)

            def layer_stats(b, which, src, half):
                blocks = range(4 * half, 4 * half + 4)
                for k in blocks:
                    v.bn_stats(stats[:, which, k, :], src[:, k, :]).then_inc(stats_done[which], 1)
                if half == 1:
                    dve.wait_ge(stats_done[which], count(dve, BLK * b + BLK))
                    apart(dve, BLK * b + BLK)
                    for k in range(BLK):
                        m = v.bn_aggr(mv[:, which, k, :], stats[:, which, k, :])
                    m.then_inc(mv_ready[which], 1)

            def piece(name, pair, p):
                b, _, par = image(SHARED[name][1], pair, p)
                if name == "gram":
                    ps = from_shared(name, pair, p)
                    v.tensor_copy(usum[:, :], ps[:, C:C + 1]).then_inc(kv_step, 1)
                    dve.wait_ge(kv_step, count(dve, 6 * b + 1))
                    v.tensor_scalar(udiag[:, :], ident[:, :], usum[:, :], None, ALU.mult).then_inc(udiag_ready, 1)
                    v.tensor_scalar(kvw[:, 0, :], ps[:, 0:C], kcol[:, 0:1], None, ALU.mult).then_inc(kv_step, 1)
                    v.scalar_tensor_tensor(kcc[:, :], usum[:, :], kcol[:, 0:1], kb_n[:, :], ALU.mult, ALU.add)\
                     .then_inc(kv_step, 1)
                elif name[:3] == "t2_":
                    half = int(name[3])
                    ps = from_shared(name, pair, p)
                    if positive(16 * b):
                        dve.wait_ge(t2_stored, count(dve, 16 * b))
                    if positive(BLK * b):
                        dve.wait_ge(z2_ready, count(dve, BLK * b))
                    v.tensor_tensor(t2[:, 4 * half:4 * half + 4, :], ps[:, :].rearrange("p (k c) -> p k c", c=C),
                                    t1[:, 4 * half:4 * half + 4, :], ALU.add).then_inc(t2_ready, 1)
                    dve.wait_ge(t2_ready, count(dve, 2 * b + half + 1))
                    layer_stats(b, 1, t2, half)
                elif name == "logits":
                    ps = from_shared(name, pair, p)
                    pl = ps[:, 0:BLK * E].rearrange("p (k e) -> p k e", e=E)
                    v.tensor_tensor(lg[:, 2, :, :], pl, gate_b[:, :].unsqueeze(1).broadcast_to([P, BLK, E]),
                                    ALU.add).then_inc(lmax_step, 1)
                    dve.wait_ge(lmax_step, count(dve, 2 * b + 1))
                    v.tensor_reduce(lred[:, 0, :], lg[:, 2, :, :], AX.X, ALU.max).then_inc(lmax_step, 1)
                    dve.wait_ge(lmax_step, count(dve, 2 * b + 2))
                    v.tensor_tensor(lg[:, 0, :, :], lg[:, 2, :, :],
                                    lred[:, 0, :].unsqueeze(2).broadcast_to([P, BLK, E]), ALU.subtract)\
                     .then_inc(lsub_ready, 1)

            def kv_product(b, which, pair=None, p=None):
                if which == 0:
                    ps = from_shared("usum", pair, p)
                    dve.wait_ge(kv_step, count(dve, 6 * b + 3))
                    v.scalar_tensor_tensor(kvw[:, 1, :], ps[:, 0:C], kcol[:, 1:2], kvw[:, 0, :],
                                           ALU.mult, ALU.add).then_inc(kv_step, 1)
                elif which == 1:
                    dve.wait_ge(kv_step, count(dve, 6 * b + 4))
                    v.tensor_tensor(kvw[:, 2, :], kvw[:, 1, :], vrow[:, 0, :], ALU.mult).then_inc(kv_step, 1)
                elif which == 2:
                    dve.wait_ge(kv_step, count(dve, 6 * b + 5))
                    v.scalar_tensor_tensor(kvw[:, 3, :], vrow[:, 1, :], kcc[:, :], kvw[:, 2, :],
                                           ALU.mult, ALU.add).then_inc(kv_step, 1)
                else:
                    dve.wait_ge(kv_step, count(dve, 6 * b + 6))
                    v.tensor_tensor(kvw[:, 4, :], kvw[:, 3, :], headmask[:, :], ALU.mult).then_inc(bd_ready, 1)
                    dve.wait_ge(bd_ready, count(dve, 2 * b + 1))
                    v.tensor_tensor(bd[:, :], kvw[:, 4, :], ident[:, :], ALU.add).then_inc(bd_ready, 1)

            GATE_STEPS = {15: range(0, 3), 16: range(3, 6), 17: range(6, 7), 19: range(7, 10), 20: range(10, 13),
                          23: range(13, 14), 24: range(14, 15), 26: range(15, 16)}

            def gate(b, par, steps):
                def wide(r):
                    return lred[:, r, :].unsqueeze(2).broadcast_to([P, BLK, E])

                rank = rank_w[:, :].unsqueeze(1).broadcast_to([P, BLK, E])
                ex, pr, pr2 = lg[:, 1, :, :], lg[:, 3, :, :], lg[:, 4, :, :]
                w, sel1, sel2, eq = lg[:, 5, :, :], lg[:, 6, :, :], lg[:, 7, :, :], lg[:, 8, :, :]
                for step in steps:
                    if step == 0:
                        dve.wait_ge(gexp_ready, count(dve, b + 1))
                    else:
                        dve.wait_ge(gate_step, count(dve, 16 * b + step))
                    if step == 0:
                        ins = v.tensor_reduce(lred[:, 1, :], ex, AX.X, ALU.add)
                    elif step == 1:
                        ins = v.reciprocal(lred[:, 2, :], lred[:, 1, :])
                    elif step == 2:
                        ins = v.tensor_tensor(pr, ex, wide(2), ALU.mult)
                    elif step == 3:
                        ins = v.tensor_reduce(lred[:, 3, :], pr, AX.X, ALU.max)
                    elif step == 4:
                        ins = v.tensor_tensor(eq, pr, wide(3), ALU.is_equal)
                    elif step == 5:
                        ins = v.tensor_tensor(w, eq, rank, ALU.mult)
                    elif step == 6:
                        ins = v.tensor_reduce(lred[:, 4, :], w, AX.X, ALU.max)
                    elif step == 7:
                        ins = v.tensor_tensor(sel1, w, wide(4), ALU.is_equal)
                    elif step == 8:
                        ins = v.scalar_tensor_tensor(pr2, sel1, -2.0, pr, ALU.mult, ALU.add)
                    elif step == 9:
                        ins = v.tensor_reduce(lred[:, 5, :], pr2, AX.X, ALU.max)
                    elif step == 10:
                        ins = v.tensor_tensor(eq, pr2, wide(5), ALU.is_equal)
                    elif step == 11:
                        ins = v.tensor_tensor(w, eq, rank, ALU.mult)
                    elif step == 12:
                        ins = v.tensor_reduce(lred[:, 6, :], w, AX.X, ALU.max)
                    elif step == 13:
                        ins = v.tensor_tensor(sel2, w, wide(6), ALU.is_equal)
                    elif step == 14:
                        ins = v.tensor_tensor(eq, sel1, sel2, ALU.add)
                    else:
                        ins = v.tensor_tensor(rows[:, par, :, WAT:DAT], pr, eq, ALU.mult)
                    ins.then_inc(gate_step, 1)

            def prefix(b, blocks):
                for k in blocks:
                    if k == 0:
                        dve.wait_ge(gate_step, count(dve, 16 * b + 15))
                    else:
                        dve.wait_ge(prefix_step, count(dve, 8 * b + k))
                    v.tensor_tensor(before[:, k + 1, :], before[:, k, :], lg[:, 8, k, :], ALU.add)\
                     .then_inc(prefix_step, 1)

            def slots(b, par, pair, p):
                ps = from_shared("rank", pair, p)
                if positive(b):
                    dve.wait_ge(base_ready, count(dve, b))
                v.tensor_tensor(slot[:, 0, :, :], ps[:, 0:BLK * E].rearrange("p (k e) -> p k e", e=E),
                                base[:, :].unsqueeze(1).broadcast_to([P, BLK, E]), ALU.add).then_inc(slot_step, 1)
                dve.wait_ge(slot_step, count(dve, 6 * b + 1))
                for c in range(2):
                    v.tensor_tensor(slot[:, 1 + c, :, :], slot[:, 0, :, :], lg[:, 6 + c, :, :], ALU.mult)\
                     .then_inc(slot_step, 1)
                if positive(b):
                    dve.wait_ge(token_ready, count(dve, b))
                v.scalar_tensor_tensor(rows[:, par, :, DAT:ROW], lg[:, 7, :, :], float(TOKENS),
                                       token[:, :].unsqueeze(2).broadcast_to([P, BLK, E]), ALU.mult, ALU.add)\
                 .then_inc(slot_step, 1)

            def move_on(b, pair, p):
                ps = from_shared("total", pair, p)
                v.tensor_tensor(base[:, :], base[:, :], ps[:, 0:E], ALU.add).then_inc(base_ready, 1)
                v.tensor_scalar(token[:, :], token[:, :], float(N), None, ALU.add).then_inc(token_ready, 1)

            def slot_numbers(b, par):
                dve.wait_ge(slot_step, count(dve, 6 * b + 4))
                for c in range(2):
                    v.tensor_reduce(slot_of[:, c, :], slot[:, 1 + c, :, :], AX.X, ALU.add).then_inc(slot_step, 1)
                dve.wait_ge(slot_step, count(dve, 6 * b + 6))
                v.tensor_copy(slot_idx[:, par, :], slot_of[:, :, :].rearrange("p c k -> p (c k)")).then_inc(idx_ready, 1)

            def iteration(pair, p):
                for q in range(QUARTERS):
                    s, j = divmod(q, 4)
                    lag, half, h = row_target(s + 1)
                    if in_range(lag, pair, p):
                        b, _, _ = image(lag, pair, p)
                        for kh in range(2):
                            n = 64 * b + 32 * half + 8 * h + 2 * j + kh
                            dve.wait_ge(row_ready, count(dve, n + 1))
                            v.tensor_reduce(rowmax[:, h % 2, kh, j:j + 1], row_ps[kh][:, :], AX.X, ALU.max)\
                             .then_inc(row_used, 1)
                    lag, half, h = row_target(s)
                    if j < 2 and in_range(lag, pair, p):
                        b, _, _ = image(lag, pair, p)
                        g = 8 * b + 4 * half + h
                        if j == 0:
                            dve.wait_ge(row_used, count(dve, 8 * g + 8))
                            v.tensor_tensor(rowm[:, h % 2, :], rowmax[:, h % 2, 0, :], rowmax[:, h % 2, 1, :],
                                            ALU.max).then_inc(max_step, 1)
                            dve.wait_ge(max_step, count(dve, 2 * g + 1))
                            if positive(g - 1):
                                dve.wait_ge(mrow_ready, count(dve, g - 1))
                            v.tensor_scalar(negm[:, h % 2, :, 0], rowm[:, h % 2, :], -1.0, None, ALU.mult)\
                             .then_inc(max_step, 1)
                        else:
                            dve.wait_ge(max_step, count(dve, 2 * g + 2))
                            v.scalar_tensor_tensor(negm[:, h % 2, :, 1], rowm[:, h % 2, :], -1.0,
                                                   negm[:, h % 2, :, 0], ALU.mult, ALU.subtract)\
                             .then_inc(negm_ready, 1)
                    lag, before_s = steps_before(s, 1)
                    if j == 1 and in_range(lag, pair, p):
                        add_pairs(image(lag, pair, p)[0], before_s)
                    if q == 0 and in_range(1, pair, p):
                        b, pr, par = image(1, pair, p)
                        dve.wait_ge(x_loaded, count(dve, 16 * b + 16))
                        v.tensor_scalar(xn[:, :], x_in[:, :], bn_scale[:, :], bn_shift[:, :],
                                        ALU.mult, ALU.add).then_inc(xn_ready, 1)
                    if q < 3 and in_range(-2, pair, p):
                        kv_product(image(-2, pair, p)[0], q + 1)
                    if q in (6, 7, 8, 11) and in_range(-1, pair, p):
                        reciprocals(image(-1, pair, p)[0], 1, (6, 7, 8, 11).index(q))
                    if q in (23, 24, 26, 27) and in_range(0, pair, p):
                        reciprocals(image(0, pair, p)[0], 0, (23, 24, 26, 27).index(q))
                    for name in at_quarter(q, pair, p):
                        piece(name, pair, p)
                    if in_range(-1, pair, p):
                        b, _, _ = image(-1, pair, p)
                        if q in (10, 14):
                            half1 = (q - 10) // 4
                            dve.wait_ge(t1_ready, count(dve, 2 * b + half1 + 1))
                            layer_stats(b, 0, t1, half1)
                        if q == 18:
                            dve.wait_ge(z_ready, count(dve, BLK * b + BLK))
                            v.tensor_reduce(gsum[:, 0, :], z[:, :, :].rearrange("p k (g d) -> p (k g) d", d=G16),
                                            AX.X, ALU.add).then_inc(gsum_ready, 1)
                            dve.wait_ge(gsum_ready, count(dve, 2 * b + 1))
                            v.tensor_scalar(gsum[:, 1, :], gsum[:, 0, :], 1.0 / G16, None, ALU.mult)\
                             .then_inc(gsum_ready, 1)
                        if q == 22:
                            dve.wait_ge(sq_ready, count(dve, b + 1))
                            v.tensor_reduce(ss16[:, 0, :], sq16[:, :, :].rearrange("p k (g d) -> p (k g) d", d=G16),
                                            AX.X, ALU.add).then_inc(ss_ready, 1)
                        if q == 28:
                            dve.wait_ge(std_ready, count(dve, 2 * b + 2))
                            v.tensor_scalar(rs16[:, 0, :], ss16[:, 2, :], EPS_HEAD, None, ALU.add)\
                             .then_inc(rs_step, 1)
                            dve.wait_ge(rs_step, count(dve, 2 * b + 1))
                            v.reciprocal(rs16[:, 1, :], rs16[:, 0, :]).then_inc(rs_step, 1)
                        if q == 31:
                            kv_product(b, 0, pair, p)
                    if in_range(-2, pair, p):
                        b, _, _ = image(-2, pair, p)
                        if q in GATE_STEPS:
                            gate(b, p, GATE_STEPS[q])
                        if q in (27, 28, 30):
                            prefix(b, {27: range(0, 2), 28: range(2, 5), 30: range(5, BLK)}[q])
                    if in_range(-3, pair, p):
                        b, _, par = image(-3, pair, p)
                        if q == 2:
                            slots(b, par, pair, p)
                        if q == 8:
                            slot_numbers(b, par)
                        if q == 10:
                            move_on(b, pair, p)

            iterations(dve, iteration)

            steps = [0]

            def then(ins):
                steps[0] += 1
                ins.then_inc(table_step, 1)
                dve.wait_ge(table_step, steps[0])

            dve.wait_ge(den_done, 8 * B)
            dve.wait_ge(base_ready, B)

            def space(first, *shape):
                size = shape[0] * (shape[1] if len(shape) > 1 else 1)
                v_ = tables[:, first:first + size]
                return v_.rearrange("p (a b) -> p a b", a=shape[0]) if len(shape) > 1 else v_

            used, tiles_of, until = space(0, E), space(E, E), space(2 * E, E)
            full, sums = space(3 * E, E, MOST), space(3 * E, E, E)
            passed = space(3 * E, TILES, E)
            work = [space(3 * E + TILES * (E + i), TILES) for i in range(4)]
            then(v.tensor_tensor(used, base[:, :], region[:, :], ALU.subtract))
            then(v.tensor_tensor(full, used.unsqueeze(2).broadcast_to([P, E, MOST]),
                                 filled[:, :].unsqueeze(1).broadcast_to([P, E, MOST]), ALU.is_ge))
            then(v.tensor_reduce(tiles_of, full, AX.X, ALU.add))
            then(v.tensor_tensor(sums, emask[:, :, :], tiles_of.unsqueeze(1).broadcast_to([P, E, E]), ALU.mult))
            then(v.tensor_reduce(until, sums, AX.X, ALU.add))
            then(v.tensor_tensor(passed, tile_no[:, :].unsqueeze(2).broadcast_to([P, TILES, E]),
                                 until.unsqueeze(1).broadcast_to([P, TILES, E]), ALU.is_ge))
            then(v.tensor_reduce(work[0], passed, AX.X, ALU.add))
            then(v.tensor_tensor(passed, passed, tiles_of.unsqueeze(1).broadcast_to([P, TILES, E]), ALU.mult))
            then(v.tensor_reduce(work[1], passed, AX.X, ALU.add))
            then(v.tensor_tensor(work[2], tile_no[:, :], work[1], ALU.subtract))
            then(v.tensor_scalar(work[1], work[0], float(CAP), None, ALU.mult))
            then(v.scalar_tensor_tensor(work[3], work[2], float(TILE), work[1], ALU.mult, ALU.add))
            then(v.tensor_copy(tile_row[:, :], work[3]))
            v.tensor_copy(region_end[:, :], base[:, :])
            then(v.tensor_scalar(work[2], work[0], float(E - 1), None, ALU.min))
            then(v.tensor_copy(tile_expert[:, :], work[2]))
            assert steps[0] == TABLE_STEPS

            def expert(t):
                return dve.value_load(tile_expert[0:1, bass.ds(t, 1)], min_val=0, max_val=E - 1)

            def prepare(r, i):
                t = r * UNROLL + i
                e = expert(t)
                dve.wait_ge(z_loaded[i % DEPTH], 16 * (2 * r + i // DEPTH + 1))
                if positive(r):
                    dve.wait_ge(y_scattered[i], 32 * r)
                cols = z_rows[i % DEPTH]
                v.tensor_copy(w_tile[:, i, :].unsqueeze(2), cols[:, :, bass.ds(e + WAT, 1)]).then_inc(w_tile_ready, 1)
                v.tensor_copy(d_tile[:, i, :].unsqueeze(2), cols[:, :, bass.ds(e + DAT, 1)]).then_inc(d_tile_ready, 1)
                if positive(t - 1):
                    dve.wait_ge(hid_ps, t - 1)
                v.tensor_copy(w1_tile[i % 2], w1[:, bass.ds(e, 1), :].rearrange("p a i -> p (a i)"))\
                 .then_inc(w1_tile_ready, 1)
                if positive(t - 1):
                    dve.wait_ge(hid_ready, HC * (t - 1))
                v.tensor_copy(b1_tile[:, i % 2, :], b1[:, bass.ds(e, 1), :].rearrange("p a j -> p (a j)"))\
                 .then_inc(b1_tile_ready, 1)
                if positive(t - 3):
                    dve.wait_ge(y_sum_ready, t - 3)
                v.tensor_copy(b2_tile[i % 4], b2[:, bass.ds(e, 1), :].rearrange("p a c -> p (a c)"))\
                 .then_inc(b2_tile_ready, 1)

            def add_bias(r, i):
                t = r * UNROLL + i
                dve.wait_ge(y_ps, t + 1)
                dve.wait_ge(b2_tile_ready, t + 1)
                if positive(t - 1):
                    dve.wait_ge(y_out_ready, 2 * (t - 1))
                v.tensor_tensor(y_sum[i % 2], bank[4 + i % 2][:, 0:TILE].rearrange("p (k c) -> p k c", k=2),
                                b2_tile[i % 4].unsqueeze(1).broadcast_to([P, 2, C]), ALU.add).then_inc(y_sum_ready, 1)

            dve.wait_ge(experts_in, 48)
            dve.wait_ge(low_ready, 4 * B)
            for i in range(UNROLL):
                prepare(0, i)
                if i > 1:
                    add_bias(0, i - 2)
            with dve.Fori(1, ROUNDS) as r:
                for i in range(UNROLL):
                    prepare(r, i)
                    add_bias(r - 1 if i < 2 else r, (i - 2) % UNROLL)
            add_bias(ROUNDS - 1, UNROLL - 2)
            add_bias(ROUNDS - 1, UNROLL - 1)

            dve.wait_ge(t2_loaded, 16 * (B // 2))

            def add_up(r, i):
                half = i % 2
                n = 4 * r + i
                dve.wait_ge(y_in_ready[i], 32 * r + 32)
                v.tensor_tensor(y_in[i][0], y_in[i][0], y_in[i][1], ALU.add).then_inc(sum_step, 1)
                dve.wait_ge(sum_step, 2 * n + 1)
                t2_part = t2_all[:, bass.ds(2 * r + i // 2, 1), 4 * half:4 * half + 4, :]\
                    .rearrange("p a k c -> p (a k) c")
                v.tensor_tensor(y_in[i][0], y_in[i][0], t2_part, ALU.add).then_inc(sum_step, 1)

            with dve.Fori(0, B // 2) as r:
                for i in range(4):
                    add_up(r, i)

        @block.tensor
        def _(pe):
            t_ = nc.tensor
            pe.wait_ge(weights_in, 16 * N_WEIGHT_DMAS)
            pe.wait_ge(pool_const, POOL_CONSTS)
            for j in range(3):
                t_.transpose(bank[j][:, 0:P], wload[:, j, :], ident[:, :]).then_inc(wT_ps, 1)
            t_.transpose(bank[3][:, 0:P], woload, ident[:, :]).then_inc(wT_ps, 1)
            t_.transpose(bank[4][:, 0:E * HC], b1_rows, ident[0:E * HC, 0:E * HC]).then_inc(wT_ps, 1)
            pe.wait_ge(wT_ready, 14)
            pe.wait_ge(ones_rows, 2)
            pe.wait_ge(dve_const, 7)

            def piece(name, pair, p):
                b, _, par = image(SHARED[name][1], pair, p)
                bk = BANK[name]
                ps = shared_ps[bk]
                if name in ("q0", "k0", "q1", "k1"):
                    which, half = "qk".index(name[0]), int(name[1])
                    pe.wait_ge(xn_ready, count(pe, b + 1))
                    free_shared(name, pair, p)
                    last = t_.matmul(ps[:, :], wqkvT[:, which, :, :].rearrange("p n d -> p (n d)"),
                                     xn[:, half * HALF:(half + 1) * HALF], start=True, stop=True)
                elif name in ("v0", "v1"):
                    free_shared(name, pair, p)
                    half = int(name[1])
                    for i in range(4):
                        k = 4 * half + i
                        last = t_.matmul(ps[:, i * C:(i + 1) * C], xn[:, k * P:(k + 1) * P],
                                         wqkvT[:, 2, :, :].rearrange("p n d -> p (n d)"), start=True, stop=True)
                elif name[:4] == "mrow":
                    s = int(name[4:])
                    half, h = (1, s) if s < 4 else (0, s - 4)
                    pe.wait_ge(negm_ready, count(pe, 8 * b + 4 * half + h + 1))
                    free_shared(name, pair, p)
                    for i in range(4):
                        last = t_.matmul(ps[64:66, i * P:(i + 1) * P], negm[:, h % 2, i, :], identb[:, :],
                                         start=True, stop=True)
                elif name[:4] == "proj":
                    half = int(name[4])
                    pe.wait_ge(xr_ready, count(pe, b + 1))
                    pe.wait_ge(norm_done, count(pe, 2 * b + half + 1))
                    free_shared(name, pair, p)
                    for i in range(4):
                        k = 4 * half + i
                        o = ps[:, i * C:(i + 1) * C]
                        t_.matmul(o, avn[:, k * P:(k + 1) * P], woT[:, :], start=True, stop=False)
                        last = t_.matmul(o, x_res[:, k * P:(k + 1) * P], ident[:, :], start=False, stop=True)
                elif name[:2] == "zT":
                    half = int(name[2])
                    pe.wait_ge(z_ready, count(pe, BLK * b + 4 * half + 4))
                    free_shared(name, pair, p)
                    for i in range(4):
                        last = t_.transpose(ps[:, i * P:(i + 1) * P], z[:, 4 * half + i, :], ident[:, :])
                elif name == "gram":
                    pe.wait_ge(u_ready, count(pe, b + 1))
                    free_shared(name, pair, p)
                    for k in range(BLK):
                        last = t_.matmul(ps[:, 0:C + 1], u[:, k, 0:C], u[:, k, :],
                                         start=(k == 0), stop=(k == BLK - 1))
                elif name == "usum":
                    pe.wait_ge(udiag_ready, count(pe, b + 1))
                    free_shared(name, pair, p)
                    last = t_.matmul(ps[:, 0:C], ones[:, :], udiag[:, :], start=True, stop=True)
                elif name[:3] == "t2_":
                    half = int(name[3])
                    pe.wait_ge(zT_ready, count(pe, 2 * b + half + 1))
                    pe.wait_ge(bd_ready, count(pe, 2 * b + 2))
                    free_shared(name, pair, p)
                    for i in range(4):
                        k = 4 * half + i
                        last = t_.matmul(ps[:, i * C:(i + 1) * C], zT[:, k * P:(k + 1) * P], bd[:, :],
                                         start=True, stop=True)
                elif name[:3] == "z2T":
                    half = int(name[3])
                    pe.wait_ge(z2_ready, count(pe, BLK * b + 4 * half + 4))
                    free_shared(name, pair, p)
                    for i in range(4):
                        last = t_.transpose(ps[:, i * P:(i + 1) * P], rows[:, par, 4 * half + i, 0:C], ident[:, :])
                elif name == "rank":
                    pe.wait_ge(prefix_step, count(pe, 8 * b + 8))
                    free_shared(name, pair, p)
                    t_.matmul(ps[:, 0:BLK * E], tri[:, :], lg[:, 8, :, :].rearrange("p k e -> p (k e)"),
                              start=True, stop=False)
                    last = t_.matmul(ps[:, 0:BLK * E], ones[:, :],
                                     before[:, 0:BLK, :].rearrange("p k e -> p (k e)"), start=False, stop=True)
                elif name == "total":
                    free_shared(name, pair, p)
                    last = t_.matmul(ps[:, 0:E], ones[:, :], before[:, BLK, :], start=True, stop=True)
                elif name == "logits":
                    pe.wait_ge(z2T_ready, count(pe, 2 * b + 2))
                    free_shared(name, pair, p)
                    for k in range(BLK):
                        last = t_.matmul(ps[:, k * E:(k + 1) * E], z2T[:, k * P:(k + 1) * P], gate_w[:, :],
                                         start=True, stop=True)
                last.then_inc(shared_ready[bk], 1)

            def free_shared(name, pair, p):
                prev_name, prev_pair, prev_p = previous(name, pair, p)
                if prev_name is None:
                    return
                b = image(SHARED[prev_name][1], prev_pair, prev_p)[0]
                if prev_name in ("q0", "k0", "q1", "k1"):
                    pe.wait_ge(raw_ready, count(pe, 4 * b + 2 * int(prev_name[1]) + "qk".index(prev_name[0]) + 1))
                elif prev_name in ("v0", "v1"):
                    pe.wait_ge(v_ready, count(pe, 2 * b + int(prev_name[1]) + 1))
                elif prev_name[:4] == "mrow":
                    s = int(prev_name[4:])
                    half, h = (1, s) if s < 4 else (0, s - 4)
                    pe.wait_ge(mrow_ready, count(pe, 8 * b + 4 * half + h + 1))
                elif prev_name[:4] == "proj":
                    pe.wait_ge(t1_ready, count(pe, 2 * b + int(prev_name[4]) + 1))
                elif prev_name[:2] == "zT":
                    pe.wait_ge(zT_ready, count(pe, 2 * b + int(prev_name[2]) + 1))
                elif prev_name == "gram":
                    pe.wait_ge(kv_step, count(pe, 6 * b + 3))
                elif prev_name == "usum":
                    pe.wait_ge(kv_step, count(pe, 6 * b + 4))
                elif prev_name[:3] == "t2_":
                    pe.wait_ge(t2_ready, count(pe, 2 * b + int(prev_name[3]) + 1))
                elif prev_name[:3] == "z2T":
                    pe.wait_ge(z2T_ready, count(pe, 2 * b + int(prev_name[3]) + 1))
                elif prev_name == "rank":
                    pe.wait_ge(slot_step, count(pe, 6 * b + 1))
                elif prev_name == "total":
                    pe.wait_ge(base_ready, count(pe, b + 1))
                elif prev_name == "logits":
                    pe.wait_ge(lmax_step, count(pe, 2 * b + 1))

            def previous(name, pair, p):
                mine = [n for n in ORDER if BANK[n] == BANK[name]]
                i = mine.index(name)
                while True:
                    i -= 1
                    if i < 0:
                        i = len(mine) - 1
                        pair, p = (pair, 0) if p == 1 else (pair - 1, 1)
                        if isinstance(pair, int) and 2 * pair + p < FIRST:
                            return None, None, None
                    if in_range(SHARED[mine[i]][1], pair, p):
                        return mine[i], pair, p

            def iteration(pair, p):
                for q in range(QUARTERS):
                    s, j = divmod(q, 4)
                    if in_range(0, pair, p):
                        b, pr, par = image(0, pair, p)
                        half = s // 4
                        for t in (2 * j, 2 * j + 1):
                            kb, h = 2 * (s % 4) + t // 4, t % 4
                            keys = slice(kb * P, (kb + 1) * P)
                            queries = slice(half * HALF, (half + 1) * HALF)
                            tile = 64 * b + 8 * s + t
                            if s % 4 == 0 and t < 4:
                                pe.wait_ge(mrow_ready, count(pe, 8 * b + 4 * half + h + 1))
                            if s == 0 and t == 0:
                                pe.wait_ge(stacked2[par], count(pe, 16 * STACK2_DMAS * (pr + 1)))
                            if positive(tile - 1):
                                pe.wait_ge(exp_done, count(pe, tile - 1))
                            t_.matmul(st_ps[t % 2][:, :], ks1[:, par, h, keys], qs1[:, par, h, queries],
                                      start=True, stop=False)
                            t_.matmul(st_ps[t % 2][:, :], ks2[0:66, par, h, keys], qs2[0:66, par, h, queries],
                                      start=False, stop=True).then_inc(st_ready, 1)
                    lag, half, h = row_target(s + 1)
                    if in_range(lag, pair, p):
                        b, pr, par = image(lag, pair, p)
                        if half == 0 and j == 0:
                            pe.wait_ge(stacked1[par][h], count(pe, 16 * STACK1_DMAS * (pr + 1)))
                        for kh in range(2):
                            n = 64 * b + 32 * half + 8 * h + 2 * j + kh
                            if positive(n - 1):
                                pe.wait_ge(row_used, count(pe, n - 1))
                            qb = 4 * half + j
                            t_.matmul(row_ps[kh][:, :], qs1[:, par, h, qb * P:(qb + 1) * P],
                                      ks1[:, par, h, kh * HALF:(kh + 1) * HALF], start=True, stop=True)\
                              .then_inc(row_ready, 1)
                    lag, sv = steps_before(s, 1)
                    if in_range(lag, pair, p) and j in (1, 2):
                        b, _, par = image(lag, pair, p)
                        half, slot = sv // 4, 8 * (sv % 2)
                        first, last_kb = 2 * (sv % 4), 2 * (sv % 4) + 1
                        kb = first + j - 1
                        pe.wait_ge(exp_done, count(pe, 64 * b + 8 * sv + 4 * j))
                        if kb == 0:
                            if positive(4 * b + 2 * half - 1):
                                pe.wait_ge(av_out, count(pe, 4 * b + 2 * half - 1))
                            pe.wait_ge(v_ready, count(pe, 2 * b + 2))
                        for h in range(NH):
                            rows = slice(HD * h, HD * h + HD)
                            mm = t_.matmul(av_ps[rows, :], v_sb[:, par, kb, rows], probs[:, slot + 4 * (j - 1) + h, :],
                                      start=(kb == 0), stop=(kb == NKB - 1))
                        if j == 2:
                            mm.then_inc(probs_used, 1)
                    lag, sv = steps_before(s, 2)
                    if in_range(lag, pair, p) and j == 0:
                        b, _, par = image(lag, pair, p)
                        pe.wait_ge(pairs_pool, count(pe, 8 * b + sv + 1))
                        pe.wait_ge(pairs_dve, count(pe, 8 * b + sv + 1))
                        if sv % 4 == 0 and positive(4 * b + 2 * (sv // 4)):
                            pe.wait_ge(av_out, count(pe, 4 * b + 2 * (sv // 4)))
                        for h in range(NH):
                            mm = t_.matmul(den_ps[HD * h:HD * h + HD, :], ones[:, 0:HD], pairs[:, h, :],
                                           start=(sv % 4 == 0), stop=(sv % 4 == 3))
                        mm.then_inc(den_done, 1)
                    for name in at_quarter(q, pair, p):
                        piece(name, pair, p)

            iterations(pe, iteration)

            pe.wait_ge(experts_in, 48)
            pe.wait_ge(table_step, TABLE_STEPS)

            def turn_rows(r, i):
                t = r * UNROLL + i
                pe.wait_ge(z_loaded[i % DEPTH], 16 * (2 * r + i // DEPTH + 1))
                if positive(t - 1):
                    pe.wait_ge(zT_tile_ready, t - 1)
                for k in range(2):
                    last = t_.transpose(bank[2 + i % 2][:, k * P:(k + 1) * P], z_rows[i % DEPTH][:, k, 0:C], ident[:, :])
                last.then_inc(zT_ps, 1)

            def up(r, i):
                t = r * UNROLL + i
                pe.wait_ge(zT_tile_ready, t + 1)
                pe.wait_ge(w1_tile_ready, t + 1)
                if positive(t - 1):
                    pe.wait_ge(hid_ready, HC * (t - 1))
                for j in range(HC):
                    last = t_.matmul(bank[i % 2][:, j * TILE:(j + 1) * TILE], w1_tile[i % 2][:, j * P:(j + 1) * P],
                                     zT_tile[i % 2], start=True, stop=True)
                last.then_inc(hid_ps, 1)

            def down(r, i):
                t = r * UNROLL + i
                e = pe.value_load(tile_expert[0:1, bass.ds(t, 1)], min_val=0, max_val=E - 1)
                pe.wait_ge(hid_ready, HC * t + HC)
                if positive(t - 1):
                    pe.wait_ge(y_sum_ready, t - 1)
                for k in range(2):
                    for j in range(HC):
                        last = t_.matmul(bank[4 + i % 2][:, k * P:(k + 1) * P], hid[i % 2][:, j, k * P:(k + 1) * P],
                                         w2[:, bass.ds(e, 1), j, :].rearrange("p a c -> p (a c)"),
                                         start=(j == 0), stop=(j == HC - 1))
                last.then_inc(y_ps, 1)

            turn_rows(0, 0)
            for i in range(UNROLL):
                turn_rows((i + 1) // UNROLL, (i + 1) % UNROLL)
                up(0, i)
                if i > 0:
                    down(0, i - 1)
            with pe.Fori(1, ROUNDS - 1) as r:
                for i in range(UNROLL):
                    turn_rows(r if i < UNROLL - 1 else r + 1, (i + 1) % UNROLL)
                    up(r, i)
                    down(r - 1 if i == 0 else r, (i - 1) % UNROLL)
            for i in range(UNROLL):
                if i < UNROLL - 1:
                    turn_rows(ROUNDS - 1, i + 1)
                up(ROUNDS - 1, i)
                down(ROUNDS - 2 if i == 0 else ROUNDS - 1, (i - 1) % UNROLL)
            down(ROUNDS - 1, UNROLL - 1)

            def turn_out(r, i):
                n = 4 * r + i
                pe.wait_ge(sum_step, 2 * n + 2)
                if positive(n - 1):
                    pe.wait_ge(outT_ready, n - 1)
                for k in range(4):
                    last = t_.transpose(bank[i % 2][:, k * P:(k + 1) * P], y_in[i][0][:, k, :], ident[:, :])
                last.then_inc(outT_ps, 1)

            for i in range(4):
                turn_out(0, i)
            with pe.Fori(1, B // 2) as r:
                for i in range(4):
                    turn_out(r, i)


_INS = ['x', 'L0_conv_gamma', 'L0_conv_beta', 'L0_conv_run_mean', 'L0_conv_run_var', 'L0_conv_qkv_w',
        'L0_conv_qkv_b', 'L0_conv_out_w', 'L0_conv_out_b', 'L1_attn_kln_weight', 'L1_attn_kln_bias',
        'L1_attn_vln_weight', 'L1_attn_vln_bias', 'L1_ffn_gate_w', 'L1_ffn_gate_b', 'L1_ffn_W1',
        'L1_ffn_b1', 'L1_ffn_W2', 'L1_ffn_b2']
_OUTS = [((16, 128, 32, 32), 'float32')]


def kernel(**inputs):
    import numpy as _np
    import concourse.bacc as _bacc
    from concourse import mybir as _mybir
    from concourse.bass_utils import run_bass_kernel_spmd as _run

    nc = _bacc.Bacc("TRN2", target_bir_lowering=False, num_devices=1)
    arrays, args = {}, []
    for name in _INS:
        a = _np.ascontiguousarray(inputs[name])
        arrays[f"in_{name}_dram"] = a
        args.append(nc.dram_tensor(f"in_{name}_dram", a.shape, _mybir.dt.from_np(a.dtype), kind="ExternalInput").ap())
    for i, (shape, dtype) in enumerate(_OUTS):
        dt = _mybir.dt.from_np(_np.dtype(dtype))
        args.append(nc.dram_tensor(f"out_{i}_dram", shape, dt, kind="ExternalOutput").ap())
    conv_attention_hybrid_kernel(nc, *args)
    r = _run(nc, [arrays], core_ids=[0])
    got = tuple(r.results[0][f"out_{i}_dram"] for i in range(len(_OUTS)))
    return got[0]
```
